# Optimizing a Trainium2 kernel written in Bass

```python
import numpy as np
import jax
import jax.numpy as jnp

def _softmax(x, axis=-1):
    return jax.nn.softmax(x, axis=axis)

def _gelu(x):
    return jax.nn.gelu(x, approximate=True)

def _silu(x):
    return jax.nn.silu(x)

def _sigmoid(x):
    return jax.nn.sigmoid(x)

def _layernorm(x, axis=-1, eps=1e-05):
    m = jnp.mean(x, axis=axis, keepdims=True)
    v = jnp.var(x, axis=axis, keepdims=True)
    return (x - m) / jnp.sqrt(v + eps)

def _scatter_add(tgt, idx, src, axis=0):
    return tgt.at[idx].add(src)

def _segment_sum(src, seg, n):
    return jax.ops.segment_sum(src, seg, n)
kernel_name = 'mk_decoder_preln_d2_seqx_r8_778fd9'

def setup_inputs(seed: int=0):
    np.random.seed(seed)
    _w = jnp.asarray

    def _rec_inputs():
        import jax
        import jax.numpy as jnp
        _rk = jax.random.key(seed)
        x = -0.0003929 + 0.9999 * jax.random.normal(jax.random.fold_in(_rk, 1), (128, 64, 128), jnp.float32)
        _lenS = 64 - jax.random.randint(jax.random.fold_in(_rk, 7), (128,), 0, max(1, 64 // 4) + 1, jnp.int32)
        _lenS2 = 64 - jax.random.randint(jax.random.fold_in(_rk, 8), (128,), 0, max(1, 64 // 4) + 1, jnp.int32)
        _ctx_1024P = jax.random.normal(jax.random.fold_in(_rk, 11), (128, 16, 128), jnp.float32)
        _ctx_1024c = jax.random.dirichlet(jax.random.fold_in(_rk, 511), 0.3 * jnp.ones((16,), jnp.float32), (128, 64))
        _ctx_1024t = jnp.einsum('bsk,bkd->bsd', _ctx_1024c, _ctx_1024P)
        _ctx_1024t = _ctx_1024t * jax.lax.rsqrt(jnp.mean(jnp.square(_ctx_1024t)) + 1e-12) * 0.953939
        ctx_1024 = 2.81802e-05 + 1.00001 * (_ctx_1024t + 0.3 * jax.random.normal(jax.random.fold_in(_rk, 611), (128, 64, 128), jnp.float32))
        _validS = jnp.arange(64)[None, :] < _lenS[:, None]
        _validS2 = jnp.arange(64)[None, :] < _lenS2[:, None]
        _causal = jnp.tril(jnp.ones((64, 64), dtype=bool))
        mask_Bx1xS2_bk0 = jnp.logical_not(jnp.broadcast_to(_validS2[:, None, :], (128, 1, 64)))
        return (x, ctx_1024, mask_Bx1xS2_bk0)
    x, ctx_1024, mask_Bx1xS2_bk0 = _rec_inputs()

    def _L0_attn_setup():
        import jax, jax.numpy as jnp
        import numpy as np
        H = 16
        HK = 8
        E = 128
        KV_E = E // H * HK
        EPS = 1e-05

        def rmsnorm(x):
            return x * jax.lax.rsqrt(jnp.mean(jnp.square(x), axis=-1, keepdims=True) + EPS)

        def act_quant(x):
            scale = 127.0 / jnp.clip(jnp.max(jnp.abs(x), axis=-1, keepdims=True), 1e-05, None)
            return jnp.clip(jnp.round(x * scale), -128, 127) / scale

        def weight_quant(w):
            scale = 1.0 / jnp.clip(jnp.mean(jnp.abs(w)), 1e-05, None)
            return jnp.clip(jnp.round(w * scale), -1, 1) / scale

        def bitlinear(x, w, b):
            xn = rmsnorm(x)
            xq = xn + jax.lax.stop_gradient(act_quant(xn) - xn)
            wq = w + jax.lax.stop_gradient(weight_quant(w) - w)
            return xq @ wq.T + b

        def layernorm(x, g, b):
            m = jnp.mean(x, axis=-1, keepdims=True)
            v = jnp.var(x, axis=-1, keepdims=True)
            return (x - m) * jax.lax.rsqrt(v + EPS) * g + b
        key = jax.random.key(seed)
        ks = jax.random.split(key, 6)
        B, N = (2, 256)
        x = jax.random.normal(ks[0], (B, N, E), dtype=jnp.float32)
        wq = jax.random.normal(ks[1], (E, E), dtype=jnp.float32) * 0.02
        wk = jax.random.normal(ks[2], (KV_E, E), dtype=jnp.float32) * 0.02
        wv = jax.random.normal(ks[3], (KV_E, E), dtype=jnp.float32) * 0.02
        wo = jax.random.normal(ks[4], (E, E), dtype=jnp.float32) * 0.02
        return {'x': x, 'wq': wq, 'bq': jnp.zeros((E,), jnp.float32), 'wk': wk, 'bk': jnp.zeros((KV_E,), jnp.float32), 'wv': wv, 'bv': jnp.zeros((KV_E,), jnp.float32), 'wo': wo, 'bo': jnp.zeros((E,), jnp.float32), 'ln_g': jnp.ones((E,), jnp.float32), 'ln_b': jnp.zeros((E,), jnp.float32)}
    _L0_attn_all = _L0_attn_setup()
    _L0_attn_in = {k: v for k, v in _L0_attn_all.items() if k in ('wq', 'bq', 'wk', 'bk', 'wv', 'bv', 'wo', 'bo', 'ln_g', 'ln_b')}
    del _L0_attn_all

    def _L0_xattn_setup():
        import jax, jax.numpy as jnp
        import numpy as np
        import math
        B, S, D = (8, 256, 128)
        key = jax.random.key(seed)
        ks = jax.random.split(key, 8)
        s_in = 1.0 / math.sqrt(D)
        s_ent = 1.0 / math.sqrt(2 * D)
        return {'x': jax.random.normal(ks[0], (B, S, D), dtype=jnp.float32), 'context': jax.random.normal(ks[1], (B, S, D), dtype=jnp.float32), 'Wq': jax.random.normal(ks[2], (D, D), dtype=jnp.float32) * s_in, 'bq': jnp.zeros((D,), jnp.float32), 'Wk': jax.random.normal(ks[3], (D, D), dtype=jnp.float32) * s_in, 'bk': jnp.zeros((D,), jnp.float32), 'Wv': jax.random.normal(ks[4], (D, D), dtype=jnp.float32) * s_in, 'bv': jnp.zeros((D,), jnp.float32), 'We': jax.random.normal(ks[5], (D, 2 * D), dtype=jnp.float32) * s_ent, 'be': jnp.zeros((D,), jnp.float32)}
    _L0_xattn_all = _L0_xattn_setup()
    _L0_xattn_in = {k: v for k, v in _L0_xattn_all.items() if k in ('Wq', 'bq', 'Wk', 'bk', 'Wv', 'bv', 'We', 'be')}
    del _L0_xattn_all

    def _L0_ffn_setup():
        import jax, jax.numpy as jnp
        import numpy as np
        TOPK = 8
        BN_EPS = 1e-05
        key = jax.random.key(seed)
        ks = jax.random.split(key, 5)
        b, n, d = (2, 128, 128)
        h, nk, kd = (8, 32, 128)
        ne = nk * nk
        scale = 0.02
        return {'inputs': jax.random.normal(ks[0], (b, n, d), jnp.float32), 'gamma': jnp.ones((d,), jnp.float32), 'beta': jnp.zeros((d,), jnp.float32), 'w_q': jax.random.normal(ks[1], (2 * h * kd, d), jnp.float32) * scale, 'keys': jax.random.normal(ks[2], (h, nk, 2, kd), jnp.float32) * scale, 'key_in': jax.random.normal(ks[3], (ne, d), jnp.float32) * scale, 'key_out': jax.random.normal(ks[4], (ne, d), jnp.float32) * scale}
    _L0_ffn_all = _L0_ffn_setup()
    _L0_ffn_in = {k: v for k, v in _L0_ffn_all.items() if k in ('gamma', 'beta', 'w_q', 'keys', 'key_in', 'key_out')}
    del _L0_ffn_all

    def _L1_attn_setup():
        import jax, jax.numpy as jnp
        import numpy as np
        import math
        D_MODEL = 128
        N_HEADS = 16
        HEAD_DIM = D_MODEL // N_HEADS

        def get_slopes(n_heads: int) -> jnp.ndarray:

            def pow2_slopes(n):
                start = 2.0 ** (-8.0 / n)
                return np.array([start * start ** i for i in range(n)], dtype=np.float32)
            if math.log2(n_heads).is_integer():
                return jnp.asarray(pow2_slopes(n_heads))
            closest = 2 ** math.floor(math.log2(n_heads))
            base = pow2_slopes(closest)
            extra = pow2_slopes(2 * closest)[::2][:n_heads - closest]
            return jnp.asarray(np.concatenate([base, extra]))
        key = jax.random.key(seed)
        ks = jax.random.split(key, 9)
        s = 1.0 / math.sqrt(D_MODEL)
        x = jax.random.normal(ks[0], (2, 256, D_MODEL), dtype=jnp.float32)
        q_w = jax.random.uniform(ks[1], (D_MODEL, D_MODEL), jnp.float32, -s, s)
        q_b = jax.random.uniform(ks[2], (D_MODEL,), jnp.float32, -s, s)
        k_w = jax.random.uniform(ks[3], (D_MODEL, D_MODEL), jnp.float32, -s, s)
        k_b = jax.random.uniform(ks[4], (D_MODEL,), jnp.float32, -s, s)
        v_w = jax.random.uniform(ks[5], (D_MODEL, D_MODEL), jnp.float32, -s, s)
        v_b = jax.random.uniform(ks[6], (D_MODEL,), jnp.float32, -s, s)
        o_w = jax.random.uniform(ks[7], (D_MODEL, D_MODEL), jnp.float32, -s, s)
        o_b = jax.random.uniform(ks[8], (D_MODEL,), jnp.float32, -s, s)
        return {'x': x, 'q_w': q_w, 'q_b': q_b, 'k_w': k_w, 'k_b': k_b, 'v_w': v_w, 'v_b': v_b, 'o_w': o_w, 'o_b': o_b}
    _L1_attn_all = _L1_attn_setup()
    _L1_attn_in = {k: v for k, v in _L1_attn_all.items() if k in ('q_w', 'q_b', 'k_w', 'k_b', 'v_w', 'v_b', 'o_w', 'o_b')}
    del _L1_attn_all

    def _L1_xattn_setup():
        import jax, jax.numpy as jnp
        import numpy as np
        B, S, E, H = (4, 256, 128, 16)
        DH = E // H

        def _make_heads(v, n_heads):
            b, n, e = v.shape
            return jnp.moveaxis(v.reshape(b, n, n_heads, e // n_heads), -2, 0)
        key = jax.random.key(seed)
        k1, k2, k3, k4, k5 = jax.random.split(key, 5)
        return {'query': jax.random.normal(k1, (B, S, E), dtype=jnp.float32), 'key': jax.random.normal(k2, (B, S, E), dtype=jnp.float32), 'value': jax.random.normal(k3, (B, S, E), dtype=jnp.float32), 'mask': jax.random.randint(k4, (B, 1, S), 0, 2).astype(bool), 'W_out': jax.random.normal(k5, (E, E), dtype=jnp.float32) / np.sqrt(E), 'scale': jnp.asarray(1.0, dtype=jnp.float32), 'log_C': jnp.asarray(np.log(10.0), dtype=jnp.float32)}
    _L1_xattn_all = _L1_xattn_setup()
    _L1_xattn_in = {k: v for k, v in _L1_xattn_all.items() if k in ('W_out', 'scale', 'log_C')}
    del _L1_xattn_all

    def _L1_ffn_setup():
        import jax, jax.numpy as jnp
        import numpy as np
        B, S, D = (2, 512, 128)
        H = 512
        E = 8
        K = 4
        key = jax.random.key(seed)
        kx, kr, ku, kd = jax.random.split(key, 4)
        x = jax.random.normal(kx, (B, S, D), dtype=jnp.float32)
        router_w = jax.random.normal(kr, (D, E), dtype=jnp.float32) / np.sqrt(D)
        up_w = jax.random.normal(ku, (E, D, H), dtype=jnp.float32) / np.sqrt(D)
        down_w = jax.random.normal(kd, (E, H, D), dtype=jnp.float32) / np.sqrt(H)
        return {'x': x, 'router_w': router_w, 'up_w': up_w, 'down_w': down_w}
    _L1_ffn_all = _L1_ffn_setup()
    _L1_ffn_in = {k: v for k, v in _L1_ffn_all.items() if k in ('router_w', 'up_w', 'down_w')}
    del _L1_ffn_all
    return {'x': x, 'ctx_1024': ctx_1024, 'mask_Bx1xS2_bk0': mask_Bx1xS2_bk0, 'L0_attn_wq': _L0_attn_in['wq'], 'L0_attn_bq': _L0_attn_in['bq'], 'L0_attn_wk': _L0_attn_in['wk'], 'L0_attn_bk': _L0_attn_in['bk'], 'L0_attn_wv': _L0_attn_in['wv'], 'L0_attn_bv': _L0_attn_in['bv'], 'L0_attn_wo': _L0_attn_in['wo'], 'L0_attn_bo': _L0_attn_in['bo'], 'L0_attn_ln_g': _L0_attn_in['ln_g'], 'L0_attn_ln_b': _L0_attn_in['ln_b'], 'L0_xattn_Wq': _L0_xattn_in['Wq'], 'L0_xattn_bq': _L0_xattn_in['bq'], 'L0_xattn_Wk': _L0_xattn_in['Wk'], 'L0_xattn_bk': _L0_xattn_in['bk'], 'L0_xattn_Wv': _L0_xattn_in['Wv'], 'L0_xattn_bv': _L0_xattn_in['bv'], 'L0_xattn_We': _L0_xattn_in['We'], 'L0_xattn_be': _L0_xattn_in['be'], 'L0_ffn_gamma': _L0_ffn_in['gamma'], 'L0_ffn_beta': _L0_ffn_in['beta'], 'L0_ffn_w_q': _L0_ffn_in['w_q'], 'L0_ffn_keys': _L0_ffn_in['keys'], 'L0_ffn_key_in': _L0_ffn_in['key_in'], 'L0_ffn_key_out': _L0_ffn_in['key_out'], 'L1_attn_q_w': _L1_attn_in['q_w'], 'L1_attn_q_b': _L1_attn_in['q_b'], 'L1_attn_k_w': _L1_attn_in['k_w'], 'L1_attn_k_b': _L1_attn_in['k_b'], 'L1_attn_v_w': _L1_attn_in['v_w'], 'L1_attn_v_b': _L1_attn_in['v_b'], 'L1_attn_o_w': _L1_attn_in['o_w'], 'L1_attn_o_b': _L1_attn_in['o_b'], 'L1_xattn_W_out': _L1_xattn_in['W_out'], 'L1_xattn_scale': _L1_xattn_in['scale'], 'L1_xattn_log_C': _L1_xattn_in['log_C'], 'L1_ffn_router_w': _L1_ffn_in['router_w'], 'L1_ffn_up_w': _L1_ffn_in['up_w'], 'L1_ffn_down_w': _L1_ffn_in['down_w']}

def reference(x, ctx_1024, mask_Bx1xS2_bk0, L0_attn_wq, L0_attn_bq, L0_attn_wk, L0_attn_bk, L0_attn_wv, L0_attn_bv, L0_attn_wo, L0_attn_bo, L0_attn_ln_g, L0_attn_ln_b, L0_xattn_Wq, L0_xattn_bq, L0_xattn_Wk, L0_xattn_bk, L0_xattn_Wv, L0_xattn_bv, L0_xattn_We, L0_xattn_be, L0_ffn_gamma, L0_ffn_beta, L0_ffn_w_q, L0_ffn_keys, L0_ffn_key_in, L0_ffn_key_out, L1_attn_q_w, L1_attn_q_b, L1_attn_k_w, L1_attn_k_b, L1_attn_v_w, L1_attn_v_b, L1_attn_o_w, L1_attn_o_b, L1_xattn_W_out, L1_xattn_scale, L1_xattn_log_C, L1_ffn_router_w, L1_ffn_up_w, L1_ffn_down_w):
    import jax
    import jax.numpy as jnp

    def _L0_attn_ref(x, wq, bq, wk, bk, wv, bv, wo, bo, ln_g, ln_b):
        import jax, jax.numpy as jnp
        import numpy as np
        H = 16
        HK = 8
        E = 128
        KV_E = E // H * HK
        EPS = 1e-05

        def rmsnorm(x):
            return x * jax.lax.rsqrt(jnp.mean(jnp.square(x), axis=-1, keepdims=True) + EPS)

        def act_quant(x):
            scale = 127.0 / jnp.clip(jnp.max(jnp.abs(x), axis=-1, keepdims=True), 1e-05, None)
            return jnp.clip(jnp.round(x * scale), -128, 127) / scale

        def weight_quant(w):
            scale = 1.0 / jnp.clip(jnp.mean(jnp.abs(w)), 1e-05, None)
            return jnp.clip(jnp.round(w * scale), -1, 1) / scale

        def bitlinear(x, w, b):
            xn = rmsnorm(x)
            xq = xn + jax.lax.stop_gradient(act_quant(xn) - xn)
            wq = w + jax.lax.stop_gradient(weight_quant(w) - w)
            return xq @ wq.T + b

        def layernorm(x, g, b):
            m = jnp.mean(x, axis=-1, keepdims=True)
            v = jnp.var(x, axis=-1, keepdims=True)
            return (x - m) * jax.lax.rsqrt(v + EPS) * g + b
        B, N, _ = x.shape
        d = E // H
        g = H // HK
        q = bitlinear(x, wq, bq).reshape(B, N, H, d)
        k = bitlinear(x, wk, bk).reshape(B, N, HK, d)
        v = bitlinear(x, wv, bv).reshape(B, N, HK, d)
        q = q.transpose(0, 2, 1, 3).reshape(B, HK, g, N, d).transpose(0, 2, 1, 3, 4)
        k = k.transpose(0, 2, 1, 3)
        v = v.transpose(0, 2, 1, 3)
        scale = jnp.float32(d) ** 0.5
        sim = jnp.einsum('bghnd,bhsd->bghns', q, k) / scale
        attn = jax.nn.softmax(sim, axis=-1)
        out = jnp.einsum('bghns,bhsd->bghnd', attn, v)
        out = out.transpose(0, 3, 2, 1, 4).reshape(B, N, E)
        out = layernorm(out, ln_g, ln_b)
        return bitlinear(out, wo, bo)

    def _L0_xattn_ref(x, context, Wq, bq, Wk, bk, Wv, bv, We, be):
        import jax, jax.numpy as jnp
        import numpy as np
        import math
        B, S, D = (8, 256, 128)
        q = jnp.einsum('bsd,ed->bse', x, Wq) + bq
        k = jnp.einsum('bsd,ed->bse', context, Wk) + bk
        v = jnp.einsum('bsd,ed->bse', context, Wv) + bv
        entangled = jnp.tanh(jnp.einsum('bsd,ed->bse', jnp.concatenate([q, k], axis=-1), We) + be)
        scale = 1.0 / math.sqrt(x.shape[-1])
        scores = jnp.einsum('bqd,bkd->bqk', entangled, v) * scale
        attn = jax.nn.softmax(scores, axis=-1)
        return jnp.einsum('bqk,bkd->bqd', attn, v)

    def _L0_ffn_ref(inputs, gamma, beta, w_q, keys, key_in, key_out):
        import jax, jax.numpy as jnp
        import numpy as np
        TOPK = 8
        BN_EPS = 1e-05
        b, n, d = inputs.shape
        h, nk, _, kd = keys.shape
        k = TOPK
        x = inputs.reshape(b * n, d)
        mu = jnp.mean(x, axis=0)
        var = jnp.mean(jnp.square(x - mu), axis=0)
        xn = (x - mu) * jax.lax.rsqrt(var + BN_EPS) * gamma + beta
        q = (xn @ w_q.T).reshape(b, n, 2, h, kd).transpose(2, 0, 1, 3, 4)
        sim = jnp.einsum('pbnhd,hkpd->pbnhk', q, keys)
        s, i = jax.lax.top_k(sim, k)
        sx, sy = (s[0], s[1])
        ix, iy = (i[0], i[1])
        all_scores = (sx[..., :, None] + sy[..., None, :]).reshape(b, n, h, k * k)
        all_idx = (ix[..., :, None] * nk + iy[..., None, :]).reshape(b, n, h, k * k)
        scores, pk = jax.lax.top_k(all_scores, k)
        idx = jnp.take_along_axis(all_idx, pk, axis=-1)
        w_down = key_in[idx]
        w_up = key_out[idx]
        o = jnp.einsum('bnd,bnhkd->bnhk', inputs, w_down)
        o = jax.nn.gelu(o, approximate=False) * jax.nn.softmax(scores, axis=-1)
        return jnp.einsum('bnhk,bnhkd->bnd', o, w_up)

    def _L1_attn_ref(x, q_w, q_b, k_w, k_b, v_w, v_b, o_w, o_b):
        import jax, jax.numpy as jnp
        import numpy as np
        import math
        D_MODEL = 128
        N_HEADS = 16
        HEAD_DIM = D_MODEL // N_HEADS

        def get_slopes(n_heads: int) -> jnp.ndarray:

            def pow2_slopes(n):
                start = 2.0 ** (-8.0 / n)
                return np.array([start * start ** i for i in range(n)], dtype=np.float32)
            if math.log2(n_heads).is_integer():
                return jnp.asarray(pow2_slopes(n_heads))
            closest = 2 ** math.floor(math.log2(n_heads))
            base = pow2_slopes(closest)
            extra = pow2_slopes(2 * closest)[::2][:n_heads - closest]
            return jnp.asarray(np.concatenate([base, extra]))
        B, S, D = x.shape
        H, hd = (N_HEADS, HEAD_DIM)
        Q = (x @ q_w.T + q_b).reshape(B, S, H, hd).transpose(0, 2, 1, 3)
        K = (x @ k_w.T + k_b).reshape(B, S, H, hd).transpose(0, 2, 1, 3)
        V = (x @ v_w.T + v_b).reshape(B, S, H, hd).transpose(0, 2, 1, 3)
        scores = jnp.einsum('bhqd,bhkd->bhqk', Q, K) / math.sqrt(hd)
        pos = jnp.arange(S)
        rel = (pos[None, :] - pos[:, None]).astype(scores.dtype)
        slopes = get_slopes(H)
        scores = scores + slopes[None, :, None, None] * rel[None, None, :, :]
        causal = pos[None, :] <= pos[:, None]
        scores = jnp.where(causal[None, None], scores, -jnp.inf)
        attn = jax.nn.softmax(scores, axis=-1)
        out = jnp.einsum('bhqk,bhkd->bhqd', attn, V)
        out = out.transpose(0, 2, 1, 3).reshape(B, S, D)
        return out @ o_w.T + o_b

    def _L1_xattn_ref(query, key, value, mask, W_out, scale, log_C):
        import jax, jax.numpy as jnp
        import numpy as np
        B, S, E, H = (4, 256, 128, 16)
        DH = E // H

        def _make_heads(v, n_heads):
            b, n, e = v.shape
            return jnp.moveaxis(v.reshape(b, n, n_heads, e // n_heads), -2, 0)
        q = _make_heads(query, H)
        k = _make_heads(key, H)
        v = _make_heads(value, H)
        d_k = q.shape[-1]
        u = jnp.einsum('hbqd,hbkd->hbqk', q, k) * scale / np.sqrt(d_k)
        logits = jnp.tanh(u) * jnp.exp(log_C)
        logits = jnp.where(mask, -jnp.inf, logits)
        attn = jax.nn.softmax(logits, axis=-1)
        out_heads = jnp.einsum('hbqk,hbkd->hbqd', attn, v)
        out = jnp.moveaxis(out_heads, 0, -2).reshape(query.shape)
        return out @ W_out.T

    def _L1_ffn_ref(x, router_w, up_w, down_w):
        import jax, jax.numpy as jnp
        import numpy as np
        B, S, D = (2, 512, 128)
        H = 512
        E = 8
        K = 4
        router_logits = jnp.einsum('bsd,de->bse', x, router_w)
        routing_weights = jax.nn.softmax(router_logits, axis=-1)
        topk_weights, topk_indices = jax.lax.top_k(routing_weights, K)
        topk_weights = topk_weights / jnp.sum(topk_weights, axis=-1, keepdims=True)
        h = jnp.einsum('bsd,edh->bseh', x, up_w)
        h = jax.nn.gelu(h)
        expert_outputs = jnp.einsum('bseh,ehd->bsed', h, down_w)
        gathered = jnp.take_along_axis(expert_outputs, topk_indices[:, :, :, None], axis=2)
        output = jnp.sum(topk_weights[:, :, :, None] * gathered, axis=2)
        return output
    x = x + _L0_attn_ref(_layernorm(x, axis=-1), L0_attn_wq, L0_attn_bq, L0_attn_wk, L0_attn_bk, L0_attn_wv, L0_attn_bv, L0_attn_wo, L0_attn_bo, L0_attn_ln_g, L0_attn_ln_b)
    x = x + _L0_xattn_ref(_layernorm(x, axis=-1), ctx_1024, L0_xattn_Wq, L0_xattn_bq, L0_xattn_Wk, L0_xattn_bk, L0_xattn_Wv, L0_xattn_bv, L0_xattn_We, L0_xattn_be)
    x = x + _L0_ffn_ref(_layernorm(x, axis=-1), L0_ffn_gamma, L0_ffn_beta, L0_ffn_w_q, L0_ffn_keys, L0_ffn_key_in, L0_ffn_key_out)
    x = x + _L1_attn_ref(_layernorm(x, axis=-1), L1_attn_q_w, L1_attn_q_b, L1_attn_k_w, L1_attn_k_b, L1_attn_v_w, L1_attn_v_b, L1_attn_o_w, L1_attn_o_b)
    x = x + _L1_xattn_ref(_layernorm(x, axis=-1), ctx_1024, ctx_1024, mask_Bx1xS2_bk0, L1_xattn_W_out, L1_xattn_scale, L1_xattn_log_C)
    x = x + _L1_ffn_ref(_layernorm(x, axis=-1), L1_ffn_router_w, L1_ffn_up_w, L1_ffn_down_w)
    return x

_drawn_inputs = setup_inputs


def setup_inputs(seed=0):
    import zlib

    import numpy as np

    out = dict(_drawn_inputs(seed))
    spreads = {'L0_attn_bq': (0.0, 0.8),
     'L0_attn_bk': (0.0, 2.0),
     'L0_attn_bv': (0.0, 0.1),
     'L0_attn_bo': (0.0, 0.1),
     'L0_attn_ln_g': (1.0, 0.547),
     'L0_attn_ln_b': (0.0, 0.443),
     'L0_xattn_bq': (0.0, 0.568),
     'L0_xattn_bk': (0.0, 0.647),
     'L0_xattn_bv': (0.0, 0.1),
     'L0_xattn_be': (0.0, 0.466),
     'L0_ffn_gamma': (1.0, 0.6),
     'L0_ffn_beta': (0.0, 0.8)}
    factors = {'L0_attn_wq': 8.0,
     'L0_attn_wk': 8.0,
     'L0_ffn_w_q': 8.0,
     'L0_ffn_keys': 8.0,
     'L0_ffn_key_in': 8.0,
     'L0_ffn_key_out': 8.0,
     'L1_attn_q_b': 26.338,
     'L1_attn_k_b': 64.0}
    for name, (base, spread) in spreads.items():
        noise = np.random.default_rng([zlib.crc32(name.encode()), seed]).standard_normal(out[name].shape)
        drawn = base * np.exp(spread * noise) if base else spread * noise
        out[name] = jnp.asarray(drawn.astype(out[name].dtype))
    for name, factor in factors.items():
        out[name] = (out[name] * factor).astype(out[name].dtype)
    return out
```

```python
from contextlib import ExitStack

import numpy as np

import concourse.bass as bass
from concourse import mybir

P = 128
SEQ = 64
HEADS = 16
DH = P // HEADS
SETS = 4
SLOTS = 4
SLOT = 32
FOLD_MAX = 2 * DH
EPS = 1e-5
MAGIC = 1.5 * 2.0 ** 23
NEG = -1e30
NKEY = 32
PH = 8
TOPK = 8
NEXP = NKEY * NKEY
CHUNKS = NEXP // P
MOE = 8
MOE_K = 4
HID = 512

F32 = mybir.dt.float32
BF16 = mybir.dt.bfloat16
U8 = mybir.dt.uint8
U32 = mybir.dt.uint32
ALU = mybir.AluOpType
ACT = mybir.ActivationFunctionType
X = mybir.AxisListType.X

CONST = {}
_at = 0
for _name, _n in (("ident", P), ("half", P), ("key0", P), ("key1", P), ("query1", SETS * P), ("causal", 4 * SEQ),
                  ("causalT", 4 * SEQ), ("stack", SEQ), ("shift", 3 * SEQ), ("vones", HEADS * 2 * (DH + 1))):
    CONST[_name] = (_at, _n)
    _at += _n
CONSTS = _at
ROWS = ("bv0", "bo0", "g0", "b0", "bv1", "bo1")
COLS = {"xbq": (0, 1), "xbk": (1, 1), "xbv": (2, 1), "xbe": (3, 1), "gamma": (4, 1), "beta": (5, 1),
        "bq0": (6, SETS), "bk0": (6 + SETS, SETS), "bq1": (6 + 2 * SETS, SETS), "bk1": (6 + 3 * SETS, SETS)}
NCOLS = 6 + 4 * SETS


class Tile:

    def __init__(self, t, u, pair):
        self.t, self.u, self.pair = t, u, pair

    def now(self, base=0):
        return self.t + (base + 1)

    def before(self, n, base=0):
        return self.t + (base + 1 - n)

    def step(self, per_tile, k, base=0):
        return self.t * per_tile + (base * per_tile + k)


def need(eng, sem, value):
    if isinstance(value, int) and value <= 0:
        return
    eng.wait_ge(sem, value)


def tile_col(block, T):
    return block.rearrange("p (t o) -> p t o", o=1)[:, T.t, :]


def staggered(nc, eng, tiles, segments):
    lag = max(l for l, _ in segments)
    peel = lag + 2 + lag % 2
    for s in range(peel):
        for l, seg in segments:
            if s >= l:
                seg(Tile(s - l, (s - l) % 2, (s - l) // 2))
    with nc.Fori(peel // 2, tiles // 2, engines=[eng.engine]) as i:
        for u in range(2):
            for l, seg in segments:
                seg(Tile(2 * i + (u - l), (u - l) % 2, i + (u - l) // 2))
    for s in range(tiles, tiles + lag):
        for l, seg in segments:
            if s - l < tiles:
                seg(Tile(s - l, (s - l) % 2, (s - l) // 2))


def build(nc, x, ctxT, ctx, mask, consts, rows, cols, wq0, wk0, wv0, wo0, xWq, xWk, xWvT, xWeT, wqk, keysT, key_inT,
          key_out, wq1, wk1, wv1, wo1, headsel, wout, scal, router, up, down, out):
    NT = x.shape[0] // P
    with ExitStack() as es:
        def sb(name, shape, dt=F32):
            return es.enter_context(nc.sbuf_tensor(name, shape, dt))

        def sem(name):
            return es.enter_context(nc.semaphore(name))

        xs = sb("x_all", [P, NT, P])
        cT = sb("ctxT_all", [P, NT * P])
        big = sb("big", [P, 8192])
        o_all = big[:, 0:NT * P].rearrange("p (t d) -> p t d", d=P)
        xT_all = big[:, 0:NT * P]
        up_w = big[:, 0:MOE * HID].rearrange("p (e h) -> p e h", e=MOE)
        down_w = big[:, MOE * HID:2 * MOE * HID].rearrange("p (e c d) -> p e c d", e=MOE, c=HID // P)
        cst = sb("consts_sb", [P, CONSTS])
        row = sb("rows_sb", [P, len(ROWS) * P])
        col = sb("cols_sb", [P, NCOLS])
        w8 = sb("w8", [P, 2048])
        wq0_s = w8[:, 0:1024].rearrange("p (b g c) -> p b g c", b=2, g=SETS)
        wk0_s = w8[:, 1024:2048].rearrange("p (b g c) -> p b g c", b=2, g=SETS)
        kin = w8[:, 0:NEXP]
        kout = w8[:, 1024:2048].rearrange("p (c d) -> p c d", c=CHUNKS)
        wqk1 = sb("wqk1", [P, 2, 2, SETS, P])
        sel_s = sb("headsel_sb", [P, 2, SETS, P])
        small = sb("small_w", [P, 8, P])
        WV0, WO0, A1, A2, XWV, WV1, WO1, WOUT = range(8)
        wo0_b = sb("wo0_bf", [P, P], BF16)
        rt = sb("router_sb", [P, MOE])
        Mk = sb("Mk", [P, 2 * PH * NKEY])
        bmq = sb("bmq", [P, SETS, P])
        bmk = sb("bmk", [P, SETS, P])
        ident_b = sb("ident_bf", [P, P], BF16)
        causal_b = sb("causal_bf", [P, 2, 4 * SEQ], BF16)
        mv = sb("mv", [P, 2, NT])
        st_all = sb("st_all", [P, NT, 6])
        rs = sb("rstd", [P, NT])
        t64 = sb("t64", [P, 8, NT])
        sc = sb("scalars", [P, 32])
        mask4 = sb("mask4", [P, NT // 4], U32)
        mbias = sb("mbias", [P, NT])
        ones = sb("ones", [P, P])
        s_in = sb("quant_scale", [P, 2, NT])
        bnst = sb("bn_stats_all", [P, NT, 6])

        def C(name):
            a, n = CONST[name]
            return cst[:, a:a + n]

        def R(name):
            a = ROWS.index(name) * P
            return row[:, a:a + P]

        def K(name):
            a, n = COLS[name]
            return col[:, a:a + n]

        ident = C("ident")

        WORK = 10752
        work = sb("work", [P, WORK])
        top = [0]

        def carve(n):
            a = top[0]
            top[0] += n
            assert top[0] <= WORK, top[0]
            return work[:, a:a + n]

        xn = carve(2 * P).rearrange("p (u d) -> p u d", u=2)
        aT = carve(2 * P).rearrange("p (u d) -> p u d", u=2)
        after_aT = top[0]
        QB = carve(2 * SETS * P).rearrange("p (u g c) -> p u g c", u=2, g=SETS)
        KB = carve(2 * SETS * P).rearrange("p (u g c) -> p u g c", u=2, g=SETS)
        QC = carve(2 * SETS * SEQ).rearrange("p (u g c) -> p u g c", u=2, g=SETS)
        KC = carve(2 * SETS * SEQ).rearrange("p (u g c) -> p u g c", u=2, g=SETS)
        QM = carve(2 * SETS * SEQ).rearrange("p (u g c) -> p u g c", u=2, g=SETS)
        VB = carve(2 * HEADS * 2 * (DH + 1)).rearrange("p (u h b d) -> p u h b d", u=2, h=HEADS, b=2)
        PT = carve(2 * HEADS * SEQ).rearrange("p (u s g q) -> p u s g q", u=2, s=SLOTS, g=SETS)
        NM = carve(2 * SETS * P).rearrange("p (u g s r) -> p u g s r", u=2, g=SETS, s=SLOTS)
        O = carve(2 * 2 * P).rearrange("p (u b h d) -> p u b h d", u=2, b=2, h=HEADS)
        OT = carve(2 * P).rearrange("p (u d) -> p u d", u=2)
        mx = carve(2 * HEADS).rearrange("p (u s g) -> p u s g", u=2, s=SLOTS)
        rec = carve(2 * HEADS * 2).rearrange("p (u h b) -> p u h b", u=2, h=HEADS)
        ctile = carve(2 * P).rearrange("p (u d) -> p u d", u=2)
        ytmp = carve(2 * P).rearrange("p (u d) -> p u d", u=2)
        top[0] = 0
        raw = carve(4 * P).rearrange("p (n d) -> p n d", n=4)
        RWQ, RWK, RWE1, RWE2 = range(4)
        rqk = carve(2 * PH * P).rearrange("p (n d) -> p n d", n=2 * PH)
        rkey = carve(2 * PH * NKEY).rearrange("p (n d) -> p n d", n=2 * PH)
        top[0] = after_aT
        ent = carve(2 * P).rearrange("p (u d) -> p u d", u=2)
        VT = carve(2 * P).rearrange("p (u d) -> p u d", u=2)
        Vt = carve(2 * P).rearrange("p (u d) -> p u d", u=2)
        PB = carve(2 * P).rearrange("p (u d) -> p u d", u=2)
        PBT = carve(2 * P).rearrange("p (u d) -> p u d", u=2)
        xden = carve(8).rearrange("p (u n) -> p u n", u=2)
        top[0] = 0
        NS = 2 * PH * NKEY
        xb = carve(2 * P).rearrange("p (u d) -> p u d", u=2)
        EX = carve(2 * (NS + 2 * PH * TOPK)).rearrange("p (u n) -> p u n", u=2)
        V8 = carve(2 * 2 * PH * TOPK).rearrange("p (u n k) -> p u n k", u=2, k=TOPK)
        CD = carve(PH * TOPK * TOPK).rearrange("p (h n) -> p h n", h=PH)
        T8 = carve(2 * PH * TOPK).rearrange("p (u h k) -> p u h k", u=2, k=TOPK)
        Z = carve(2 * PH).rearrange("p (u h) -> p u h", u=2)
        RZ = carve(2 * PH).rearrange("p (u h) -> p u h", u=2)
        DG = carve(2 * PH * P).rearrange("p (u h d) -> p u h d", u=2, h=PH)
        EE = carve(2 * NEXP).rearrange("p (u n) -> p u n", u=2)
        WW = carve(2 * NEXP).rearrange("p (u n) -> p u n", u=2)
        HT = carve(NEXP).rearrange("p (c d) -> p c d", c=CHUNKS)
        HG = carve(NEXP).rearrange("p (c d) -> p c d", c=CHUNKS)
        HC = HID // P
        RING = 4
        top[0] = after_aT
        hT = carve(RING * HID).rearrange("p (n c d) -> p n c d", n=RING, c=HC)
        lg = carve(2 * MOE).rearrange("p (u e) -> p u e", u=2)
        l8 = carve(2 * MOE).rearrange("p (u e) -> p u e", u=2)
        le = carve(2 * MOE).rearrange("p (u e) -> p u e", u=2)
        lw = carve(2 * MOE).rearrange("p (u e) -> p u e", u=2)
        ls = carve(8).rearrange("p (u e) -> p u e", u=2)

        ps = es.enter_context(nc.psum_tensor("ps", [P, 8, 512], F32))

        def bank(b, a, n=P):
            return ps[:, b, a:a + n]

        psQ = ps[:, 0, :].rearrange("p (g c) -> p g c", g=SETS)
        psK = ps[:, 1, :].rearrange("p (g c) -> p g c", g=SETS)
        psA, psV = bank(2, 0), bank(2, P)
        psOT, psY = bank(3, 0), bank(3, P)
        psO = ps[0:SEQ, 3, 0:HEADS * 2 * (DH + 1)].rearrange("p (h b d) -> p h b d", h=HEADS, b=2)
        psS = ps[:, 4:8, 0:SETS * SEQ].rearrange("p s (g k) -> p s g k", g=SETS)
        psST = ps[:, 4:8, SETS * SEQ:512].rearrange("p s (g q) -> p s g q", g=SETS)
        psN = ps[:, 4, 0:SETS * SEQ].rearrange("p (g q) -> p g q", g=SETS)
        psE, psVT, psVx, psSx, psPT, psXO = bank(0, 0), bank(1, 0), bank(3, 0), bank(4, 0, SEQ), bank(5, 0), bank(6, 0)
        psG = [ps[:, 1:3, :].rearrange("p b (c d) -> p (b c) d", d=P), ps[:, 3:5, :].rearrange("p b (c d) -> p (b c) d", d=P)]
        psH = ps[:, 5:7, :].rearrange("p b (c d) -> p (b c) d", d=P)
        psM = bank(7, 0)
        psU = ps[:, 0:RING, :].rearrange("p n (c d) -> p n c d", d=P)
        psD = [bank(4, 0), bank(5, 0)]
        psXA, psR = bank(6, 0), bank(7, 0, MOE)

        cTv = cT[:, :].rearrange("p (t b q) -> p t b q", b=2, q=SEQ)
        cTt = cT[:, :].rearrange("p (t d) -> p t d", d=P)
        xTt = xT_all.rearrange("p (t d) -> p t d", d=P)

        loaded, tables, experts_in, stored = sem("loaded"), sem("tables_loaded"), sem("experts_loaded"), sem("stored")
        ctx_in = [sem("ctx_tile0_in"), sem("ctx_tile1_in")]
        ones_ready, sums_done, quantised, folds_done, folds_ready, bound_ready = (
            sem("ones_ready"), sem("sums_done"), sem("quantised"), sem("folds_done"), sem("folds_ready"), sem("bound_ready"))
        phase = sem("phase_ready")
        var_ready, std_ready = sem("var_ready"), sem("std_ready")
        xn_step, xn_ready, aT_raw, aT_ready = sem("xn_step"), sem("xn_ready"), sem("aT_raw"), sem("aT_ready")
        q_done, k_done, v_done = sem("q_done"), sem("k_done"), sem("v_done")
        qb_ready, kb_ready, vb_ready = sem("qb_ready"), sem("kb_ready"), sem("vb_ready")
        qc_ready, kc_ready = sem("qc_ready"), sem("kc_ready")
        s_done, mx_ready, nm_ready, nmT_done, qm_ready = (
            sem("scores_done"), sem("max_ready"), sem("negmax_placed"), sem("negmaxT_done"), sem("q_with_max_ready"))
        sT_done, tanh_done, probs_ready, pv_done = sem("scoresT_done"), sem("tanh_done"), sem("probs_ready"), sem("pv_done")
        rec_ready, o_ready, oT_done, oT_ready = sem("rec_ready"), sem("o_ready"), sem("oT_done"), sem("oT_ready")
        y_done, y_used = sem("y_done"), sem("y_used")
        ln_step, ln_gain, ln_ready, squares_done = sem("ln_step"), sem("ln_gain"), sem("ln_ready"), sem("squares_done")
        o_seen, xT_seen, sim_seen = sem("o_seen"), sem("xT_seen"), sem("sim_seen")
        e_done, vT_done, e_ready, vT_ready, v_raw, v_ready = (
            sem("e_done"), sem("vT_done"), sem("e_ready"), sem("vT_ready"), sem("v_raw"), sem("v_ready"))
        xs_done, xmx_ready, nmx_ready, p_ready, pT_raw, pT_ready, xo_done, rden_ready = (
            sem("xscores_done"), sem("xmax_ready"), sem("xnegmax_ready"), sem("xprobs_ready"), sem("xprobsT_raw"),
            sem("xprobsT_ready"), sem("xout_done"), sem("rden_ready"))
        bn_done = sem("bn_done")
        xb_ready, sim_done, v8_ready, d_ready, ex_ready = (
            sem("xb_ready"), sem("sim_done"), sem("v8_ready"), sem("d_ready"), sem("ex_ready"))
        t8_ready, z_ready, rz_ready, dg_ready = (
            sem("t8_ready"), sem("z_ready"), sem("rz_ready"), sem("dg_ready"))
        ee_ready, ww_ready, g_part = sem("ee_ready"), sem("ww_ready"), sem("g_part")
        h_done, h_ready, hg_ready, m_done = sem("h_done"), sem("h_ready"), sem("hg_ready"), sem("m_done")
        y_used_x, y_used_m = sem("xout_used"), sem("memory_used")
        lg_done, lg_ready, l8_ready, nl_ready, le_ready, lw_step, lw_ready = (
            sem("lg_done"), sem("lg_ready"), sem("l8_ready"), sem("nl_ready"), sem("le_ready"), sem("lw_step"), sem("lw_ready"))
        up_done, hT_ready, down_done, acc_done = sem("up_done"), sem("hT_ready"), sem("down_done"), sem("acc_done")

        PHASE = dict(attn0=1, norm0=2, out0=3, cross0=4, bn=5, memory=6, attn1=7, cross1=8, experts=9)
        NORM = dict(attn0=0, out0=NT, cross0=2 * NT, bn=3 * NT, attn1=4 * NT, cross1=5 * NT, experts=6 * NT)
        ATTN = dict(attn0=0, attn1=NT, cross1=2 * NT)
        OUTT = dict(attn0=0, attn1=NT, cross1=2 * NT)
        PROJ = dict(out0=0, attn1=NT, cross1=2 * NT)
        XSCALE = float(P) ** -0.5
        HSCALE = float(DH) ** -0.5
        N_LOADS = 24

        block = es.enter_context(nc.Block())

        @block.sync
        def _(sp):
            loads = [
                (cst[:, :], consts), (row[:, :], rows), (col[:, :], cols), (w8[:, 0:1024], wq0), (w8[:, 1024:2048], wk0),
                (small[:, WV0, :], wv0), (small[:, WO0, :], wo0), (small[:, XWV, :], xWvT), (small[:, WV1, :], wv1),
                (small[:, WO1, :], wo1), (small[:, WOUT, :], wout), (raw[:, RWQ, :], xWq), (raw[:, RWK, :], xWk),
                (raw[:, RWE1, :], xWeT[0:P, :]), (raw[:, RWE2, :], xWeT[P:2 * P, :]),
                (rqk, wqk.rearrange("(n p) d -> p n d", p=P)), (rkey, keysT.rearrange("n p k -> p n k")), (rt[:, :], router),
                (mask4[:, :], mask), (sc[:, 0:2], scal),
                (wqk1[:, 0].rearrange("p b g c -> p (b g c)"), wq1), (wqk1[:, 1].rearrange("p b g c -> p (b g c)"), wk1),
                (sel_s[:, :, :, :].rearrange("p b g c -> p (b g c)"), headsel), (xs[:, :, :], x.rearrange("(t p) d -> p t d", p=P)),
            ]
            assert len(loads) == N_LOADS
            for dst, src in loads:
                sp.dma_start(dst, src).then_inc(loaded, 16)
            sp.dma_start(cT[:, :], ctxT).then_inc(loaded, 16)
            sp.wait_ge(phase, PHASE["norm0"])
            sp.dma_start(kin, key_inT).then_inc(tables, 16)
            sp.dma_start(kout, key_out.rearrange("(c p) d -> p c d", p=P)).then_inc(tables, 16)
            sp.wait_ge(phase, PHASE["attn1"])
            sp.dma_start(up_w, up.rearrange("e p h -> p e h")).then_inc(experts_in, 16)
            sp.dma_start(down_w, down.rearrange("e (c p) d -> p e c d", p=P)).then_inc(experts_in, 16)
            sp.wait_ge(phase, PHASE["cross1"])
            ctx_v = ctx.rearrange("(t p) d -> t p d", p=P)

            def ctx_load(T):
                need(sp, vb_ready, T.before(2, ATTN["cross1"]))
                sp.dma_start(ctile[:, T.u, :], ctx_v[T.t]).then_inc(ctx_in[T.u], 16)
            staggered(nc, sp, NT, [(0, ctx_load)])
            ov = out.rearrange("(t p) d -> p t d", p=P)
            parts = 4
            for n in range(parts):
                a, b = n * NT // parts, (n + 1) * NT // parts
                sp.wait_ge(acc_done, MOE * b)
                sp.dma_start(ov[:, a:b, :], xs[:, a:b, :]).then_inc(stored, 16)
            sp.wait_ge(stored, 16 * parts)

        @block.gpsimd
        def _(pool):
            pool.memset(ones[:, :], 1.0).then_inc(ones_ready, 1)

            def halves(base, masked):
                def seg(T):
                    u = T.u
                    if masked:
                        pool.wait_ge(kb_ready, T.now(base))
                        need(pool, s_done, T.before(2, base))
                        pool.tensor_tensor(KC[:, u], KB[:, u, :, 0:SEQ], KB[:, u, :, SEQ:P], ALU.add).then_inc(kc_ready, 1)
                    pool.wait_ge(qb_ready, T.now(base))
                    need(pool, qm_ready if masked else sT_done, T.before(2, base))
                    pool.tensor_tensor(QC[:, u], QB[:, u, :, 0:SEQ], QB[:, u, :, SEQ:P], ALU.add).then_inc(qc_ready, 1)
                return seg

            pool.wait_ge(phase, PHASE["attn0"])
            staggered(nc, pool, NT, [(0, halves(ATTN["attn0"], True))])

            pool.wait_ge(phase, PHASE["memory"])

            def outer(T):
                pool.wait_ge(ex_ready, T.now())
                for h in range(PH):
                    a, b = NKEY * h, NKEY * (PH + h)
                    need(pool, ww_ready, T.step(PH, h - 1))
                    pool.tensor_tensor(EE[:, h % 2, :].rearrange("p (i j) -> p i j", i=NKEY),
                                       EX[:, T.u, a:a + NKEY].unsqueeze(2).to_broadcast([P, NKEY, NKEY]),
                                       EX[:, T.u, b:b + NKEY].unsqueeze(1).to_broadcast([P, NKEY, NKEY]),
                                       ALU.mult).then_inc(ee_ready, 1)
            staggered(nc, pool, NT, [(0, outer)])

            pool.wait_ge(phase, PHASE["attn1"])
            staggered(nc, pool, NT, [(0, halves(ATTN["attn1"], True))])
            pool.wait_ge(phase, PHASE["cross1"])

            staggered(nc, pool, NT, [(0, halves(ATTN["cross1"], False))])

        @block.scalar
        def _(act):
            act.wait_ge(loaded, 16 * (N_LOADS + 1))
            act.activation(sc[:, 2:3], sc[:, 1:2], ACT.Exp).then_inc(bound_ready, 1)
            act.wait_ge(folds_done, 1)
            act.activation(small[:, A1, :], bank(0, 0), ACT.Copy)
            act.activation(small[:, A2, :], bank(0, P), ACT.Copy)
            act.activation(Mk[:, :], ps[:, 1, :], ACT.Copy).then_inc(folds_ready, 1)

            def deviations(n, width=NT):
                act.wait_ge(var_ready, n)
                act.activation(t64[:, 1, 0:width], t64[:, 0, 0:width], ACT.Sqrt).then_inc(std_ready, 1)

            def copy_aT(base, projected, projected_base):
                def seg(T):
                    act.wait_ge(aT_raw, T.now(base))
                    need(act, projected, T.before(2, projected_base))
                    act.activation(aT[:, T.u, :], psA, ACT.Copy).then_inc(aT_ready, 1)
                return seg

            def copy_aT_experts(T):
                act.wait_ge(aT_raw, T.now(NORM["experts"]))
                need(act, up_done, T.step(MOE, -MOE))
                act.activation(aT[:, T.u, :], psXA, ACT.Copy).then_inc(aT_ready, 1)

            def exps(base):
                def seg(T):
                    act.wait_ge(sT_done, T.now(base))
                    need(act, pv_done, T.before(2, base))
                    act.activation(PT[:, T.u], psST, ACT.Exp).then_inc(probs_ready, 1)
                return seg

            def copy_oT(base):
                def seg(T):
                    act.wait_ge(oT_done, T.now(base))
                    need(act, y_done, T.before(2, base))
                    act.activation(OT[:, T.u, :], psOT, ACT.Copy).then_inc(oT_ready, 1)
                return seg

            deviations(1)
            deviations(2)
            act.wait_ge(phase, PHASE["attn0"])

            def keep_o(T):
                act.wait_ge(oT_done, T.now())
                act.activation(o_all[:, T.t, :], psY, ACT.Copy).then_inc(oT_ready, 1)
            staggered(nc, act, NT, [(0, copy_aT(NORM["attn0"], v_done, ATTN["attn0"])), (1, exps(ATTN["attn0"])), (2, keep_o)])

            deviations(3)

            def squares(T):
                act.wait_ge(ln_ready, T.now())
                need(act, squares_done, T.before(2))
                act.activation(ytmp[:, T.u, :], o_all[:, T.t, :], ACT.Square, accum_out=tile_col(t64[:, 2, :], T))\
                    .then_inc(squares_done, 1)
            staggered(nc, act, NT, [(0, squares)])
            deviations(4)

            OTb = OT[:, :, :].bitcast(BF16)

            def copy_ints(T):
                act.wait_ge(aT_raw, T.now(NORM["out0"]))
                need(act, y_done, T.before(2, PROJ["out0"]))
                act.activation(OTb[:, T.u, 0:P], psA, ACT.Copy).then_inc(aT_ready, 1)
            staggered(nc, act, NT, [(0, copy_ints)])

            deviations(5)
            act.wait_ge(phase, PHASE["cross0"])

            def entangle(T):
                u = T.u
                act.wait_ge(e_done, T.now())
                need(act, xs_done, T.before(2))
                act.activation(ent[:, u, :], psE, ACT.Tanh, bias=sc[:, 12:13]).then_inc(e_ready, 1)
                act.wait_ge(vT_done, T.now())
                need(act, v_raw, T.before(2))
                act.activation(VT[:, u, :], psVT, ACT.Identity, bias=K("xbv")).then_inc(vT_ready, 1)

            def x_exps(T):
                u = T.u
                act.wait_ge(nmx_ready, T.now())
                need(act, pT_raw, T.before(2))
                need(act, rden_ready, T.before(2))
                for b in range(2):
                    part = slice(SEQ * b, SEQ * b + SEQ)
                    ins = act.activation(PB[part, u, part], psSx[part, :], ACT.Exp, bias=xden[part, u, 1:2], scale=XSCALE,
                                         accum_out=xden[part, u, 2:3])
                ins.then_inc(p_ready, 1)

            def copy_pT(T):
                act.wait_ge(pT_raw, T.now())
                need(act, xo_done, T.before(2))
                act.activation(PBT[:, T.u, :], psPT, ACT.Copy).then_inc(pT_ready, 1)
            staggered(nc, act, NT, [(0, copy_aT(NORM["cross0"], e_done, 0)), (2, copy_pT), (1, x_exps), (0, entangle)])

            deviations(6)

            def keep_xT(T):
                act.wait_ge(aT_raw, T.now(NORM["bn"]))
                act.activation(xTt[:, T.t, :], psA, ACT.Copy).then_inc(aT_ready, 1)
            staggered(nc, act, NT, [(0, keep_xT)])
            deviations(7, 1)

            act.wait_ge(phase, PHASE["memory"])

            def normed(T):
                need(act, sim_done, T.before(2))
                act.activation(xb[:, T.u, :], xTt[:, T.t, :], ACT.Identity, scale=sc[:, 13:14], bias=sc[:, 14:15])\
                    .then_inc(xb_ready, 1)

            def key_exps(T):
                act.wait_ge(d_ready, T.now())
                act.activation(EX[:, T.u, :], EX[:, T.u, :], ACT.Exp).then_inc(ex_ready, 1)

            def diagonals(T):
                act.wait_ge(rz_ready, T.now())
                need(act, g_part, T.step(PH, -PH))
                for h in range(PH):
                    ins = act.activation(DG[:, T.u, h, :], ident, ACT.Copy, scale=RZ[:, T.u, h:h + 1])
                ins.then_inc(dg_ready, 1)

            def hidden(T):
                act.wait_ge(h_done, T.now())
                need(act, hg_ready, T.before(1))
                act.activation(HT, psH, ACT.Gelu).then_inc(h_ready, 1)
            staggered(nc, act, NT, [(0, normed), (1, hidden), (0, key_exps), (0, diagonals)])

            deviations(8)
            act.wait_ge(phase, PHASE["attn1"])
            staggered(nc, act, NT, [(0, copy_aT(NORM["attn1"], v_done, ATTN["attn1"])), (1, exps(ATTN["attn1"])),
                                    (2, copy_oT(OUTT["attn1"]))])

            deviations(9)
            act.wait_ge(phase, PHASE["cross1"])

            def bounded_exps(T):
                base = ATTN["cross1"]
                act.wait_ge(sT_done, T.now(base))
                need(act, pv_done, T.before(2, base))
                act.activation(PT[:, T.u], psST, ACT.Tanh, scale=sc[:, 3:4]).then_inc(tanh_done, 1)
                act.wait_ge(tanh_done, T.now())
                act.activation(PT[:, T.u], PT[:, T.u], ACT.Exp, scale=sc[:, 2:3], bias=tile_col(mbias[:, :], T))\
                    .then_inc(probs_ready, 1)
            staggered(nc, act, NT, [(0, copy_aT(NORM["cross1"], q_done, ATTN["cross1"])), (1, bounded_exps),
                                    (2, copy_oT(OUTT["cross1"]))])

            deviations(10)
            act.wait_ge(phase, PHASE["experts"])

            def gelus(T):
                for e in range(MOE):
                    act.wait_ge(up_done, T.step(MOE, e + 1))
                    need(act, down_done, T.step(MOE, e + 1 - RING))
                    act.activation(hT[:, e % RING], psU[:, e % RING], ACT.Gelu_apprx_tanh).then_inc(hT_ready, 1)

            def router_exps(T):
                act.wait_ge(nl_ready, T.now())
                act.activation(le[:, T.u, :], lg[:, T.u, :], ACT.Exp, bias=ls[:, T.u, 0:1]).then_inc(le_ready, 1)
            staggered(nc, act, NT, [(0, copy_aT_experts), (1, gelus), (0, router_exps)])

        @block.tensor
        def _(pe):
            pe.wait_ge(loaded, 16 * (N_LOADS + 1))
            pe.wait_ge(ones_ready, 1)
            pe.wait_ge(quantised, 1)
            pe.matmul(bank(3, 0, 4), ones[:, :], sc[:, 4:8], start=True, stop=True).then_inc(sums_done, 1)
            pe.matmul(bank(0, 0), raw[:, RWQ, :], raw[:, RWE1, :], start=True, stop=True)
            pe.matmul(bank(0, P), raw[:, RWK, :], raw[:, RWE2, :], start=True, stop=True)
            pe.matmul(bank(4, 0, 1), raw[:, RWE1, :], K("xbq"), start=True, stop=False)
            pe.matmul(bank(4, 0, 1), raw[:, RWE2, :], K("xbk"), start=False, stop=True)
            for n in range(2 * PH):
                ins = pe.matmul(bank(1, n * NKEY, NKEY), rqk[:, n, :], rkey[:, n, :], start=True, stop=True)
            ins.then_inc(folds_done, 1)

            def transposed(base, v_placed=None, v_base=0, dst=psA):
                def seg(T):
                    pe.wait_ge(xn_ready, T.now(base))
                    need(pe, aT_ready, T.before(1, base))
                    if v_placed is not None:
                        need(pe, v_placed, T.before(1, v_base))
                    pe.transpose(dst, xn[:, T.u, :], ident).then_inc(aT_raw, 1)
                return seg

            def project(base, nbase, wq, wk, wv):
                def seg(T):
                    u = T.u
                    pe.wait_ge(aT_ready, T.now(nbase))
                    for w, to, done, copied in ((wq, psQ, q_done, qb_ready), (wk, psK, k_done, kb_ready)):
                        need(pe, copied, T.before(1, base))
                        for b in range(2):
                            for g in range(SETS):
                                src = cTv[:, T.t, b, :] if wv is None and to is psK else aT[:, u, SEQ * b:SEQ * b + SEQ]
                                ins = pe.matmul(to[:, g, SEQ * b:SEQ * b + SEQ], w[:, b, g, :], src, start=True, stop=True)
                        ins.then_inc(done, 1)
                    if wv is not None:
                        need(pe, vb_ready, T.before(1, base))
                        pe.matmul(psV, aT[:, u, :], wv, start=True, stop=True).then_inc(v_done, 1)
                return seg

            def scores(base, causal):
                def seg(T):
                    u = T.u
                    pe.wait_ge(qb_ready, T.now(base))
                    pe.wait_ge(kc_ready, T.now(base))
                    need(pe, probs_ready, T.before(1, base))
                    if causal:
                        for s in range(SLOTS):
                            pe.matmul(psS[:, s], ident_b[:, :], causal_b[:, 0, :], start=True, stop=True)
                    for g in range(SETS):
                        for s in range(SLOTS):
                            slot = slice(SLOT * s, SLOT * s + SLOT)
                            ins = pe.matmul(psS[:, s, g, :], QB[slot, u, g, :], KC[slot, u, g, :], start=not causal, stop=True,
                                            skip_group_check=True)
                    ins.then_inc(s_done, 1)
                return seg

            def max_rows(base):
                def seg(T):
                    pe.wait_ge(nm_ready, T.now(base))
                    for g in range(SETS):
                        ins = pe.matmul(psN[:, g, :], NM[:, T.u, g].rearrange("p s r -> p (s r)"), C("stack"), start=True, stop=True)
                    ins.then_inc(nmT_done, 1)
                return seg

            def scoresT(base, causal, masked):
                def seg(T):
                    u = T.u
                    pe.wait_ge(qm_ready if masked else qc_ready, T.now(base))
                    pe.wait_ge(kb_ready, T.now(base))
                    need(pe, probs_ready, T.before(1, base))
                    src = QM if masked else QC
                    if causal:
                        for s in range(SLOTS):
                            pe.matmul(psST[:, s], ident_b[:, :], causal_b[:, 1, :], start=True, stop=True)
                    for g in range(SETS):
                        for s in range(SLOTS):
                            slot = slice(SLOT * s, SLOT * s + SLOT)
                            ins = pe.matmul(psST[:, s, g, :], KB[slot, u, g, :], src[slot, u, g, :], start=not causal, stop=True,
                                            skip_group_check=True)
                    ins.then_inc(sT_done, 1)
                return seg

            def values(base, through, through_base):
                def seg(T):
                    u = T.u
                    pe.wait_ge(probs_ready, T.now(base))
                    pe.wait_ge(vb_ready, T.now(base))
                    need(pe, through, T.before(1, through_base))
                    for h in range(HEADS):
                        ins = pe.matmul(psO[:, h].rearrange("p b d -> p (b d)"), PT[:, u, h % SLOTS, h // SLOTS, :],
                                        VB[:, u, h].rearrange("p b d -> p (b d)"), start=True, stop=True)
                    ins.then_inc(pv_done, 1)
                return seg

            def output_rows(base):
                def seg(T):
                    pe.wait_ge(o_ready, T.now(base))
                    for b in range(2):
                        a = SEQ - SEQ * b
                        ins = pe.matmul(psY, C("shift")[0:SEQ, a:a + P], O[0:SEQ, T.u, b].rearrange("p h d -> p (h d)"),
                                        start=b == 0, stop=b == 1)
                    ins.then_inc(oT_done, 1)
                return seg

            def outputT(base):
                def seg(T):
                    pe.wait_ge(o_ready, T.now(base))
                    for b in range(2):
                        ins = pe.matmul(psOT[:, SEQ * b:SEQ * b + SEQ], O[0:SEQ, T.u, b].rearrange("p h d -> p (h d)"),
                                        ident[0:SEQ, 0:SEQ], start=True, stop=True)
                    ins.then_inc(oT_done, 1)
                return seg

            def out_project(ready, rbase, base, src, w):
                def seg(T):
                    pe.wait_ge(ready, T.now(rbase))
                    need(pe, y_used, T.before(1, base))
                    pe.matmul(psY, src(T.u), w, start=True, stop=True).then_inc(y_done, 1)
                return seg

            b0 = ATTN["attn0"]
            pe.wait_ge(phase, PHASE["attn0"])
            staggered(nc, pe, NT, [(0, transposed(NORM["attn0"], vb_ready, b0)),
                                   (0, project(b0, NORM["attn0"], wq0_s, wk0_s, small[:, WV0, :])), (1, scores(b0, False)),
                                   (2, values(b0, oT_ready, OUTT["attn0"])), (1, max_rows(b0)), (1, scoresT(b0, False, True)),
                                   (2, output_rows(b0))])
            pe.wait_ge(phase, PHASE["out0"])
            OTb = OT[:, :, :].bitcast(BF16)
            staggered(nc, pe, NT, [(0, transposed(NORM["out0"])),
                                   (1, out_project(aT_ready, NORM["out0"], PROJ["out0"], lambda u: OTb[:, u, 0:P], wo0_b[:, :]))])

            pe.wait_ge(phase, PHASE["cross0"])

            def entangled(T):
                u = T.u
                pe.wait_ge(aT_ready, T.now(NORM["cross0"]))
                need(pe, e_ready, T.before(1))
                pe.matmul(psE, small[:, A2, :], cTt[:, T.t, :], start=True, stop=False)
                pe.matmul(psE, small[:, A1, :], aT[:, u, :], start=False, stop=True).then_inc(e_done, 1)
                need(pe, vT_ready, T.before(1))
                pe.matmul(psVT, small[:, XWV, :], cTt[:, T.t, :], start=True, stop=True).then_inc(vT_done, 1)

            def x_scores(T):
                u = T.u
                pe.wait_ge(e_ready, T.now())
                pe.wait_ge(vT_ready, T.now())
                need(pe, p_ready, T.before(1))
                for b in range(2):
                    part = slice(SEQ * b, SEQ * b + SEQ)
                    ins = pe.matmul(psSx[part, :], ent[:, u, part], VT[:, u, part], start=True, stop=True)
                ins.then_inc(xs_done, 1)
                need(pe, v_ready, T.before(1))
                pe.transpose(psVx, VT[:, u, :], ident).then_inc(v_raw, 1)

            def x_probsT(T):
                pe.wait_ge(p_ready, T.now())
                need(pe, pT_ready, T.before(1))
                pe.transpose(psPT, PB[:, T.u, :], ident).then_inc(pT_raw, 1)

            def x_values(T):
                pe.wait_ge(pT_ready, T.now())
                pe.wait_ge(v_ready, T.now())
                need(pe, y_used_x, T.before(1))
                pe.matmul(psXO, PBT[:, T.u, :], Vt[:, T.u, :], start=True, stop=True).then_inc(xo_done, 1)
            staggered(nc, pe, NT, [(1, x_scores), (0, transposed(NORM["cross0"])), (2, x_probsT), (0, entangled), (2, x_values)])

            pe.wait_ge(phase, PHASE["bn"])
            staggered(nc, pe, NT, [(0, transposed(NORM["bn"]))])

            pe.wait_ge(phase, PHASE["memory"])
            pe.wait_ge(tables, 32)

            def key_scores(T):
                pe.wait_ge(xb_ready, T.now())
                need(pe, d_ready, T.before(1))
                pe.matmul(ps[:, 0, :], xb[:, T.u, :], Mk[:, :], start=True, stop=True).then_inc(sim_done, 1)

            def hidden(T):
                need(pe, h_ready, T.before(1))
                for c in range(CHUNKS):
                    ins = pe.matmul(psH[:, c, :], kin[:, c * P:c * P + P], xTt[:, T.t, :], start=True, stop=True)
                ins.then_inc(h_done, 1)

            def gates(first, last):
                def seg(T):
                    for h in range(first, last):
                        pe.wait_ge(ww_ready, T.step(PH, h + 1))
                        if h == 0:
                            pe.wait_ge(dg_ready, T.now())
                            need(pe, hg_ready, T.before(2))
                        for c in range(CHUNKS):
                            ins = pe.matmul(psG[T.u][:, c, :], WW[:, h % 2, c * P:c * P + P], DG[:, T.u, h, :],
                                            start=h == 0 and c % 4 == 0, stop=h == PH - 1, skip_group_check=True)
                        ins.then_inc(g_part, 1)
                return seg

            def mixed(T):
                pe.wait_ge(hg_ready, T.now())
                need(pe, y_used_m, T.before(1))
                for c in range(CHUNKS):
                    ins = pe.matmul(psM, HG[:, c, :], kout[:, c, :], start=c == 0, stop=c == CHUNKS - 1)
                ins.then_inc(m_done, 1)
            staggered(nc, pe, NT, [(0, key_scores), (1, hidden), (1, gates(0, 4)), (2, mixed), (1, gates(4, PH))])

            b1 = ATTN["attn1"]
            pe.wait_ge(phase, PHASE["attn1"])
            staggered(nc, pe, NT, [
                (0, transposed(NORM["attn1"], vb_ready, b1)),
                (3, out_project(oT_ready, OUTT["attn1"], PROJ["attn1"], lambda u: OT[:, u, :], small[:, WO1, :])),
                (0, project(b1, NORM["attn1"], wqk1[:, 0], wqk1[:, 1], small[:, WV1, :])), (1, scores(b1, True)),
                (2, values(b1, y_used, PROJ["attn1"])), (1, max_rows(b1)), (1, scoresT(b1, True, True)), (2, outputT(b1))])

            b2 = ATTN["cross1"]
            pe.wait_ge(phase, PHASE["cross1"])
            staggered(nc, pe, NT, [
                (0, transposed(NORM["cross1"])), (1, scoresT(b2, False, False)),
                (3, out_project(oT_ready, OUTT["cross1"], PROJ["cross1"], lambda u: OT[:, u, :], small[:, WOUT, :])),
                (0, project(b2, NORM["cross1"], sel_s, sel_s, None)), (2, values(b2, y_used, PROJ["cross1"])),
                (2, outputT(b2))])

            pe.wait_ge(phase, PHASE["experts"])
            pe.wait_ge(experts_in, 32)

            def route(T):
                pe.wait_ge(aT_ready, T.now(NORM["experts"]))
                need(pe, lg_ready, T.before(1))
                pe.matmul(psR, aT[:, T.u, :], rt[:, :], start=True, stop=True).then_inc(lg_done, 1)

            def up_project(T, e):
                if e == 0:
                    pe.wait_ge(aT_ready, T.now(NORM["experts"]))
                need(pe, hT_ready, T.step(MOE, e + 1 - RING))
                for c in range(HC):
                    ins = pe.matmul(psU[:, e % RING, c, :], up_w[:, e, c * P:c * P + P], aT[:, T.u, :], start=True, stop=True)
                ins.then_inc(up_done, 1)

            def down_project(T, e):
                pe.wait_ge(hT_ready, T.step(MOE, e + 1))
                need(pe, acc_done, T.step(MOE, e - 1))
                for c in range(HC):
                    ins = pe.matmul(psD[e % 2], hT[:, e % RING, c, :], down_w[:, e, c, :], start=c == 0, stop=c == HC - 1)
                ins.then_inc(down_done, 1)

            def experts_a(T):
                up_project(T, 0)
                up_project(T, 1)
                for e in range(MOE // 2):
                    up_project(T, e + 2)
                    down_project(T, e)

            def experts_b(T):
                for e in range(MOE // 2, MOE):
                    if e + 2 < MOE:
                        up_project(T, e + 2)
                    down_project(T, e)
            staggered(nc, pe, NT, [(0, transposed(NORM["experts"], dst=psXA)), (1, experts_a), (0, route), (1, experts_b)])

        @block.vector
        def _(dve):
            seen = [0]

            def rsqrt(dst, src, width=NT):
                seen[0] += 1
                dve.tensor_scalar(t64[:, 0, 0:width], src, EPS, None, ALU.add).then_inc(var_ready, 1)
                dve.wait_ge(std_ready, seen[0])
                dve.reciprocal(dst, t64[:, 1, 0:width])
                dve.drain()

            dve.wait_ge(loaded, 16 * (N_LOADS + 1))
            quant = ((w8[:, 0:1024], 2 * P * P), (w8[:, 1024:2048], 4 * SEQ * P), (small[:, WV0, :], 2 * SEQ * P),
                     (small[:, WO0, :], P * P))
            for n, (w, count) in enumerate(quant):
                dve.tensor_reduce(sc[:, 4 + n:5 + n], w, X, ALU.add, apply_absolute_value=True)
                dve.drain()
            dve.sem_inc(quantised, 1)
            dve.wait_ge(sums_done, 1)
            for n, (w, count) in enumerate(quant):
                dve.tensor_scalar(sc[:, 16 + n:17 + n], bank(3, n, 1), 1.0 / count, 1e-5, ALU.mult, ALU.max)
            dve.drain()
            dve.reciprocal(sc[:, 20:24], sc[:, 16:20])
            dve.tensor_scalar(sc[:, 24:25], sc[:, 16:17], HSCALE, None, ALU.mult)
            dve.drain()
            for n, (w, count) in enumerate(quant):
                dve.tensor_scalar(w, w, sc[:, 20 + n:21 + n], MAGIC, ALU.mult, ALU.add)
                dve.drain()
                dve.tensor_scalar(w, w, -MAGIC, 1.0, ALU.add, ALU.min)
                dve.drain()
                if n < 3:
                    dve.tensor_scalar(w, w, -1.0, sc[:, 24:25] if n == 0 else sc[:, 16 + n:17 + n], ALU.max, ALU.mult)
                else:
                    dve.tensor_scalar(wo0_b[:, :], w, -1.0, None, ALU.max)
            dve.tensor_scalar(wqk1[:, 0].rearrange("p b g c -> p (b g c)"), wqk1[:, 0].rearrange("p b g c -> p (b g c)"),
                              HSCALE, None, ALU.mult)
            for name in ("bq0", "bq1"):
                dve.tensor_scalar(K(name), K(name), HSCALE, None, ALU.mult)
            dve.tensor_copy(ident_b[:, :], ident)
            dve.tensor_copy(causal_b[:, 0, :], C("causal"))
            dve.tensor_copy(causal_b[:, 1, :], C("causalT"))
            dve.wait_ge(folds_done, 1)
            dve.tensor_tensor(sc[:, 12:13], bank(4, 0, 1), K("xbe"), ALU.add)
            dve.tensor_scalar(sc[:, 3:4], sc[:, 0:1], HSCALE, None, ALU.mult)
            dve.tensor_copy(mbias[:, :], mask4[:, :].bitcast(U8))
            dve.wait_ge(bound_ready, 1)
            dve.drain()
            dve.tensor_scalar(mbias[:, :], mbias[:, :], NEG, sc[:, 2:3], ALU.mult, ALU.subtract)
            dve.wait_ge(folds_ready, 1)

            def blank_attention():
                dve.memset(NM[:, :, :, :, :], 0.0)
                for u in range(2):
                    dve.tensor_copy(VB[:, u].rearrange("p h b d -> p (h b d)"), C("vones"))

            def bias_tiles(bq, bk, query, key):
                for g in range(SETS):
                    q_rows = C(query)[:, g * P:g * P + P] if query else None
                    if query:
                        dve.scalar_tensor_tensor(out=bmq[:, g, :], in0=C("half"), scalar=K(bq)[:, g:g + 1], in1=q_rows,
                                                 op0=ALU.mult, op1=ALU.add)
                    else:
                        dve.tensor_scalar(bmq[:, g, :], C("half"), K(bq)[:, g:g + 1], None, ALU.mult)
                    dve.scalar_tensor_tensor(out=bmk[:, g, :], in0=C("half"), scalar=K(bk)[:, g:g + 1], in1=C(key),
                                             op0=ALU.mult, op1=ALU.add)

            dve.drain()
            blank_attention()
            bias_tiles("bq0", "bk0", None, "key0")

            def row_moments():
                dve.drain()
                even, odd = st_all[:, :, 1], st_all[:, :, 4]
                dve.tensor_tensor(mv[:, 0, :], even, odd, ALU.add)
                dve.tensor_tensor(t64[:, 0, :], even, odd, ALU.subtract)
                dve.tensor_tensor(mv[:, 1, :], st_all[:, :, 2], st_all[:, :, 5], ALU.add)
                dve.drain()
                dve.tensor_scalar(mv[:, 0, :], mv[:, 0, :], 0.5, None, ALU.mult)
                dve.scalar_tensor_tensor(out=t64[:, 0, :], in0=t64[:, 0, :], scalar=0.25, in1=t64[:, 0, :], op0=ALU.mult, op1=ALU.mult)
                dve.drain()
                dve.scalar_tensor_tensor(out=mv[:, 1, :], in0=mv[:, 1, :], scalar=1.0 / P, in1=t64[:, 0, :], op0=ALU.mult, op1=ALU.add)
                dve.drain()

            def input_stats(T):
                dve.bn_stats(st_all[:, T.t, :], xs[:, T.t, :])
                dve.tensor_reduce(tile_col(t64[:, 3, :], T), xs[:, T.t, :], X, ALU.max)
                dve.tensor_reduce(tile_col(t64[:, 4, :], T), xs[:, T.t, :], X, ALU.min)
            staggered(nc, dve, NT, [(0, input_stats)])
            row_moments()
            mean, var = mv[:, 0, :], mv[:, 1, :]
            rsqrt(rs[:, :], var)
            dve.tensor_tensor(t64[:, 5, :], rs[:, :], rs[:, :], ALU.mult)
            dve.tensor_tensor(t64[:, 3, :], t64[:, 3, :], mean, ALU.subtract)
            dve.tensor_tensor(t64[:, 4, :], mean, t64[:, 4, :], ALU.subtract)
            dve.drain()
            dve.tensor_tensor(t64[:, 5, :], t64[:, 5, :], var, ALU.mult)
            dve.tensor_tensor(t64[:, 3, :], t64[:, 3, :], t64[:, 4, :], ALU.max)
            dve.drain()
            rsqrt(t64[:, 6, :], t64[:, 5, :])
            dve.tensor_tensor(rs[:, :], rs[:, :], t64[:, 6, :], ALU.mult)
            dve.drain()

            def quant_factors(largest, factor, back=None):
                dve.tensor_tensor(t64[:, 7, :], largest, factor, ALU.mult)
                dve.drain()
                dve.tensor_scalar(t64[:, 7, :], t64[:, 7, :], 1e-5, 1.0 / 127.0, ALU.max, ALU.mult)
                dve.drain()
                dve.reciprocal(t64[:, 4, :], t64[:, 7, :])
                if back is None:
                    dve.tensor_copy(s_in[:, 1, :], t64[:, 7, :])
                else:
                    dve.tensor_scalar(s_in[:, 1, :], t64[:, 7, :], back, None, ALU.mult)
                dve.drain()
                dve.tensor_tensor(s_in[:, 0, :], t64[:, 4, :], factor, ALU.mult)
                dve.drain()
            quant_factors(t64[:, 3, :], rs[:, :])
            dve.sem_inc(phase, 1)

            def quantised_rows(T):
                u = T.u
                need(dve, aT_raw, T.before(2, NORM["attn0"]))
                dve.tensor_scalar(xn[:, u, :], xs[:, T.t, :], tile_col(mv[:, 0, :], T), tile_col(s_in[:, 0, :], T), ALU.subtract, ALU.mult)\
                    .then_inc(xn_step, 1)
                dve.wait_ge(xn_step, T.step(2, 1))
                dve.tensor_scalar(xn[:, u, :], xn[:, u, :], MAGIC, -MAGIC, ALU.add, ALU.add).then_inc(xn_step, 1)
                dve.wait_ge(xn_step, T.step(2, 2))
                dve.tensor_scalar(xn[:, u, :], xn[:, u, :], tile_col(s_in[:, 1, :], T), None, ALU.mult).then_inc(xn_ready, 1)

            def normed_rows(base):
                def seg(T):
                    need(dve, aT_raw, T.before(2, base))
                    dve.tensor_scalar(xn[:, T.u, :], xs[:, T.t, :], tile_col(mv[:, 0, :], T), tile_col(rs[:, :], T), ALU.subtract, ALU.mult)\
                        .then_inc(xn_ready, 1)
                return seg

            def biased(base, bv):
                def seg(T):
                    u = T.u
                    dve.wait_ge(q_done, T.now(base))
                    need(dve, s_done if bv is not None else qc_ready, T.before(2, base))
                    dve.tensor_tensor(QB[:, u], psQ, bmq[:, :, :], ALU.add).then_inc(qb_ready, 1)
                    dve.wait_ge(k_done, T.now(base))
                    need(dve, sT_done, T.before(2, base))
                    dve.tensor_tensor(KB[:, u], psK, bmk[:, :, :], ALU.add).then_inc(kb_ready, 1)
                    if bv is None:
                        return
                    dve.wait_ge(v_done, T.now(base))
                    need(dve, pv_done, T.before(2, base))
                    for b in range(2):
                        part = slice(SEQ * b, SEQ * b + SEQ)
                        ins = dve.tensor_tensor(VB[part, u, :, b, 0:DH], psV[part, :].rearrange("p (h d) -> p h d", h=HEADS),
                                                bv[part, :].rearrange("p (h d) -> p h d", h=HEADS), ALU.add)
                    ins.then_inc(vb_ready, 1)
                return seg

            def maxima(base):
                def seg(T):
                    u = T.u
                    dve.wait_ge(s_done, T.now(base))
                    dve.tensor_reduce(mx[:, u], psS, X, ALU.max).then_inc(mx_ready, 1)
                    dve.wait_ge(mx_ready, T.now(base))
                    need(dve, nmT_done, T.before(2, base))
                    for b in range(2):
                        part = slice(SEQ * b, SEQ * b + SEQ)
                        ins = dve.tensor_scalar(NM[part, u, :, :, FOLD_MAX + b].rearrange("p g s -> p s g"), mx[part, u], -1.0, None,
                                                ALU.mult)
                    ins.then_inc(nm_ready, 1)
                return seg

            def less_max(base):
                def seg(T):
                    dve.wait_ge(nmT_done, T.now(base))
                    dve.wait_ge(qc_ready, T.now(base))
                    need(dve, sT_done, T.before(2, base))
                    dve.tensor_tensor(QM[:, T.u], QC[:, T.u], psN, ALU.add).then_inc(qm_ready, 1)
                return seg

            def normalised(base, obase):
                def seg(T):
                    u = T.u
                    dve.wait_ge(pv_done, T.now(base))
                    dve.reciprocal(rec[0:SEQ, u], psO[:, :, :, DH]).then_inc(rec_ready, 1)
                    dve.wait_ge(rec_ready, T.now(base))
                    need(dve, oT_done, T.before(2, obase))
                    dve.tensor_tensor(O[0:SEQ, u].rearrange("p b h d -> p h b d"), psO[:, :, :, 0:DH],
                                      rec[0:SEQ, u].unsqueeze(3).to_broadcast([SEQ, HEADS, 2, DH]), ALU.mult).then_inc(o_ready, 1)
                return seg

            def stats_of_new(T):
                dve.drain()
                dve.bn_stats(st_all[:, T.t, :], xs[:, T.t, :])

            def add_output(name, bias, scale=None):
                base = PROJ[name]

                def seg(T):
                    u = T.u
                    dve.wait_ge(y_done, T.now(base))
                    if bias is None:
                        dve.tensor_tensor(xs[:, T.t, :], psY, xs[:, T.t, :], ALU.add).then_inc(y_used, 1)
                        stats_of_new(T)
                        return
                    if scale is None:
                        dve.tensor_tensor(ytmp[:, u, :], psY, bias, ALU.add).then_inc(y_used, 1)
                    else:
                        dve.scalar_tensor_tensor(out=ytmp[:, u, :], in0=psY, scalar=tile_col(scale[:, :], T), in1=bias, op0=ALU.mult,
                                                 op1=ALU.add).then_inc(y_used, 1)
                    dve.wait_ge(y_used, T.now(base))
                    dve.tensor_tensor(xs[:, T.t, :], xs[:, T.t, :], ytmp[:, u, :], ALU.add)
                    stats_of_new(T)
                return seg

            def output_stats(T):
                dve.wait_ge(oT_ready, T.now())
                dve.sem_inc(o_seen, 1)
                dve.bn_stats(st_all[:, T.t, :], o_all[:, T.t, :])
            b0 = ATTN["attn0"]
            staggered(nc, dve, NT, [(0, quantised_rows), (0, biased(b0, R("bv0"))), (1, maxima(b0)), (2, normalised(b0, OUTT["attn0"])),
                                    (1, less_max(b0)), (3, output_stats)])
            row_moments()
            rsqrt(rs[:, :], var)
            dve.sem_inc(phase, 1)

            def output_norm(T):
                o = o_all[:, T.t, :]
                dve.tensor_scalar(o, o, tile_col(mv[:, 0, :], T), tile_col(rs[:, :], T), ALU.subtract, ALU.mult).then_inc(ln_step, 1)

            def output_gain(T):
                o = o_all[:, T.t, :]
                dve.wait_ge(ln_step, T.now())
                dve.tensor_tensor(o, o, R("g0"), ALU.mult).then_inc(ln_gain, 1)

            def output_shift(T):
                o = o_all[:, T.t, :]
                dve.wait_ge(ln_gain, T.now())
                dve.tensor_tensor(o, o, R("b0"), ALU.add).then_inc(ln_ready, 1)

            def output_max(T):
                dve.wait_ge(ln_ready, T.now())
                dve.tensor_reduce(tile_col(t64[:, 3, :], T), o_all[:, T.t, :], X, ALU.max, apply_absolute_value=True)
            staggered(nc, dve, NT, [(0, output_norm), (1, output_gain), (2, output_shift), (3, output_max)])
            dve.wait_ge(squares_done, NT)
            dve.drain()
            dve.tensor_scalar(t64[:, 5, :], t64[:, 2, :], 1.0 / P, None, ALU.mult)
            dve.drain()
            rsqrt(t64[:, 6, :], t64[:, 5, :])
            quant_factors(t64[:, 3, :], t64[:, 6, :], sc[:, 19:20])
            dve.sem_inc(phase, 1)

            def quantised_output(T):
                u = T.u
                need(dve, aT_raw, T.before(2, NORM["out0"]))
                dve.tensor_scalar(xn[:, u, :], o_all[:, T.t, :], tile_col(s_in[:, 0, :], T), MAGIC, ALU.mult, ALU.add).then_inc(xn_step, 1)
                dve.wait_ge(xn_step, T.step(1, 2 * NT + 1))
                dve.tensor_scalar(xn[:, u, :], xn[:, u, :], -MAGIC, None, ALU.add).then_inc(xn_ready, 1)
            staggered(nc, dve, NT, [(0, quantised_output), (2, add_output("out0", R("bo0"), s_in[:, 1, :]))])

            row_moments()
            rsqrt(rs[:, :], var)
            dve.memset(PB[:, :, :], 0.0)
            dve.drain()
            dve.sem_inc(phase, 1)

            def x_maxima(T):
                u = T.u
                dve.wait_ge(xs_done, T.now())
                need(dve, p_ready, T.before(2))
                dve.tensor_reduce(xden[:, u, 0:1], psSx, X, ALU.max).then_inc(xmx_ready, 1)
                dve.wait_ge(xmx_ready, T.now())
                dve.tensor_scalar(xden[:, u, 1:2], xden[:, u, 0:1], -XSCALE, None, ALU.mult).then_inc(nmx_ready, 1)
                dve.wait_ge(v_raw, T.now())
                need(dve, xo_done, T.before(2))
                dve.tensor_copy(Vt[:, u, :], psVx).then_inc(v_ready, 1)

            def add_cross(T):
                u = T.u
                dve.wait_ge(p_ready, T.now())
                dve.reciprocal(xden[:, u, 3:4], xden[:, u, 2:3]).then_inc(rden_ready, 1)
                dve.wait_ge(rden_ready, T.now())
                dve.wait_ge(xo_done, T.now())
                dve.scalar_tensor_tensor(out=xs[:, T.t, :], in0=psXO, scalar=xden[:, u, 3:4], in1=xs[:, T.t, :], op0=ALU.mult,
                                         op1=ALU.add).then_inc(y_used_x, 1)
                stats_of_new(T)
            staggered(nc, dve, NT, [(0, normed_rows(NORM["cross0"])), (1, x_maxima), (2, add_cross)])

            row_moments()
            rsqrt(rs[:, :], var)
            dve.sem_inc(phase, 1)

            def feature_stats(T):
                dve.wait_ge(aT_ready, T.now(NORM["bn"]))
                dve.sem_inc(xT_seen, 1)
                dve.bn_stats(bnst[:, T.t, :], xTt[:, T.t, :]).then_inc(bn_done, 1)
            staggered(nc, dve, NT, [(0, normed_rows(NORM["bn"])), (1, feature_stats)])
            dve.wait_ge(bn_done, NT)
            dve.bn_aggr(sc[:, 26:28], bnst[:, :, :].rearrange("p t s -> p (t s)"))
            dve.drain()
            rsqrt(sc[:, 28:29], sc[:, 27:28], 1)
            dve.tensor_tensor(sc[:, 13:14], sc[:, 28:29], K("gamma"), ALU.mult)
            dve.drain()
            dve.tensor_tensor(sc[:, 29:30], sc[:, 26:27], sc[:, 13:14], ALU.mult)
            dve.drain()
            dve.tensor_tensor(sc[:, 14:15], K("beta"), sc[:, 29:30], ALU.subtract)
            dve.wait_ge(aT_ready, NORM["bn"] + NT)
            dve.drain()
            dve.sem_inc(phase, 1)

            def top_keys(T):
                u = T.u
                dve.wait_ge(sim_done, T.now())
                dve.sem_inc(sim_seen, 1)
                sim = ps[:, 0, :].rearrange("p (n k) -> p n k", k=NKEY)
                for n in range(2 * PH):
                    ins = dve.max(V8[:, u, n, :], sim[:, n, :])
                ins.then_inc(v8_ready, 1)
                dve.wait_ge(v8_ready, T.now())
                need(dve, ee_ready, T.step(PH, -PH))
                dve.tensor_tensor(EX[:, u, NS:].rearrange("p (n k) -> p n k", k=TOPK), V8[:, u],
                                  V8[:, u, :, 0:1].to_broadcast([P, 2 * PH, TOPK]), ALU.subtract)
                dve.tensor_tensor(EX[:, u, 0:NS].rearrange("p (n k) -> p n k", k=NKEY), sim,
                                  V8[:, u, :, 0:1].to_broadcast([P, 2 * PH, NKEY]), ALU.subtract).then_inc(d_ready, 1)

            def top_pairs(T):
                u = T.u
                dve.wait_ge(ex_ready, T.now())
                best = EX[:, u, NS:].rearrange("p (n k) -> p n k", k=TOPK)
                dve.tensor_tensor(CD.rearrange("p h (i j) -> p h i j", i=TOPK),
                                  best[:, 0:PH].unsqueeze(3).to_broadcast([P, PH, TOPK, TOPK]),
                                  best[:, PH:].unsqueeze(2).to_broadcast([P, PH, TOPK, TOPK]), ALU.mult)
                dve.drain()
                for h in range(PH):
                    ins = dve.max(T8[:, u, h, :], CD[:, h, :])
                ins.then_inc(t8_ready, 1)
                dve.wait_ge(t8_ready, T.now())
                dve.tensor_reduce(Z[:, u, :], T8[:, u], X, ALU.add).then_inc(z_ready, 1)
                dve.wait_ge(z_ready, T.now())
                need(dve, dg_ready, T.before(2))
                dve.reciprocal(RZ[:, u, :], Z[:, u, :]).then_inc(rz_ready, 1)

            def chosen(first, last):
                def seg(T):
                    for h in range(first, last):
                        if h == 0:
                            dve.wait_ge(t8_ready, T.now())
                        dve.wait_ge(ee_ready, T.step(PH, h + 1))
                        need(dve, g_part, T.step(PH, h - 1))
                        dve.scalar_tensor_tensor(out=WW[:, h % 2, :], in0=EE[:, h % 2, :], scalar=T8[:, T.u, h, TOPK - 1:TOPK],
                                                 in1=EE[:, h % 2, :], op0=ALU.is_ge, op1=ALU.mult).then_inc(ww_ready, 1)
                return seg

            def gated(T):
                dve.wait_ge(h_ready, T.now())
                dve.wait_ge(g_part, T.step(PH, PH))
                need(dve, m_done, T.before(1))
                dve.tensor_tensor(HG, psG[T.u], HT, ALU.mult).then_inc(hg_ready, 1)

            def add_memory(T):
                dve.wait_ge(m_done, T.now())
                dve.tensor_tensor(xs[:, T.t, :], psM, xs[:, T.t, :], ALU.add).then_inc(y_used_m, 1)
                stats_of_new(T)
            staggered(nc, dve, NT, [(2, gated), (1, chosen(0, 2)), (0, top_keys), (1, chosen(2, 5)), (2, add_memory), (0, top_pairs),
                                    (1, chosen(5, PH))])

            row_moments()
            rsqrt(rs[:, :], var)
            blank_attention()
            bias_tiles("bq1", "bk1", "query1", "key1")
            dve.drain()
            dve.sem_inc(phase, 1)
            b1 = ATTN["attn1"]
            staggered(nc, dve, NT, [(0, normed_rows(NORM["attn1"])), (3, add_output("attn1", R("bo1"))), (0, biased(b1, R("bv1"))),
                                    (1, maxima(b1)), (2, normalised(b1, OUTT["attn1"])), (1, less_max(b1))])

            row_moments()
            rsqrt(rs[:, :], var)
            dve.memset(bmq[:, :, :], 0.0)
            dve.memset(bmk[:, :, :], 0.0)
            dve.drain()
            dve.sem_inc(phase, 1)
            b2 = ATTN["cross1"]

            def ctx_values(T):
                u = T.u
                dve.wait_ge(ctx_in[u], T.pair * 16 + 16)
                need(dve, pv_done, T.before(2, b2))
                for b in range(2):
                    part = slice(SEQ * b, SEQ * b + SEQ)
                    ins = dve.tensor_copy(VB[part, u, :, b, 0:DH], ctile[part, u, :].rearrange("p (h d) -> p h d", h=HEADS))
                ins.then_inc(vb_ready, 1)
            staggered(nc, dve, NT, [(0, normed_rows(NORM["cross1"])), (3, add_output("cross1", None)), (0, biased(b2, None)),
                                    (0, ctx_values),
                                    (2, normalised(b2, OUTT["cross1"]))])

            row_moments()
            rsqrt(rs[:, :], var)
            dve.sem_inc(phase, 1)

            def logits(T):
                u = T.u
                dve.wait_ge(lg_done, T.now())
                need(dve, le_ready, T.before(2))
                dve.tensor_copy(lg[:, u, :], psR).then_inc(lg_ready, 1)
                dve.drain()
                dve.max(l8[:, u, :], lg[:, u, :]).then_inc(l8_ready, 1)
                dve.wait_ge(l8_ready, T.now())
                dve.tensor_scalar(ls[:, u, 0:1], l8[:, u, 0:1], -1.0, None, ALU.mult).then_inc(nl_ready, 1)

            def route_weights(T):
                u = T.u
                dve.wait_ge(le_ready, T.now())
                dve.scalar_tensor_tensor(out=lw[:, u, :], in0=lg[:, u, :], scalar=l8[:, u, MOE_K - 1:MOE_K], in1=le[:, u, :],
                                         op0=ALU.is_ge, op1=ALU.mult).then_inc(lw_step, 1)
                dve.wait_ge(lw_step, T.step(3, 1))
                dve.tensor_reduce(ls[:, u, 1:2], lw[:, u, :], X, ALU.add).then_inc(lw_step, 1)
                dve.wait_ge(lw_step, T.step(3, 2))
                dve.reciprocal(ls[:, u, 2:3], ls[:, u, 1:2]).then_inc(lw_step, 1)
                dve.wait_ge(lw_step, T.step(3, 3))
                dve.tensor_scalar(lw[:, u, :], lw[:, u, :], ls[:, u, 2:3], None, ALU.mult).then_inc(lw_ready, 1)

            def add_experts(first, last):
                def seg(T):
                    for e in range(first, last):
                        if e == 0:
                            dve.wait_ge(lw_ready, T.now())
                        else:
                            dve.wait_ge(acc_done, T.step(MOE, e))
                        dve.wait_ge(down_done, T.step(MOE, e + 1))
                        dve.scalar_tensor_tensor(out=xs[:, T.t, :], in0=psD[e % 2], scalar=lw[:, T.u, e:e + 1],
                                                 in1=xs[:, T.t, :], op0=ALU.mult, op1=ALU.add).then_inc(acc_done, 1)
                return seg
            staggered(nc, dve, NT, [(0, normed_rows(NORM["experts"])), (1, add_experts(0, 4)), (0, logits), (1, add_experts(4, MOE)),
                                    (0, route_weights)])


def slotted(w):
    heads = w.reshape(-1, DH, P)
    heads = np.repeat(heads, HEADS // len(heads), axis=0)
    out = np.zeros((P, 2, SETS, SLOTS, SLOT), np.float32)
    for b in range(2):
        out[:, b, :, :, DH * b:DH * b + DH] = heads.reshape(SETS, SLOTS, DH, P).transpose(3, 0, 1, 2)
    return out.reshape(P, -1)


def slotted_bias(b):
    heads = b.reshape(-1, DH)
    heads = np.repeat(heads, HEADS // len(heads), axis=0).reshape(SETS, SLOTS, DH)
    out = np.zeros((SLOTS, SLOT, SETS), np.float32)
    for n in range(2):
        out[:, DH * n:DH * n + DH, :] = heads.transpose(1, 2, 0)
    return out.reshape(P, SETS)


def constants():
    c = np.zeros((P, CONSTS), np.float32)

    def put(name, a):
        at, n = CONST[name]
        c[:a.shape[0], at:at + n] = a.reshape(a.shape[0], n)

    tok = np.arange(P)
    entry, pos = tok // SEQ, tok % SEQ
    r = np.arange(P) % SLOT
    own = lambda first: (r[:, None] - first == entry[None, :]).astype(np.float32)
    put("ident", np.eye(P))
    put("half", (r[:, None] // DH == entry[None, :]).astype(np.float32))
    put("key0", own(FOLD_MAX))
    put("key1", own(FOLD_MAX) + own(FOLD_MAX + 2) * pos + own(FOLD_MAX + 4))
    start = 2.0 ** (-8.0 / HEADS)
    slopes = np.array([start * start ** i for i in range(HEADS)], np.float32)
    head = SLOTS * np.arange(SETS)[None, :] + (np.arange(P) // SLOT)[:, None]
    s = slopes[head][:, :, None]
    put("query1", own(FOLD_MAX + 2)[:, None, :] * s - own(FOLD_MAX + 4)[:, None, :] * s * pos)
    late = np.where(np.arange(SEQ)[None, :] > pos[:, None], NEG, 0.0)
    put("causal", np.tile(late, (1, SETS)))
    early = np.where(pos[:, None] > np.arange(SEQ)[None, :], NEG, 0.0)
    put("causalT", np.tile(early, (1, SETS)))
    put("stack", (pos[:, None] == np.arange(SEQ)[None, :]).astype(np.float32))
    put("shift", (np.arange(SEQ)[:, None] + SEQ == np.arange(3 * SEQ)[None, :]).astype(np.float32))
    v = np.zeros((P, HEADS, 2, DH + 1), np.float32)
    for b in range(2):
        v[SEQ * b:SEQ * b + SEQ, :, b, DH] = 1.0
    put("vones", v)
    return c


def layout(i):
    f = lambda name: np.asarray(i[name])
    D = P
    tokens = f("x").shape[0] * SEQ
    x = f("x").reshape(tokens, D)
    ctx = f("ctx_1024").reshape(tokens, D)
    repeat = lambda w: np.repeat(w.reshape(-1, DH, *w.shape[1:]), 2, axis=0).reshape(D, *w.shape[1:])
    rows = (repeat(f("L0_attn_bv")), f("L0_attn_bo"), f("L0_attn_ln_g"), f("L0_attn_ln_b"), f("L1_attn_v_b"), f("L1_attn_o_b"))
    cols = [f(n)[:, None] for n in ("L0_xattn_bq", "L0_xattn_bk", "L0_xattn_bv", "L0_xattn_be", "L0_ffn_gamma", "L0_ffn_beta")]
    cols += [slotted_bias(f(n)) for n in ("L0_attn_bq", "L0_attn_bk", "L1_attn_q_b", "L1_attn_k_b")]
    a = dict(
        x=x, ctxT=ctx.T, ctx=ctx, mask=np.ascontiguousarray(f("mask_Bx1xS2_bk0").reshape(-1, D).T).view(np.uint32), consts=constants(),
        rows=np.broadcast_to(np.concatenate(rows)[None], (D, len(rows) * D)), cols=np.concatenate(cols, axis=1),
        wq0=slotted(f("L0_attn_wq")), wk0=slotted(f("L0_attn_wk")), wv0=repeat(f("L0_attn_wv")).T, wo0=f("L0_attn_wo").T,
        xWq=f("L0_xattn_Wq"), xWk=f("L0_xattn_Wk"), xWvT=f("L0_xattn_Wv").T, xWeT=f("L0_xattn_We").T,
        wqk=f("L0_ffn_w_q"), keysT=f("L0_ffn_keys").transpose(2, 0, 3, 1).reshape(2 * PH, D, NKEY),
        key_inT=f("L0_ffn_key_in").T, key_out=f("L0_ffn_key_out"),
        wq1=slotted(f("L1_attn_q_w")), wk1=slotted(f("L1_attn_k_w")), wv1=f("L1_attn_v_w").T, wo1=f("L1_attn_o_w").T,
        headsel=slotted(np.eye(D, dtype=np.float32)), wout=f("L1_xattn_W_out").T,
        scal=np.broadcast_to(np.stack([f("L1_xattn_scale"), f("L1_xattn_log_C")])[None], (D, 2)),
        router=f("L1_ffn_router_w"), up=f("L1_ffn_up_w"), down=f("L1_ffn_down_w"))
    return {k: np.ascontiguousarray(v) for k, v in a.items()}


def kernel(**inputs):
    import concourse.bacc as bacc
    from concourse.bass_utils import run_bass_kernel_spmd as run

    nc = bacc.Bacc("TRN2", target_bir_lowering=False, num_devices=1)
    arrays = {f"in_{k}": v for k, v in layout(inputs).items()}
    args = [nc.dram_tensor(k, v.shape, mybir.dt.from_np(v.dtype), kind="ExternalInput").ap() for k, v in arrays.items()]
    out = nc.dram_tensor("out", arrays["in_x"].shape, F32, kind="ExternalOutput").ap()
    build(nc, *args, out)
    r = run(nc, [arrays], core_ids=[0])
    return r.results[0]["out"].reshape(np.asarray(inputs["x"]).shape)
```

```python
from contextlib import ExitStack

import numpy as np

import concourse.bass as bass
from concourse import mybir

P = 128
SEQ = 64
HEADS = 16
DH = P // HEADS
PAIRS = HEADS // 2
ROWS2 = 2 * DH
PER_SET = P // ROWS2
SETS = HEADS // PER_SET
PARTS = 3
MASK_ROWS = SEQ + 2 * PARTS
EPS = 1e-5
MAGIC = 1.5 * 2.0 ** 23
NEG = -1e30
NKEY = 32
PH = 8
TOPK = 8
NEXP = NKEY * NKEY
CHUNKS = NEXP // P
MOE = 8
MOE_K = 4
HID = 512

F32 = mybir.dt.float32
BF16 = mybir.dt.bfloat16
U8 = mybir.dt.uint8
U32 = mybir.dt.uint32
ALU = mybir.AluOpType
ACT = mybir.ActivationFunctionType
X = mybir.AxisListType.X

CONST = {}
_at = 0
for _name, _n in (("ident", P), ("own_entry", P), ("own_head", PER_SET), ("mask_q", P), ("mask_k", HEADS * SEQ),
                  ("vones_pairs", PAIRS * 4 * (DH + 1)), ("vones_heads", HEADS * 2 * (DH + 1))):
    CONST[_name] = (_at, _n)
    _at += _n
CONSTS = _at
ROWS = ("bv0", "bo0", "g0", "b0", "bv1", "bo1")
COLS = {"xbq": (0, 1), "xbk": (1, 1), "xbv": (2, 1), "xbe": (3, 1), "gamma": (4, 1), "beta": (5, 1), "own": (6, 2),
        "bq0": (8, SETS), "bk0": (8 + SETS, SETS), "bq1": (8 + 2 * SETS, SETS), "bk1": (8 + 3 * SETS, SETS)}
NCOLS = 8 + 4 * SETS


class Tile:

    def __init__(self, t, u, pair):
        self.t, self.u, self.pair = t, u, pair

    def now(self, base=0):
        return self.t + (base + 1)

    def before(self, n, base=0):
        return self.t + (base + 1 - n)

    def ahead(self, n, base, tiles):
        if isinstance(self.t, int):
            return min(self.t + n, tiles - 1) + base + 1
        return self.t + (base + 1 + n)

    def step(self, per_tile, k, base=0):
        return self.t * per_tile + (base * per_tile + k)


def need(eng, sem, value):
    if isinstance(value, int) and value <= 0:
        return
    eng.wait_ge(sem, value)


def tile_col(block, T):
    return block.rearrange("p (t o) -> p t o", o=1)[:, T.t, :]


def staggered(nc, eng, tiles, segments):
    lag = max(l for l, _ in segments)
    peel = lag + 2 + lag % 2
    for s in range(peel):
        for l, seg in segments:
            if s >= l:
                seg(Tile(s - l, (s - l) % 2, (s - l) // 2))
    with nc.Fori(peel // 2, tiles // 2, engines=[eng.engine]) as i:
        for u in range(2):
            for l, seg in segments:
                seg(Tile(2 * i + (u - l), (u - l) % 2, i + (u - l) // 2))
    for s in range(tiles, tiles + lag):
        for l, seg in segments:
            if s - l < tiles:
                seg(Tile(s - l, (s - l) % 2, (s - l) // 2))


def build(nc, x, ctxT, ctx, mask, consts, rows, cols, wq0, wk0, wv0, wo0, xWq, xWk, xWvT, xWeT, wqk, keysT, key_inT,
          key_out, wq1, wk1, wv1, wo1, selq, selk, wout, scal, router, up, down, out):
    NT = x.shape[0] // P
    with ExitStack() as es:
        def sb(name, shape, dt=F32):
            return es.enter_context(nc.sbuf_tensor(name, shape, dt))

        def sem(name):
            return es.enter_context(nc.semaphore(name))

        xs = sb("x_all", [P, NT, P])
        cT = sb("ctxT_all", [P, NT * P])
        big = sb("big", [P, 8192])
        o_all = big[:, 0:NT * P].rearrange("p (t d) -> p t d", d=P)
        xT_all = big[:, 0:NT * P]
        up_w = big[:, 0:MOE * HID].rearrange("p (e h) -> p e h", e=MOE)
        down_w = big[:, MOE * HID:2 * MOE * HID].rearrange("p (e c d) -> p e c d", e=MOE, c=HID // P)
        cst = sb("consts_sb", [P, CONSTS])
        row = sb("rows_sb", [P, len(ROWS) * P])
        col = sb("cols_sb", [P, NCOLS])
        w8 = sb("w8", [P, 2048])
        wq0_s = w8[:, 0:SETS * P].rearrange("p (g c) -> p g c", g=SETS)
        wk0_s = w8[:, SETS * P:3 * SETS * P].rearrange("p (b g c) -> p b g c", b=2, g=SETS)
        kin = w8[:, 0:NEXP]
        kout = w8[:, 1024:2048].rearrange("p (c d) -> p c d", c=CHUNKS)
        wq1_s = sb("wq1_sb", [P, SETS, P])
        wk1_s = sb("wk1_sb", [P, 2, SETS, P])
        selq_s = sb("selq_sb", [P, 2, SETS, P])
        selk_s = sb("selk_sb", [P, SETS, P])
        small = sb("small_w", [P, 8, P])
        WV0, WO0, A1, A2, XWV, WV1, WO1, WOUT = range(8)
        wo0_b = sb("wo0_bf", [P, P], BF16)
        rt = sb("router_sb", [P, MOE])
        Mk = sb("Mk", [P, 2 * PH * NKEY])
        bq_own = sb("bq_own", [P, SETS, 2])
        bk_s = sb("bk", [P, SETS])
        maskq_b = sb("mask_q_bf", [P, P], BF16)
        maskk_b = sb("mask_k_bf", [P, 2, HEADS * SEQ // 2], BF16)
        mv = sb("mv", [P, 2, NT])
        st_all = sb("st_all", [P, NT, 6])
        rs = sb("rstd", [P, NT])
        t64 = sb("t64", [P, 8, NT])
        sc = sb("scalars", [P, 32])
        mask4 = sb("mask4", [P, NT // 4], U32)
        mbias = sb("mbias", [P, NT])
        ones = sb("ones", [P, P])
        s_in = sb("quant_scale", [P, 2, NT])
        bnst = sb("bn_stats_all", [P, NT, 6])

        def C(name):
            a, n = CONST[name]
            return cst[:, a:a + n]

        def R(name):
            a = ROWS.index(name) * P
            return row[:, a:a + P]

        def K(name):
            a, n = COLS[name]
            return col[:, a:a + n]

        ident = C("ident")

        WORK = 10752
        work = sb("work", [P, WORK])
        top = [0]

        def carve(n):
            a = top[0]
            top[0] += n
            assert top[0] <= WORK, top[0]
            return work[:, a:a + n]

        xn = carve(2 * P).rearrange("p (u d) -> p u d", u=2)
        aT = carve(2 * P).rearrange("p (u d) -> p u d", u=2)
        after_aT = top[0]
        QB = carve(2 * SETS * P).rearrange("p (u g c) -> p u g c", u=2, g=SETS)
        KC = carve(2 * SETS * SEQ).rearrange("p (u g k) -> p u g k", u=2, g=SETS)
        KX = carve(2 * HEADS * SEQ).rearrange("p (u g n) -> p u g n", u=2, g=SETS)
        VB = carve(2 * PAIRS * 4 * (DH + 1)).rearrange("p (u n) -> p u n", u=2)
        VBp = VB.rearrange("p u (b i h d) -> p u b i h d", b=2, i=PAIRS, h=2)
        VBh = VB.rearrange("p u (h b d) -> p u h b d", h=HEADS, b=2)
        PQ = carve(2 * HEADS * SEQ).rearrange("p (u n) -> p u n", u=2)
        PT = carve(2 * HEADS * SEQ).rearrange("p (u n) -> p u n", u=2)
        O = carve(2 * 2 * P).rearrange("p (u b d) -> p u b d", u=2, b=2)
        OT = carve(2 * P).rearrange("p (u d) -> p u d", u=2)
        mx = carve(2 * HEADS).rearrange("p (u h) -> p u h", u=2)
        rec = carve(2 * HEADS * 2).rearrange("p (u n) -> p u n", u=2)
        ctile = carve(2 * P).rearrange("p (u d) -> p u d", u=2)
        ytmp = carve(2 * P).rearrange("p (u d) -> p u d", u=2)
        top[0] = 0
        raw = carve(4 * P).rearrange("p (n d) -> p n d", n=4)
        RWQ, RWK, RWE1, RWE2 = range(4)
        rqk = carve(2 * PH * P).rearrange("p (n d) -> p n d", n=2 * PH)
        rkey = carve(2 * PH * NKEY).rearrange("p (n d) -> p n d", n=2 * PH)
        top[0] = after_aT
        ent = carve(2 * P).rearrange("p (u d) -> p u d", u=2)
        VT = carve(2 * P).rearrange("p (u d) -> p u d", u=2)
        Vt = carve(2 * P).rearrange("p (u d) -> p u d", u=2)
        PB = carve(2 * P).rearrange("p (u d) -> p u d", u=2)
        PBT = carve(2 * P).rearrange("p (u d) -> p u d", u=2)
        xden = carve(8).rearrange("p (u n) -> p u n", u=2)
        top[0] = 0
        NS = 2 * PH * NKEY
        xb = carve(2 * P).rearrange("p (u d) -> p u d", u=2)
        EX = carve(2 * (NS + 2 * PH * TOPK)).rearrange("p (u n) -> p u n", u=2)
        V8 = carve(2 * 2 * PH * TOPK).rearrange("p (u n k) -> p u n k", u=2, k=TOPK)
        CD = carve(PH * TOPK * TOPK).rearrange("p (h n) -> p h n", h=PH)
        T8 = carve(2 * PH * TOPK).rearrange("p (u h k) -> p u h k", u=2, k=TOPK)
        Z = carve(2 * PH).rearrange("p (u h) -> p u h", u=2)
        RZ = carve(2 * PH).rearrange("p (u h) -> p u h", u=2)
        DG = carve(2 * PH * P).rearrange("p (u h d) -> p u h d", u=2, h=PH)
        EE = carve(2 * NEXP).rearrange("p (u n) -> p u n", u=2)
        WW = carve(2 * NEXP).rearrange("p (u n) -> p u n", u=2)
        HT = carve(NEXP).rearrange("p (c d) -> p c d", c=CHUNKS)
        HG = carve(NEXP).rearrange("p (c d) -> p c d", c=CHUNKS)
        HC = HID // P
        RING = 4
        top[0] = after_aT
        hT = carve(RING * HID).rearrange("p (n c d) -> p n c d", n=RING, c=HC)
        lg = carve(2 * MOE).rearrange("p (u e) -> p u e", u=2)
        l8 = carve(2 * MOE).rearrange("p (u e) -> p u e", u=2)
        le = carve(2 * MOE).rearrange("p (u e) -> p u e", u=2)
        lw = carve(2 * MOE).rearrange("p (u e) -> p u e", u=2)
        ls = carve(8).rearrange("p (u e) -> p u e", u=2)

        ps = es.enter_context(nc.psum_tensor("ps", [P, 8, 512], F32))

        def bank(b, a, n=P):
            return ps[:, b, a:a + n]

        psS = ps[:, 0:2, :].rearrange("p b (n k) -> p (b n) k", k=SEQ)
        psPT = ps[:, 2:4, :]
        psST = [ps[:, 2 * u:2 * u + 2, :] for u in range(2)]
        psA, psOT = bank(4, 0), bank(4, P)
        psQ = bank(4, 2 * P, SETS * P).rearrange("p (g c) -> p g c", g=SETS)
        psKc = bank(5, 0, SETS * SEQ).rearrange("p (g c) -> p g c", g=SETS)
        psKd = bank(6, 2 * P, SETS * P).rearrange("p (g c) -> p g c", g=SETS)
        psV, psY = bank(6, 0), bank(6, P)
        psOq = bank(7, 0, HEADS * (DH + 1)).rearrange("p (h d) -> p h d", h=HEADS)
        psOh = ps[0:SEQ, 7, 0:HEADS * 2 * (DH + 1)].rearrange("p (h b d) -> p h b d", h=HEADS, b=2)
        psE, psVT, psVx, psSx, psXT, psXO = bank(0, 0), bank(1, 0), bank(3, 0), bank(2, 0, SEQ), bank(5, 0), bank(6, 0)
        psG = [ps[:, 1:3, :].rearrange("p b (c d) -> p (b c) d", d=P), ps[:, 3:5, :].rearrange("p b (c d) -> p (b c) d", d=P)]
        psH = ps[:, 5:7, :].rearrange("p b (c d) -> p (b c) d", d=P)
        psM = bank(7, 0)
        psU = ps[:, 0:RING, :].rearrange("p n (c d) -> p n c d", d=P)
        psD = [bank(4, 0), bank(5, 0)]
        psXA, psR = bank(6, 0), bank(7, 0, MOE)

        cTv = cT[:, :].rearrange("p (t b q) -> p t b q", b=2, q=SEQ)
        cTt = cT[:, :].rearrange("p (t d) -> p t d", d=P)
        xTt = xT_all.rearrange("p (t d) -> p t d", d=P)

        loaded, tables, experts_in, stored = sem("loaded"), sem("tables_loaded"), sem("experts_loaded"), sem("stored")
        ctx_in = [sem("ctx_tile0_in"), sem("ctx_tile1_in")]
        ones_ready, sums_done, quantised, folds_done, folds_ready, bound_ready = (
            sem("ones_ready"), sem("sums_done"), sem("quantised"), sem("folds_done"), sem("folds_ready"), sem("bound_ready"))
        phase = sem("phase_ready")
        var_ready, std_ready = sem("var_ready"), sem("std_ready")
        xn_step, xn_ready, aT_raw, aT_ready = sem("xn_step"), sem("xn_ready"), sem("aT_raw"), sem("aT_ready")
        q_done, k_done, v_done = sem("q_done"), sem("k_done"), sem("v_done")
        qb_ready, kc_ready, kx_ready, vb_ready = sem("qb_ready"), sem("kc_ready"), sem("kx_ready"), sem("vb_ready")
        s_done, mx_ready, less_max, probs_ready = sem("scores_done"), sem("max_ready"), sem("less_max"), sem("probs_ready")
        turned, turned_ready = sem("probsT_done"), sem("probsT_ready")
        sT_done, tanh_done, pv_done = sem("scoresT_done"), sem("tanh_done"), sem("pv_done")
        rec_ready, o_ready, oT_done, oT_ready = sem("rec_ready"), sem("o_ready"), sem("oT_done"), sem("oT_ready")
        y_done, y_used = sem("y_done"), sem("y_used")
        ln_step, ln_gain, ln_ready, squares_done = sem("ln_step"), sem("ln_gain"), sem("ln_ready"), sem("squares_done")
        o_seen, xT_seen, sim_seen = sem("o_seen"), sem("xT_seen"), sem("sim_seen")
        e_done, vT_done, e_ready, vT_ready, v_raw, v_ready = (
            sem("e_done"), sem("vT_done"), sem("e_ready"), sem("vT_ready"), sem("v_raw"), sem("v_ready"))
        xs_done, xmx_ready, nmx_ready, p_ready, pT_raw, pT_ready, xo_done, rden_ready = (
            sem("xscores_done"), sem("xmax_ready"), sem("xnegmax_ready"), sem("xprobs_ready"), sem("xprobsT_raw"),
            sem("xprobsT_ready"), sem("xout_done"), sem("rden_ready"))
        bn_done = sem("bn_done")
        xb_ready, sim_done, v8_ready, d_ready, ex_ready = (
            sem("xb_ready"), sem("sim_done"), sem("v8_ready"), sem("d_ready"), sem("ex_ready"))
        t8_ready, z_ready, rz_ready, dg_ready = (
            sem("t8_ready"), sem("z_ready"), sem("rz_ready"), sem("dg_ready"))
        ee_ready, ww_ready, g_part = sem("ee_ready"), sem("ww_ready"), sem("g_part")
        h_done, h_ready, hg_ready, m_done = sem("h_done"), sem("h_ready"), sem("hg_ready"), sem("m_done")
        y_used_x, y_used_m = sem("xout_used"), sem("memory_used")
        lg_done, lg_ready, l8_ready, nl_ready, le_ready, lw_step, lw_ready = (
            sem("lg_done"), sem("lg_ready"), sem("l8_ready"), sem("nl_ready"), sem("le_ready"), sem("lw_step"), sem("lw_ready"))
        up_done, hT_ready, down_done, acc_done = sem("up_done"), sem("hT_ready"), sem("down_done"), sem("acc_done")

        PHASE = dict(attn0=1, norm0=2, out0=3, cross0=4, bn=5, memory=6, attn1=7, cross1=8, experts=9)
        NORM = dict(attn0=0, out0=NT, cross0=2 * NT, bn=3 * NT, attn1=4 * NT, cross1=5 * NT, experts=6 * NT)
        ATTN = dict(attn0=0, attn1=NT, cross1=2 * NT)
        OUTT = dict(attn1=0, cross1=NT)
        PROJ = dict(out0=0, attn1=NT, cross1=2 * NT)
        XSCALE = float(P) ** -0.5
        HSCALE = float(DH) ** -0.5
        N_LOADS = 25

        block = es.enter_context(nc.Block())

        @block.sync
        def _(sp):
            loads = [
                (cst[:, :], consts), (row[:, :], rows), (col[:, :], cols), (w8[:, 0:SETS * P], wq0), (w8[:, SETS * P:3 * SETS * P], wk0),
                (small[:, WV0, :], wv0), (small[:, WO0, :], wo0), (small[:, XWV, :], xWvT), (small[:, WV1, :], wv1),
                (small[:, WO1, :], wo1), (small[:, WOUT, :], wout), (raw[:, RWQ, :], xWq), (raw[:, RWK, :], xWk),
                (raw[:, RWE1, :], xWeT[0:P, :]), (raw[:, RWE2, :], xWeT[P:2 * P, :]),
                (rqk, wqk.rearrange("(n p) d -> p n d", p=P)), (rkey, keysT.rearrange("n p k -> p n k")), (rt[:, :], router),
                (mask4[:, :], mask), (sc[:, 0:2], scal),
                (wq1_s[:, :, :].rearrange("p g c -> p (g c)"), wq1), (wk1_s[:, :, :, :].rearrange("p b g c -> p (b g c)"), wk1),
                (selq_s[:, :, :, :].rearrange("p b g c -> p (b g c)"), selq), (selk_s[:, :, :].rearrange("p g c -> p (g c)"), selk),
                (xs[:, :, :], x.rearrange("(t p) d -> p t d", p=P)),
            ]
            assert len(loads) == N_LOADS
            for dst, src in loads:
                sp.dma_start(dst, src).then_inc(loaded, 16)
            sp.dma_start(cT[:, :], ctxT).then_inc(loaded, 16)
            sp.wait_ge(phase, PHASE["norm0"])
            sp.dma_start(kin, key_inT).then_inc(tables, 16)
            sp.dma_start(kout, key_out.rearrange("(c p) d -> p c d", p=P)).then_inc(tables, 16)
            sp.wait_ge(phase, PHASE["attn1"])
            sp.dma_start(up_w, up.rearrange("e p h -> p e h")).then_inc(experts_in, 16)
            sp.dma_start(down_w, down.rearrange("e (c p) d -> p e c d", p=P)).then_inc(experts_in, 16)
            sp.wait_ge(phase, PHASE["cross1"])
            ctx_v = ctx.rearrange("(t p) d -> t p d", p=P)

            def ctx_load(T):
                need(sp, vb_ready, T.before(2, ATTN["cross1"]))
                sp.dma_start(ctile[:, T.u, :], ctx_v[T.t]).then_inc(ctx_in[T.u], 16)
            staggered(nc, sp, NT, [(0, ctx_load)])
            ov = out.rearrange("(t p) d -> p t d", p=P)
            parts = 4
            for n in range(parts):
                a, b = n * NT // parts, (n + 1) * NT // parts
                sp.wait_ge(acc_done, MOE * b)
                sp.dma_start(ov[:, a:b, :], xs[:, a:b, :]).then_inc(stored, 16)
            sp.wait_ge(stored, 16 * parts)

        @block.gpsimd
        def _(pool):
            pool.memset(ones[:, :], 1.0).then_inc(ones_ready, 1)

            own_head = C("own_head").unsqueeze(1).unsqueeze(3).to_broadcast([P, SETS, PER_SET, SEQ])

            def spread(base):
                def seg(T):
                    u = T.u
                    pool.wait_ge(kc_ready, T.now(base))
                    need(pool, sT_done if base == ATTN["cross1"] else s_done, T.before(2, 0 if base == ATTN["cross1"] else base))
                    pool.tensor_tensor(KX[:, u].rearrange("p g (h k) -> p g h k", h=PER_SET),
                                       KC[:, u].unsqueeze(2).to_broadcast([P, SETS, PER_SET, SEQ]), own_head, ALU.mult)\
                        .then_inc(kx_ready, 1)
                return seg

            pool.wait_ge(phase, PHASE["attn0"])
            staggered(nc, pool, NT, [(0, spread(ATTN["attn0"]))])

            pool.wait_ge(phase, PHASE["memory"])

            def outer(T):
                pool.wait_ge(ex_ready, T.now())
                for h in range(PH):
                    a, b = NKEY * h, NKEY * (PH + h)
                    need(pool, ww_ready, T.step(PH, h - 1))
                    pool.tensor_tensor(EE[:, h % 2, :].rearrange("p (i j) -> p i j", i=NKEY),
                                       EX[:, T.u, a:a + NKEY].unsqueeze(2).to_broadcast([P, NKEY, NKEY]),
                                       EX[:, T.u, b:b + NKEY].unsqueeze(1).to_broadcast([P, NKEY, NKEY]),
                                       ALU.mult).then_inc(ee_ready, 1)
            staggered(nc, pool, NT, [(0, outer)])

            pool.wait_ge(phase, PHASE["attn1"])
            staggered(nc, pool, NT, [(0, spread(ATTN["attn1"]))])
            pool.wait_ge(phase, PHASE["cross1"])
            staggered(nc, pool, NT, [(0, spread(ATTN["cross1"]))])

        @block.scalar
        def _(act):
            act.wait_ge(loaded, 16 * (N_LOADS + 1))
            act.activation(sc[:, 2:3], sc[:, 1:2], ACT.Exp).then_inc(bound_ready, 1)
            act.wait_ge(folds_done, 1)
            act.activation(small[:, A1, :], bank(0, 0), ACT.Copy)
            act.activation(small[:, A2, :], bank(0, P), ACT.Copy)
            act.activation(Mk[:, :], ps[:, 1, :], ACT.Copy).then_inc(folds_ready, 1)

            def deviations(n, width=NT):
                act.wait_ge(var_ready, n)
                act.activation(t64[:, 1, 0:width], t64[:, 0, 0:width], ACT.Sqrt).then_inc(std_ready, 1)

            def copy_aT(base, projected, projected_base):
                def seg(T):
                    act.wait_ge(aT_raw, T.now(base))
                    need(act, projected, T.before(2, projected_base))
                    act.activation(aT[:, T.u, :], psA, ACT.Copy).then_inc(aT_ready, 1)
                return seg

            def copy_aT_experts(T):
                act.wait_ge(aT_raw, T.now(NORM["experts"]))
                need(act, up_done, T.step(MOE, -MOE))
                act.activation(aT[:, T.u, :], psXA, ACT.Copy).then_inc(aT_ready, 1)

            def exps(base):
                def seg(T):
                    act.wait_ge(less_max, T.now(base))
                    act.activation(PQ[:, T.u, :], PQ[:, T.u, :], ACT.Exp).then_inc(probs_ready, 1)
                return seg

            def copy_probsT(base, half):
                def seg(T):
                    act.wait_ge(turned, T.step(2, half + 1, base))
                    if half == 0:
                        need(act, pv_done, T.before(2, base))
                    act.activation(PT[:, T.u, half * 512:half * 512 + 512], psPT[:, half, :], ACT.Copy).then_inc(turned_ready, 1)
                return seg

            def copy_k(base, done):
                def seg(T):
                    act.wait_ge(done, T.now(base))
                    need(act, kx_ready, T.before(2, base))
                    if base == ATTN["cross1"]:
                        act.activation(KC[:, T.u], psKc, ACT.Copy).then_inc(kc_ready, 1)
                        return
                    for g in range(SETS):
                        ins = act.activation(KC[:, T.u, g, :], psKc[:, g, :], ACT.Identity, bias=bk_s[:, g:g + 1])
                    ins.then_inc(kc_ready, 1)
                return seg

            def copy_q(base):
                def seg(T):
                    act.wait_ge(q_done, T.now(base))
                    need(act, s_done, T.before(2, base))
                    for g in range(SETS):
                        for b in range(2):
                            part = slice(SEQ * b, SEQ * b + SEQ)
                            ins = act.activation(QB[:, T.u, g, part], psQ[:, g, part], ACT.Identity, bias=bq_own[:, g, b:b + 1],
                                                 scale=K("own")[:, b:b + 1])
                    ins.then_inc(qb_ready, 1)
                return seg

            def copy_oT(base):
                def seg(T):
                    act.wait_ge(oT_done, T.now(base))
                    need(act, y_done, T.before(2, base))
                    act.activation(OT[:, T.u, :], psOT, ACT.Copy).then_inc(oT_ready, 1)
                return seg

            deviations(1)
            deviations(2)
            act.wait_ge(phase, PHASE["attn0"])

            b0 = ATTN["attn0"]
            staggered(nc, act, NT, [(1, copy_aT(NORM["attn0"], v_done, b0)), (3, copy_probsT(b0, 0)), (1, copy_k(b0, k_done)),
                                    (3, copy_probsT(b0, 1)), (1, copy_q(b0)), (2, exps(b0))])

            deviations(3)

            def squares(T):
                act.wait_ge(ln_ready, T.now())
                need(act, squares_done, T.before(2))
                act.activation(ytmp[:, T.u, :], o_all[:, T.t, :], ACT.Square, accum_out=tile_col(t64[:, 2, :], T))\
                    .then_inc(squares_done, 1)
            staggered(nc, act, NT, [(0, squares)])
            deviations(4)

            OTb = OT[:, :, :].bitcast(BF16)

            def copy_ints(T):
                act.wait_ge(aT_raw, T.now(NORM["out0"]))
                need(act, y_done, T.before(2, PROJ["out0"]))
                act.activation(OTb[:, T.u, 0:P], psA, ACT.Copy).then_inc(aT_ready, 1)
            staggered(nc, act, NT, [(0, copy_ints)])

            deviations(5)
            act.wait_ge(phase, PHASE["cross0"])

            def entangle(T):
                u = T.u
                act.wait_ge(e_done, T.now())
                need(act, xs_done, T.before(2))
                act.activation(ent[:, u, :], psE, ACT.Tanh, bias=sc[:, 12:13]).then_inc(e_ready, 1)
                act.wait_ge(vT_done, T.now())
                need(act, v_raw, T.before(2))
                act.activation(VT[:, u, :], psVT, ACT.Identity, bias=K("xbv")).then_inc(vT_ready, 1)

            def x_exps(T):
                u = T.u
                act.wait_ge(nmx_ready, T.now())
                need(act, pT_raw, T.before(2))
                need(act, rden_ready, T.before(2))
                for b in range(2):
                    part = slice(SEQ * b, SEQ * b + SEQ)
                    ins = act.activation(PB[part, u, part], psSx[part, :], ACT.Exp, bias=xden[part, u, 1:2], scale=XSCALE,
                                         accum_out=xden[part, u, 2:3])
                ins.then_inc(p_ready, 1)

            def copy_pT(T):
                act.wait_ge(pT_raw, T.now())
                need(act, xo_done, T.before(2))
                act.activation(PBT[:, T.u, :], psXT, ACT.Copy).then_inc(pT_ready, 1)
            staggered(nc, act, NT, [(0, copy_aT(NORM["cross0"], e_done, 0)), (2, copy_pT), (1, x_exps), (0, entangle)])

            deviations(6)

            def keep_xT(T):
                act.wait_ge(aT_raw, T.now(NORM["bn"]))
                act.activation(xTt[:, T.t, :], psA, ACT.Copy).then_inc(aT_ready, 1)
            staggered(nc, act, NT, [(0, keep_xT)])
            deviations(7, 1)

            act.wait_ge(phase, PHASE["memory"])

            def normed(T):
                need(act, sim_done, T.before(2))
                act.activation(xb[:, T.u, :], xTt[:, T.t, :], ACT.Identity, scale=sc[:, 13:14], bias=sc[:, 14:15])\
                    .then_inc(xb_ready, 1)

            def key_exps(T):
                act.wait_ge(d_ready, T.now())
                act.activation(EX[:, T.u, :], EX[:, T.u, :], ACT.Exp).then_inc(ex_ready, 1)

            def diagonals(T):
                act.wait_ge(rz_ready, T.now())
                need(act, g_part, T.step(PH, -PH))
                for h in range(PH):
                    ins = act.activation(DG[:, T.u, h, :], ident, ACT.Copy, scale=RZ[:, T.u, h:h + 1])
                ins.then_inc(dg_ready, 1)

            def hidden(T):
                act.wait_ge(h_done, T.now())
                need(act, hg_ready, T.before(1))
                act.activation(HT, psH, ACT.Gelu).then_inc(h_ready, 1)
            staggered(nc, act, NT, [(0, normed), (1, hidden), (0, key_exps), (0, diagonals)])

            deviations(8)
            act.wait_ge(phase, PHASE["attn1"])
            b1 = ATTN["attn1"]
            staggered(nc, act, NT, [(1, copy_aT(NORM["attn1"], v_done, b1)), (3, copy_probsT(b1, 0)), (4, copy_oT(OUTT["attn1"])),
                                    (1, copy_k(b1, k_done)), (3, copy_probsT(b1, 1)), (1, copy_q(b1)), (2, exps(b1))])

            deviations(9)
            act.wait_ge(phase, PHASE["cross1"])

            b2 = ATTN["cross1"]

            def tanhs(T):
                act.wait_ge(sT_done, T.now())
                need(act, pv_done, T.before(2, b2))
                act.activation(PT[:, T.u, :], psST[T.u], ACT.Tanh, scale=sc[:, 3:4]).then_inc(tanh_done, 1)

            def bounded_exps(T):
                act.wait_ge(tanh_done, T.now())
                act.activation(PT[:, T.u, :], PT[:, T.u, :], ACT.Exp, scale=sc[:, 2:3], bias=tile_col(mbias[:, :], T))\
                    .then_inc(probs_ready, 1)
            staggered(nc, act, NT, [(2, tanhs), (1, copy_aT(NORM["cross1"], q_done, b2)), (1, copy_k(b2, q_done)),
                                    (2, bounded_exps), (4, copy_oT(OUTT["cross1"]))])

            deviations(10)
            act.wait_ge(phase, PHASE["experts"])

            def gelus(T):
                for e in range(MOE):
                    act.wait_ge(up_done, T.step(MOE, e + 1))
                    need(act, down_done, T.step(MOE, e + 1 - RING))
                    act.activation(hT[:, e % RING], psU[:, e % RING], ACT.Gelu_apprx_tanh).then_inc(hT_ready, 1)

            def router_exps(T):
                act.wait_ge(nl_ready, T.now())
                act.activation(le[:, T.u, :], lg[:, T.u, :], ACT.Exp, bias=ls[:, T.u, 0:1]).then_inc(le_ready, 1)
            staggered(nc, act, NT, [(0, copy_aT_experts), (1, gelus), (0, router_exps)])

        @block.tensor
        def _(pe):
            pe.wait_ge(loaded, 16 * (N_LOADS + 1))
            pe.wait_ge(ones_ready, 1)
            pe.wait_ge(quantised, 1)
            pe.matmul(bank(3, 0, 4), ones[:, :], sc[:, 4:8], start=True, stop=True).then_inc(sums_done, 1)
            pe.matmul(bank(0, 0), raw[:, RWQ, :], raw[:, RWE1, :], start=True, stop=True)
            pe.matmul(bank(0, P), raw[:, RWK, :], raw[:, RWE2, :], start=True, stop=True)
            pe.matmul(bank(4, 0, 1), raw[:, RWE1, :], K("xbq"), start=True, stop=False)
            pe.matmul(bank(4, 0, 1), raw[:, RWE2, :], K("xbk"), start=False, stop=True)
            for n in range(2 * PH):
                ins = pe.matmul(bank(1, n * NKEY, NKEY), rqk[:, n, :], rkey[:, n, :], start=True, stop=True)
            ins.then_inc(folds_done, 1)

            def transposed(base, dst=psA):
                def seg(T):
                    pe.wait_ge(xn_ready, T.now(base))
                    need(pe, aT_ready, T.before(1, base))
                    pe.transpose(dst, xn[:, T.u, :], ident).then_inc(aT_raw, 1)
                return seg

            def transposed_beside_q(base, nbase):
                def seg(T):
                    pe.wait_ge(xn_ready, T.now(nbase))
                    need(pe, qb_ready, T.before(1, base))
                    pe.transpose(psA, xn[:, T.u, :], ident).then_inc(aT_raw, 1)
                return seg

            def project_k(base, nbase, w):
                def seg(T):
                    pe.wait_ge(aT_ready, T.now(nbase))
                    need(pe, kc_ready, T.before(1, base))
                    for g in range(SETS):
                        for b in range(2):
                            ins = pe.matmul(psKc[:, g, :], w[:, b, g, :], aT[:, T.u, SEQ * b:SEQ * b + SEQ], start=b == 0, stop=b == 1)
                    ins.then_inc(k_done, 1)
                return seg

            def project_q(base, w, obase):
                def seg(T):
                    if obase is not None:
                        need(pe, oT_ready, T.before(3, obase))
                    for g in range(SETS):
                        ins = pe.matmul(psQ[:, g, :], w[:, g, :], aT[:, T.u, :], start=True, stop=True)
                    ins.then_inc(q_done, 1)
                return seg

            def project_v(base, w, ybase):
                def seg(T):
                    need(pe, vb_ready, T.before(1, base))
                    if ybase is not None:
                        need(pe, y_used, T.before(3, ybase))
                    for b in range(2):
                        for h in range(2):
                            ins = pe.matmul(psV[SEQ * h:SEQ * h + SEQ, SEQ * b:SEQ * b + SEQ], aT[:, T.u, SEQ * b:SEQ * b + SEQ],
                                            w[:, SEQ * h:SEQ * h + SEQ], start=True, stop=True)
                    ins.then_inc(v_done, 1)
                return seg

            def scores(base, causal):
                def seg(T):
                    u = T.u
                    pe.wait_ge(qb_ready, T.now(base))
                    pe.wait_ge(kx_ready, T.now(base))
                    need(pe, less_max, T.before(1, base))
                    for g in range(SETS):
                        if causal:
                            pe.matmul(ps[:, g, :], maskq_b[0:MASK_ROWS, :], maskk_b[0:MASK_ROWS, g, :], start=True, stop=False)
                        ins = pe.matmul(ps[:, g, :], QB[:, u, g, :], KX[:, u, g, :], start=not causal, stop=True)
                    ins.then_inc(s_done, 1)
                return seg

            def scoresT(base):
                def seg(T):
                    u = T.u
                    pe.wait_ge(qb_ready, T.now(base))
                    pe.wait_ge(kx_ready, T.now(base))
                    need(pe, tanh_done, T.before(2))
                    for g in range(SETS):
                        ins = pe.matmul(psST[u][:, g, :], QB[:, u, g, :], KX[:, u, g, :], start=True, stop=True)
                    ins.then_inc(sT_done, 1)
                return seg

            def probsT(base, half):
                def seg(T):
                    if half == 0:
                        pe.wait_ge(probs_ready, T.now(base))
                    need(pe, turned_ready, T.step(2, half - 1, base))
                    for n in range(PAIRS // 2):
                        i = half * (PAIRS // 2) + n
                        ins = pe.transpose(psPT[:, half, n * P:n * P + P], PQ[:, T.u, i * P:i * P + P], ident)
                    ins.then_inc(turned, 1)
                return seg

            def values_of_pairs(base):
                def seg(T):
                    u = T.u
                    pe.wait_ge(vb_ready, T.now(base))
                    need(pe, o_ready, T.before(1, base))
                    for i in range(PAIRS):
                        if i % (PAIRS // 2) == 0:
                            pe.wait_ge(turned_ready, T.step(2, i // (PAIRS // 2) + 1, base))
                        for b in range(2):
                            part = slice(SEQ * b, SEQ * b + SEQ)
                            a = i * P + SEQ * b
                            ins = pe.matmul(psOq[part, 2 * i:2 * i + 2, :].rearrange("p h d -> p (h d)"), PT[:, u, a:a + SEQ],
                                            VBp[:, u, b, i].rearrange("p h d -> p (h d)"), start=True, stop=True)
                    ins.then_inc(pv_done, 1)
                return seg

            def values_of_heads(base):
                def seg(T):
                    u = T.u
                    pe.wait_ge(probs_ready, T.now(base))
                    pe.wait_ge(vb_ready, T.now(base))
                    need(pe, o_ready, T.before(1, base))
                    for h in range(HEADS):
                        ins = pe.matmul(psOh[:, h].rearrange("p b d -> p (b d)"), PT[:, u, h * SEQ:h * SEQ + SEQ],
                                        VBh[:, u, h].rearrange("p b d -> p (b d)"), start=True, stop=True)
                    ins.then_inc(pv_done, 1)
                return seg

            def outputT(base, nbase):
                def seg(T):
                    pe.wait_ge(o_ready, T.now(base))
                    pe.wait_ge(aT_ready, T.ahead(3, nbase, NT))
                    if base == ATTN["cross1"]:
                        for b in range(2):
                            ins = pe.matmul(psOT[:, SEQ * b:SEQ * b + SEQ], O[0:SEQ, T.u, b], ident[0:SEQ, 0:SEQ], start=True, stop=True)
                    else:
                        ins = pe.transpose(psOT, O[:, T.u, 0], ident)
                    ins.then_inc(oT_done, 1)
                return seg

            def out_project(ready, rbase, base, src, w, shared=None):
                def seg(T):
                    pe.wait_ge(ready, T.now(rbase))
                    need(pe, y_used, T.before(1, base))
                    if shared is not None:
                        sem, n, sbase = shared
                        pe.wait_ge(sem, T.ahead(n, sbase, NT))
                    pe.matmul(psY, src(T.u), w, start=True, stop=True).then_inc(y_done, 1)
                return seg

            b0 = ATTN["attn0"]
            pe.wait_ge(phase, PHASE["attn0"])
            n0 = NORM["attn0"]
            staggered(nc, pe, NT, [(2, scores(b0, False)), (2, project_v(b0, small[:, WV0, :], None)), (1, transposed_beside_q(b0, n0)),
                                   (3, probsT(b0, 0)), (1, project_k(b0, n0, wk0_s)), (3, probsT(b0, 1)),
                                   (1, project_q(b0, wq0_s, None)), (3, values_of_pairs(b0))])
            pe.wait_ge(phase, PHASE["out0"])
            OTb = OT[:, :, :].bitcast(BF16)
            staggered(nc, pe, NT, [(0, transposed(NORM["out0"])),
                                   (1, out_project(aT_ready, NORM["out0"], PROJ["out0"], lambda u: OTb[:, u, 0:P], wo0_b[:, :]))])

            pe.wait_ge(phase, PHASE["cross0"])

            def entangled(T):
                u = T.u
                pe.wait_ge(aT_ready, T.now(NORM["cross0"]))
                need(pe, e_ready, T.before(1))
                pe.matmul(psE, small[:, A2, :], cTt[:, T.t, :], start=True, stop=False)
                pe.matmul(psE, small[:, A1, :], aT[:, u, :], start=False, stop=True).then_inc(e_done, 1)
                need(pe, vT_ready, T.before(1))
                pe.matmul(psVT, small[:, XWV, :], cTt[:, T.t, :], start=True, stop=True).then_inc(vT_done, 1)

            def x_scores(T):
                u = T.u
                pe.wait_ge(e_ready, T.now())
                pe.wait_ge(vT_ready, T.now())
                need(pe, p_ready, T.before(1))
                for b in range(2):
                    part = slice(SEQ * b, SEQ * b + SEQ)
                    ins = pe.matmul(psSx[part, :], ent[:, u, part], VT[:, u, part], start=True, stop=True)
                ins.then_inc(xs_done, 1)
                need(pe, v_ready, T.before(1))
                pe.transpose(psVx, VT[:, u, :], ident).then_inc(v_raw, 1)

            def x_probsT(T):
                pe.wait_ge(p_ready, T.now())
                need(pe, pT_ready, T.before(1))
                pe.transpose(psXT, PB[:, T.u, :], ident).then_inc(pT_raw, 1)

            def x_values(T):
                pe.wait_ge(pT_ready, T.now())
                pe.wait_ge(v_ready, T.now())
                need(pe, y_used_x, T.before(1))
                pe.matmul(psXO, PBT[:, T.u, :], Vt[:, T.u, :], start=True, stop=True).then_inc(xo_done, 1)
            staggered(nc, pe, NT, [(1, x_scores), (0, transposed(NORM["cross0"])), (2, x_probsT), (0, entangled), (2, x_values)])

            pe.wait_ge(phase, PHASE["bn"])
            staggered(nc, pe, NT, [(0, transposed(NORM["bn"]))])

            pe.wait_ge(phase, PHASE["memory"])
            pe.wait_ge(tables, 32)

            def key_scores(T):
                pe.wait_ge(xb_ready, T.now())
                need(pe, d_ready, T.before(1))
                pe.matmul(ps[:, 0, :], xb[:, T.u, :], Mk[:, :], start=True, stop=True).then_inc(sim_done, 1)

            def hidden(T):
                need(pe, h_ready, T.before(1))
                for c in range(CHUNKS):
                    ins = pe.matmul(psH[:, c, :], kin[:, c * P:c * P + P], xTt[:, T.t, :], start=True, stop=True)
                ins.then_inc(h_done, 1)

            def gates(first, last):
                def seg(T):
                    for h in range(first, last):
                        pe.wait_ge(ww_ready, T.step(PH, h + 1))
                        if h == 0:
                            pe.wait_ge(dg_ready, T.now())
                            need(pe, hg_ready, T.before(2))
                        for c in range(CHUNKS):
                            ins = pe.matmul(psG[T.u][:, c, :], WW[:, h % 2, c * P:c * P + P], DG[:, T.u, h, :],
                                            start=h == 0 and c % 4 == 0, stop=h == PH - 1, skip_group_check=True)
                        ins.then_inc(g_part, 1)
                return seg

            def mixed(T):
                pe.wait_ge(hg_ready, T.now())
                need(pe, y_used_m, T.before(1))
                for c in range(CHUNKS):
                    ins = pe.matmul(psM, HG[:, c, :], kout[:, c, :], start=c == 0, stop=c == CHUNKS - 1)
                ins.then_inc(m_done, 1)
            staggered(nc, pe, NT, [(0, key_scores), (1, hidden), (1, gates(0, 4)), (2, mixed), (1, gates(4, PH))])

            b1 = ATTN["attn1"]
            pe.wait_ge(phase, PHASE["attn1"])
            n1 = NORM["attn1"]
            staggered(nc, pe, NT, [
                (2, scores(b1, True)), (2, project_v(b1, small[:, WV1, :], PROJ["attn1"])), (1, transposed_beside_q(b1, n1)),
                (3, probsT(b1, 0)), (4, outputT(b1, n1)), (1, project_k(b1, n1, wk1_s)), (3, probsT(b1, 1)),
                (1, project_q(b1, wq1_s, OUTT["attn1"])), (3, values_of_pairs(b1)),
                (4, out_project(oT_ready, OUTT["attn1"], PROJ["attn1"], lambda u: OT[:, u, :], small[:, WO1, :],
                                (vb_ready, 2, b1)))])

            b2 = ATTN["cross1"]
            pe.wait_ge(phase, PHASE["cross1"])
            n2 = NORM["cross1"]

            def transposed_beside_o(T):
                pe.wait_ge(xn_ready, T.now(n2))
                need(pe, aT_ready, T.before(1, n2))
                need(pe, oT_ready, T.before(4, OUTT["cross1"]))
                pe.transpose(psA, xn[:, T.u, :], ident).then_inc(aT_raw, 1)

            def place_heads(T):
                need(pe, qb_ready, T.before(1, b2))
                need(pe, y_used, T.before(4, PROJ["cross1"]))
                for g in range(SETS):
                    ins = pe.matmul(psKd[:, g, :], selk_s[:, g, :], cTt[:, T.t, :], start=True, stop=True)
                ins.then_inc(k_done, 1)
                pe.wait_ge(aT_ready, T.now(n2))
                need(pe, kc_ready, T.before(1, b2))
                for g in range(SETS):
                    for b in range(2):
                        ins = pe.matmul(psKc[:, g, :], selq_s[:, b, g, :], aT[:, T.u, SEQ * b:SEQ * b + SEQ], start=b == 0, stop=b == 1)
                ins.then_inc(q_done, 1)
            staggered(nc, pe, NT, [
                (2, scoresT(b2)), (1, transposed_beside_o), (3, values_of_heads(b2)), (4, outputT(b2, n2)), (1, place_heads),
                (4, out_project(oT_ready, OUTT["cross1"], PROJ["cross1"], lambda u: OT[:, u, :], small[:, WOUT, :],
                                (qb_ready, 3, b2)))])

            pe.wait_ge(phase, PHASE["experts"])
            pe.wait_ge(experts_in, 32)

            def route(T):
                pe.wait_ge(aT_ready, T.now(NORM["experts"]))
                need(pe, lg_ready, T.before(1))
                pe.matmul(psR, aT[:, T.u, :], rt[:, :], start=True, stop=True).then_inc(lg_done, 1)

            def up_project(T, e):
                if e == 0:
                    pe.wait_ge(aT_ready, T.now(NORM["experts"]))
                need(pe, hT_ready, T.step(MOE, e + 1 - RING))
                for c in range(HC):
                    ins = pe.matmul(psU[:, e % RING, c, :], up_w[:, e, c * P:c * P + P], aT[:, T.u, :], start=True, stop=True)
                ins.then_inc(up_done, 1)

            def down_project(T, e):
                pe.wait_ge(hT_ready, T.step(MOE, e + 1))
                need(pe, acc_done, T.step(MOE, e - 1))
                for c in range(HC):
                    ins = pe.matmul(psD[e % 2], hT[:, e % RING, c, :], down_w[:, e, c, :], start=c == 0, stop=c == HC - 1)
                ins.then_inc(down_done, 1)

            def experts_a(T):
                up_project(T, 0)
                up_project(T, 1)
                for e in range(MOE // 2):
                    up_project(T, e + 2)
                    down_project(T, e)

            def experts_b(T):
                for e in range(MOE // 2, MOE):
                    if e + 2 < MOE:
                        up_project(T, e + 2)
                    down_project(T, e)
            staggered(nc, pe, NT, [(0, transposed(NORM["experts"], dst=psXA)), (1, experts_a), (0, route), (1, experts_b)])

        @block.vector
        def _(dve):
            seen = [0]

            def rsqrt(dst, src, width=NT):
                seen[0] += 1
                dve.tensor_scalar(t64[:, 0, 0:width], src, EPS, None, ALU.add).then_inc(var_ready, 1)
                dve.wait_ge(std_ready, seen[0])
                dve.reciprocal(dst, t64[:, 1, 0:width])
                dve.drain()

            dve.wait_ge(loaded, 16 * (N_LOADS + 1))
            quant = ((w8[:, 0:SETS * P], 2 * P * P), (w8[:, SETS * P:3 * SETS * P], 4 * SEQ * P), (small[:, WV0, :], 2 * SEQ * P),
                     (small[:, WO0, :], P * P))
            for n, (w, count) in enumerate(quant):
                dve.tensor_reduce(sc[:, 4 + n:5 + n], w, X, ALU.add, apply_absolute_value=True)
                dve.drain()
            dve.sem_inc(quantised, 1)
            dve.wait_ge(sums_done, 1)
            for n, (w, count) in enumerate(quant):
                dve.tensor_scalar(sc[:, 16 + n:17 + n], bank(3, n, 1), 1.0 / count, 1e-5, ALU.mult, ALU.max)
            dve.drain()
            dve.reciprocal(sc[:, 20:24], sc[:, 16:20])
            dve.tensor_scalar(sc[:, 24:25], sc[:, 16:17], HSCALE, None, ALU.mult)
            dve.drain()
            for n, (w, count) in enumerate(quant):
                dve.tensor_scalar(w, w, sc[:, 20 + n:21 + n], MAGIC, ALU.mult, ALU.add)
                dve.drain()
                dve.tensor_scalar(w, w, -MAGIC, 1.0, ALU.add, ALU.min)
                dve.drain()
                if n < 3:
                    dve.tensor_scalar(w, w, -1.0, sc[:, 24:25] if n == 0 else sc[:, 16 + n:17 + n], ALU.max, ALU.mult)
                else:
                    dve.tensor_scalar(wo0_b[:, :], w, -1.0, None, ALU.max)
            dve.tensor_scalar(wq1_s[:, :, :], wq1_s[:, :, :], HSCALE, None, ALU.mult)
            for name in ("bq0", "bq1"):
                dve.tensor_scalar(K(name), K(name), HSCALE, None, ALU.mult)
            dve.tensor_copy(maskq_b[:, :], C("mask_q"))
            dve.tensor_copy(maskk_b[:, :, :].rearrange("p g c -> p (g c)"), C("mask_k"))
            dve.wait_ge(folds_done, 1)
            dve.tensor_tensor(sc[:, 12:13], bank(4, 0, 1), K("xbe"), ALU.add)
            dve.tensor_scalar(sc[:, 3:4], sc[:, 0:1], HSCALE, None, ALU.mult)
            dve.tensor_copy(mbias[:, :], mask4[:, :].bitcast(U8))
            dve.wait_ge(bound_ready, 1)
            dve.drain()
            dve.tensor_scalar(mbias[:, :], mbias[:, :], NEG, sc[:, 2:3], ALU.mult, ALU.subtract)
            dve.wait_ge(folds_ready, 1)

            def blank_values(name):
                for u in range(2):
                    dve.tensor_copy(VB[:, u, :], C(name))

            def bias_columns(bq, bk):
                for b in range(2):
                    dve.tensor_scalar(bq_own[:, :, b], K(bq), K("own")[:, b:b + 1], None, ALU.mult)
                dve.tensor_copy(bk_s[:, :], K(bk))

            dve.drain()
            blank_values("vones_pairs")
            bias_columns("bq0", "bk0")

            def row_moments():
                dve.drain()
                even, odd = st_all[:, :, 1], st_all[:, :, 4]
                dve.tensor_tensor(mv[:, 0, :], even, odd, ALU.add)
                dve.tensor_tensor(t64[:, 0, :], even, odd, ALU.subtract)
                dve.tensor_tensor(mv[:, 1, :], st_all[:, :, 2], st_all[:, :, 5], ALU.add)
                dve.drain()
                dve.tensor_scalar(mv[:, 0, :], mv[:, 0, :], 0.5, None, ALU.mult)
                dve.scalar_tensor_tensor(out=t64[:, 0, :], in0=t64[:, 0, :], scalar=0.25, in1=t64[:, 0, :], op0=ALU.mult, op1=ALU.mult)
                dve.drain()
                dve.scalar_tensor_tensor(out=mv[:, 1, :], in0=mv[:, 1, :], scalar=1.0 / P, in1=t64[:, 0, :], op0=ALU.mult, op1=ALU.add)
                dve.drain()

            def input_stats(T):
                dve.bn_stats(st_all[:, T.t, :], xs[:, T.t, :])
                dve.tensor_reduce(tile_col(t64[:, 3, :], T), xs[:, T.t, :], X, ALU.max)
                dve.tensor_reduce(tile_col(t64[:, 4, :], T), xs[:, T.t, :], X, ALU.min)
            staggered(nc, dve, NT, [(0, input_stats)])
            row_moments()
            mean, var = mv[:, 0, :], mv[:, 1, :]
            rsqrt(rs[:, :], var)
            dve.tensor_tensor(t64[:, 5, :], rs[:, :], rs[:, :], ALU.mult)
            dve.tensor_tensor(t64[:, 3, :], t64[:, 3, :], mean, ALU.subtract)
            dve.tensor_tensor(t64[:, 4, :], mean, t64[:, 4, :], ALU.subtract)
            dve.drain()
            dve.tensor_tensor(t64[:, 5, :], t64[:, 5, :], var, ALU.mult)
            dve.tensor_tensor(t64[:, 3, :], t64[:, 3, :], t64[:, 4, :], ALU.max)
            dve.drain()
            rsqrt(t64[:, 6, :], t64[:, 5, :])
            dve.tensor_tensor(rs[:, :], rs[:, :], t64[:, 6, :], ALU.mult)
            dve.drain()

            def quant_factors(largest, factor, back=None):
                dve.tensor_tensor(t64[:, 7, :], largest, factor, ALU.mult)
                dve.drain()
                dve.tensor_scalar(t64[:, 7, :], t64[:, 7, :], 1e-5, 1.0 / 127.0, ALU.max, ALU.mult)
                dve.drain()
                dve.reciprocal(t64[:, 4, :], t64[:, 7, :])
                if back is None:
                    dve.tensor_copy(s_in[:, 1, :], t64[:, 7, :])
                else:
                    dve.tensor_scalar(s_in[:, 1, :], t64[:, 7, :], back, None, ALU.mult)
                dve.drain()
                dve.tensor_tensor(s_in[:, 0, :], t64[:, 4, :], factor, ALU.mult)
                dve.drain()
            quant_factors(t64[:, 3, :], rs[:, :])
            dve.sem_inc(phase, 1)

            def quantised_rows(T):
                u = T.u
                need(dve, aT_raw, T.before(2, NORM["attn0"]))
                dve.tensor_scalar(xn[:, u, :], xs[:, T.t, :], tile_col(mv[:, 0, :], T), tile_col(s_in[:, 0, :], T), ALU.subtract, ALU.mult)\
                    .then_inc(xn_step, 1)
                dve.wait_ge(xn_step, T.step(2, 1))
                dve.tensor_scalar(xn[:, u, :], xn[:, u, :], MAGIC, -MAGIC, ALU.add, ALU.add).then_inc(xn_step, 1)
                dve.wait_ge(xn_step, T.step(2, 2))
                dve.tensor_scalar(xn[:, u, :], xn[:, u, :], tile_col(s_in[:, 1, :], T), None, ALU.mult).then_inc(xn_ready, 1)

            def normed_rows(base):
                def seg(T):
                    need(dve, aT_raw, T.before(2, base))
                    dve.tensor_scalar(xn[:, T.u, :], xs[:, T.t, :], tile_col(mv[:, 0, :], T), tile_col(rs[:, :], T), ALU.subtract, ALU.mult)\
                        .then_inc(xn_ready, 1)
                return seg

            def place_v(base, bv):
                def seg(T):
                    dve.wait_ge(v_done, T.now(base))
                    need(dve, pv_done, T.before(2, base))
                    for h in range(2):
                        part = slice(SEQ * h, SEQ * h + SEQ)
                        ins = dve.tensor_tensor(VBp[part, T.u, :, :, h, 0:DH], psV[part, :].rearrange("p (b i d) -> p b i d", b=2, i=PAIRS),
                                                bv[part, :].rearrange("p (b i d) -> p b i d", b=2, i=PAIRS), ALU.add)
                    ins.then_inc(vb_ready, 1)
                return seg

            def maxima(base):
                def seg(T):
                    u = T.u
                    dve.wait_ge(s_done, T.now(base))
                    dve.tensor_reduce(mx[:, u, :], psS, X, ALU.max).then_inc(mx_ready, 1)
                    dve.wait_ge(mx_ready, T.now(base))
                    need(dve, turned, T.step(2, -2, base))
                    dve.tensor_tensor(PQ[:, u, :].rearrange("p (h k) -> p h k", h=HEADS), psS,
                                      mx[:, u, :].unsqueeze(2).to_broadcast([P, HEADS, SEQ]), ALU.subtract).then_inc(less_max, 1)
                return seg

            def normalised(base, obase):
                def seg(T):
                    u = T.u
                    dve.wait_ge(pv_done, T.now(base))
                    dve.reciprocal(rec[:, u, 0:HEADS], psOq[:, :, DH]).then_inc(rec_ready, 1)
                    dve.wait_ge(rec_ready, T.now(base))
                    if obase is not None:
                        need(dve, oT_done, T.before(2, obase))
                    to = o_all[:, T.t, :] if obase is None else O[:, u, 0]
                    dve.tensor_tensor(to.rearrange("p (h d) -> p h d", h=HEADS), psOq[:, :, 0:DH],
                                      rec[:, u, 0:HEADS].unsqueeze(2).to_broadcast([P, HEADS, DH]), ALU.mult).then_inc(o_ready, 1)
                return seg

            def stats_of_new(T):
                dve.drain()
                dve.bn_stats(st_all[:, T.t, :], xs[:, T.t, :])

            def add_output(name, bias, scale=None):
                base = PROJ[name]

                def seg(T):
                    u = T.u
                    dve.wait_ge(y_done, T.now(base))
                    if bias is None:
                        dve.tensor_tensor(xs[:, T.t, :], psY, xs[:, T.t, :], ALU.add).then_inc(y_used, 1)
                        stats_of_new(T)
                        return
                    if scale is None:
                        dve.tensor_tensor(ytmp[:, u, :], psY, bias, ALU.add).then_inc(y_used, 1)
                    else:
                        dve.scalar_tensor_tensor(out=ytmp[:, u, :], in0=psY, scalar=tile_col(scale[:, :], T), in1=bias, op0=ALU.mult,
                                                 op1=ALU.add).then_inc(y_used, 1)
                    dve.wait_ge(y_used, T.now(base))
                    dve.tensor_tensor(xs[:, T.t, :], xs[:, T.t, :], ytmp[:, u, :], ALU.add)
                    stats_of_new(T)
                return seg

            def output_stats(T):
                dve.wait_ge(o_ready, T.now())
                dve.sem_inc(o_seen, 1)
                dve.bn_stats(st_all[:, T.t, :], o_all[:, T.t, :])
            b0 = ATTN["attn0"]
            staggered(nc, dve, NT, [(4, normalised(b0, None)), (2, maxima(b0)), (4, output_stats), (2, place_v(b0, R("bv0"))),
                                    (0, quantised_rows)])
            row_moments()
            rsqrt(rs[:, :], var)
            dve.sem_inc(phase, 1)

            def output_norm(T):
                o = o_all[:, T.t, :]
                dve.tensor_scalar(o, o, tile_col(mv[:, 0, :], T), tile_col(rs[:, :], T), ALU.subtract, ALU.mult).then_inc(ln_step, 1)

            def output_gain(T):
                o = o_all[:, T.t, :]
                dve.wait_ge(ln_step, T.now())
                dve.tensor_tensor(o, o, R("g0"), ALU.mult).then_inc(ln_gain, 1)

            def output_shift(T):
                o = o_all[:, T.t, :]
                dve.wait_ge(ln_gain, T.now())
                dve.tensor_tensor(o, o, R("b0"), ALU.add).then_inc(ln_ready, 1)

            def output_max(T):
                dve.wait_ge(ln_ready, T.now())
                dve.tensor_reduce(tile_col(t64[:, 3, :], T), o_all[:, T.t, :], X, ALU.max, apply_absolute_value=True)
            staggered(nc, dve, NT, [(0, output_norm), (1, output_gain), (2, output_shift), (3, output_max)])
            dve.wait_ge(squares_done, NT)
            dve.drain()
            dve.tensor_scalar(t64[:, 5, :], t64[:, 2, :], 1.0 / P, None, ALU.mult)
            dve.drain()
            rsqrt(t64[:, 6, :], t64[:, 5, :])
            quant_factors(t64[:, 3, :], t64[:, 6, :], sc[:, 19:20])
            dve.sem_inc(phase, 1)

            def quantised_output(T):
                u = T.u
                need(dve, aT_raw, T.before(2, NORM["out0"]))
                dve.tensor_scalar(xn[:, u, :], o_all[:, T.t, :], tile_col(s_in[:, 0, :], T), MAGIC, ALU.mult, ALU.add).then_inc(xn_step, 1)
                dve.wait_ge(xn_step, T.step(1, 2 * NT + 1))
                dve.tensor_scalar(xn[:, u, :], xn[:, u, :], -MAGIC, None, ALU.add).then_inc(xn_ready, 1)
            staggered(nc, dve, NT, [(0, quantised_output), (2, add_output("out0", R("bo0"), s_in[:, 1, :]))])

            row_moments()
            rsqrt(rs[:, :], var)
            dve.memset(PB[:, :, :], 0.0)
            dve.drain()
            dve.sem_inc(phase, 1)

            def x_maxima(T):
                u = T.u
                dve.wait_ge(xs_done, T.now())
                need(dve, p_ready, T.before(2))
                dve.tensor_reduce(xden[:, u, 0:1], psSx, X, ALU.max).then_inc(xmx_ready, 1)
                dve.wait_ge(xmx_ready, T.now())
                dve.tensor_scalar(xden[:, u, 1:2], xden[:, u, 0:1], -XSCALE, None, ALU.mult).then_inc(nmx_ready, 1)
                dve.wait_ge(v_raw, T.now())
                need(dve, xo_done, T.before(2))
                dve.tensor_copy(Vt[:, u, :], psVx).then_inc(v_ready, 1)

            def add_cross(T):
                u = T.u
                dve.wait_ge(p_ready, T.now())
                dve.reciprocal(xden[:, u, 3:4], xden[:, u, 2:3]).then_inc(rden_ready, 1)
                dve.wait_ge(rden_ready, T.now())
                dve.wait_ge(xo_done, T.now())
                dve.scalar_tensor_tensor(out=xs[:, T.t, :], in0=psXO, scalar=xden[:, u, 3:4], in1=xs[:, T.t, :], op0=ALU.mult,
                                         op1=ALU.add).then_inc(y_used_x, 1)
                stats_of_new(T)
            staggered(nc, dve, NT, [(0, normed_rows(NORM["cross0"])), (1, x_maxima), (2, add_cross)])

            row_moments()
            rsqrt(rs[:, :], var)
            dve.sem_inc(phase, 1)

            def feature_stats(T):
                dve.wait_ge(aT_ready, T.now(NORM["bn"]))
                dve.sem_inc(xT_seen, 1)
                dve.bn_stats(bnst[:, T.t, :], xTt[:, T.t, :]).then_inc(bn_done, 1)
            staggered(nc, dve, NT, [(0, normed_rows(NORM["bn"])), (1, feature_stats)])
            dve.wait_ge(bn_done, NT)
            dve.bn_aggr(sc[:, 26:28], bnst[:, :, :].rearrange("p t s -> p (t s)"))
            dve.drain()
            rsqrt(sc[:, 28:29], sc[:, 27:28], 1)
            dve.tensor_tensor(sc[:, 13:14], sc[:, 28:29], K("gamma"), ALU.mult)
            dve.drain()
            dve.tensor_tensor(sc[:, 29:30], sc[:, 26:27], sc[:, 13:14], ALU.mult)
            dve.drain()
            dve.tensor_tensor(sc[:, 14:15], K("beta"), sc[:, 29:30], ALU.subtract)
            dve.wait_ge(aT_ready, NORM["bn"] + NT)
            dve.drain()
            dve.sem_inc(phase, 1)

            def top_keys(T):
                u = T.u
                dve.wait_ge(sim_done, T.now())
                dve.sem_inc(sim_seen, 1)
                sim = ps[:, 0, :].rearrange("p (n k) -> p n k", k=NKEY)
                for n in range(2 * PH):
                    ins = dve.max(V8[:, u, n, :], sim[:, n, :])
                ins.then_inc(v8_ready, 1)
                dve.wait_ge(v8_ready, T.now())
                need(dve, ee_ready, T.step(PH, -PH))
                dve.tensor_tensor(EX[:, u, NS:].rearrange("p (n k) -> p n k", k=TOPK), V8[:, u],
                                  V8[:, u, :, 0:1].to_broadcast([P, 2 * PH, TOPK]), ALU.subtract)
                dve.tensor_tensor(EX[:, u, 0:NS].rearrange("p (n k) -> p n k", k=NKEY), sim,
                                  V8[:, u, :, 0:1].to_broadcast([P, 2 * PH, NKEY]), ALU.subtract).then_inc(d_ready, 1)

            def top_pairs(T):
                u = T.u
                dve.wait_ge(ex_ready, T.now())
                best = EX[:, u, NS:].rearrange("p (n k) -> p n k", k=TOPK)
                dve.tensor_tensor(CD.rearrange("p h (i j) -> p h i j", i=TOPK),
                                  best[:, 0:PH].unsqueeze(3).to_broadcast([P, PH, TOPK, TOPK]),
                                  best[:, PH:].unsqueeze(2).to_broadcast([P, PH, TOPK, TOPK]), ALU.mult)
                dve.drain()
                for h in range(PH):
                    ins = dve.max(T8[:, u, h, :], CD[:, h, :])
                ins.then_inc(t8_ready, 1)
                dve.wait_ge(t8_ready, T.now())
                dve.tensor_reduce(Z[:, u, :], T8[:, u], X, ALU.add).then_inc(z_ready, 1)
                dve.wait_ge(z_ready, T.now())
                need(dve, dg_ready, T.before(2))
                dve.reciprocal(RZ[:, u, :], Z[:, u, :]).then_inc(rz_ready, 1)

            def chosen(first, last):
                def seg(T):
                    for h in range(first, last):
                        if h == 0:
                            dve.wait_ge(t8_ready, T.now())
                        dve.wait_ge(ee_ready, T.step(PH, h + 1))
                        need(dve, g_part, T.step(PH, h - 1))
                        dve.scalar_tensor_tensor(out=WW[:, h % 2, :], in0=EE[:, h % 2, :], scalar=T8[:, T.u, h, TOPK - 1:TOPK],
                                                 in1=EE[:, h % 2, :], op0=ALU.is_ge, op1=ALU.mult).then_inc(ww_ready, 1)
                return seg

            def gated(T):
                dve.wait_ge(h_ready, T.now())
                dve.wait_ge(g_part, T.step(PH, PH))
                need(dve, m_done, T.before(1))
                dve.tensor_tensor(HG, psG[T.u], HT, ALU.mult).then_inc(hg_ready, 1)

            def add_memory(T):
                dve.wait_ge(m_done, T.now())
                dve.tensor_tensor(xs[:, T.t, :], psM, xs[:, T.t, :], ALU.add).then_inc(y_used_m, 1)
                stats_of_new(T)
            staggered(nc, dve, NT, [(2, gated), (1, chosen(0, 2)), (0, top_keys), (1, chosen(2, 5)), (2, add_memory), (0, top_pairs),
                                    (1, chosen(5, PH))])

            row_moments()
            rsqrt(rs[:, :], var)
            blank_values("vones_pairs")
            bias_columns("bq1", "bk1")
            dve.drain()
            dve.sem_inc(phase, 1)
            b1 = ATTN["attn1"]
            staggered(nc, dve, NT, [(4, normalised(b1, OUTT["attn1"])), (5, add_output("attn1", R("bo1"))), (2, maxima(b1)),
                                    (2, place_v(b1, R("bv1"))), (0, normed_rows(NORM["attn1"]))])

            row_moments()
            rsqrt(rs[:, :], var)
            blank_values("vones_heads")
            dve.drain()
            dve.sem_inc(phase, 1)
            b2 = ATTN["cross1"]

            def ctx_values(T):
                u = T.u
                dve.wait_ge(ctx_in[u], T.pair * 16 + 16)
                need(dve, pv_done, T.before(2, b2))
                for b in range(2):
                    part = slice(SEQ * b, SEQ * b + SEQ)
                    ins = dve.tensor_copy(VBh[part, u, :, b, 0:DH], ctile[part, u, :].rearrange("p (h d) -> p h d", h=HEADS))
                ins.then_inc(vb_ready, 1)

            def place_heads(T):
                u = T.u
                dve.wait_ge(k_done, T.now(b2))
                need(dve, sT_done, T.before(2))
                dve.tensor_tensor(QB[:, u], psKd, C("own_entry").unsqueeze(1).to_broadcast([P, SETS, P]), ALU.mult)\
                    .then_inc(qb_ready, 1)

            def normalised_heads(T):
                u = T.u
                dve.wait_ge(pv_done, T.now(b2))
                r = rec[0:SEQ, u, :].rearrange("p (h b) -> p h b", h=HEADS)
                dve.reciprocal(r, psOh[:, :, :, DH]).then_inc(rec_ready, 1)
                dve.wait_ge(rec_ready, T.now(b2))
                need(dve, oT_done, T.before(2, OUTT["cross1"]))
                dve.tensor_tensor(O[0:SEQ, u].rearrange("p b (h d) -> p h b d", h=HEADS), psOh[:, :, :, 0:DH],
                                  r.unsqueeze(3).to_broadcast([SEQ, HEADS, 2, DH]), ALU.mult).then_inc(o_ready, 1)
            staggered(nc, dve, NT, [(4, normalised_heads), (5, add_output("cross1", None)), (2, ctx_values),
                                    (0, normed_rows(NORM["cross1"])), (1, place_heads)])

            row_moments()
            rsqrt(rs[:, :], var)
            dve.sem_inc(phase, 1)

            def logits(T):
                u = T.u
                dve.wait_ge(lg_done, T.now())
                need(dve, le_ready, T.before(2))
                dve.tensor_copy(lg[:, u, :], psR).then_inc(lg_ready, 1)
                dve.drain()
                dve.max(l8[:, u, :], lg[:, u, :]).then_inc(l8_ready, 1)
                dve.wait_ge(l8_ready, T.now())
                dve.tensor_scalar(ls[:, u, 0:1], l8[:, u, 0:1], -1.0, None, ALU.mult).then_inc(nl_ready, 1)

            def route_weights(T):
                u = T.u
                dve.wait_ge(le_ready, T.now())
                dve.scalar_tensor_tensor(out=lw[:, u, :], in0=lg[:, u, :], scalar=l8[:, u, MOE_K - 1:MOE_K], in1=le[:, u, :],
                                         op0=ALU.is_ge, op1=ALU.mult).then_inc(lw_step, 1)
                dve.wait_ge(lw_step, T.step(3, 1))
                dve.tensor_reduce(ls[:, u, 1:2], lw[:, u, :], X, ALU.add).then_inc(lw_step, 1)
                dve.wait_ge(lw_step, T.step(3, 2))
                dve.reciprocal(ls[:, u, 2:3], ls[:, u, 1:2]).then_inc(lw_step, 1)
                dve.wait_ge(lw_step, T.step(3, 3))
                dve.tensor_scalar(lw[:, u, :], lw[:, u, :], ls[:, u, 2:3], None, ALU.mult).then_inc(lw_ready, 1)

            def add_experts(first, last):
                def seg(T):
                    for e in range(first, last):
                        if e == 0:
                            dve.wait_ge(lw_ready, T.now())
                        else:
                            dve.wait_ge(acc_done, T.step(MOE, e))
                        dve.wait_ge(down_done, T.step(MOE, e + 1))
                        dve.scalar_tensor_tensor(out=xs[:, T.t, :], in0=psD[e % 2], scalar=lw[:, T.u, e:e + 1],
                                                 in1=xs[:, T.t, :], op0=ALU.mult, op1=ALU.add).then_inc(acc_done, 1)
                return seg
            staggered(nc, dve, NT, [(0, normed_rows(NORM["experts"])), (1, add_experts(0, 4)), (0, logits), (1, add_experts(4, MOE)),
                                    (0, route_weights)])


def slotted(w, entries):
    heads = w.reshape(-1, DH, P)
    heads = np.repeat(heads, HEADS // len(heads), axis=0)
    rows = heads.reshape(SETS, PER_SET, DH, P).transpose(3, 0, 1, 2)
    out = np.zeros((P, entries, SETS, PER_SET, 2, DH), np.float32)
    for b in range(2):
        out[:, b % entries, :, :, b] = rows
    return out.reshape(P, -1)


def slotted_bias(b):
    heads = b.reshape(-1, DH)
    heads = np.repeat(heads, HEADS // len(heads), axis=0).reshape(SETS, PER_SET, DH)
    out = np.broadcast_to(heads[:, :, None], (SETS, PER_SET, 2, DH))
    return out.reshape(SETS, P).T


def by_parity(w):
    return w.reshape(*w.shape[:-1], PAIRS, 2, DH).swapaxes(-3, -2).reshape(w.shape)


def parity_rows(v):
    v = by_parity(v).reshape(2, 1, 1, SEQ)
    return np.broadcast_to(v, (2, SEQ, 2, SEQ)).reshape(P, P)


def bf16_parts(a):
    out = []
    for _ in range(PARTS):
        part = (a.view(np.uint32) & np.uint32(0xFFFF0000)).view(np.float32)
        out.append(part)
        a = a - part
    return np.stack(out)


def constants():
    c = np.zeros((P, CONSTS), np.float32)

    def put(name, a):
        at, n = CONST[name]
        c[:a.shape[0], at:at + n] = a.reshape(a.shape[0], n)

    tok = np.arange(P)
    half, pos = tok // SEQ, tok % SEQ
    put("ident", np.eye(P))
    put("own_entry", (tok[:, None] // DH % 2 == half[None, :]).astype(np.float32))
    put("own_head", (tok[:, None] // ROWS2 == np.arange(PER_SET)[None, :]).astype(np.float32))
    start = 2.0 ** (-8.0 / HEADS)
    slopes = np.array([start * start ** i for i in range(HEADS)], np.float32)[:, None]
    keys = np.arange(SEQ, dtype=np.float32)
    late = np.where(keys[None, :] > keys[:, None], np.float32(NEG), np.float32(0))
    put("mask_q", np.concatenate([keys[:, None] == pos, np.ones((PARTS, P)), np.broadcast_to(pos, (PARTS, P))]))
    put("mask_k", np.concatenate([np.tile(late, (1, HEADS)), bf16_parts((slopes * keys).reshape(-1)),
                                  bf16_parts(np.repeat(-slopes, SEQ, axis=1).reshape(-1))]))
    v = np.zeros((P, 2, PAIRS, 2, DH + 1), np.float32)
    w = np.zeros((P, HEADS, 2, DH + 1), np.float32)
    for n in range(2):
        v[SEQ * n:SEQ * n + SEQ, :, :, n, DH] = 1.0
        w[SEQ * n:SEQ * n + SEQ, :, n, DH] = 1.0
    put("vones_pairs", v)
    put("vones_heads", w)
    return c


def layout(i):
    f = lambda name: np.asarray(i[name])
    D = P
    tokens = f("x").shape[0] * SEQ
    x = f("x").reshape(tokens, D)
    ctx = f("ctx_1024").reshape(tokens, D)
    repeat = lambda w: np.repeat(w.reshape(-1, DH, *w.shape[1:]), 2, axis=0).reshape(D, *w.shape[1:])
    row = lambda v: np.broadcast_to(v[None], (D, D))
    rows = (parity_rows(repeat(f("L0_attn_bv"))), row(f("L0_attn_bo")), row(f("L0_attn_ln_g")), row(f("L0_attn_ln_b")),
            parity_rows(f("L1_attn_v_b")), row(f("L1_attn_o_b")))
    cols = [f(n)[:, None] for n in ("L0_xattn_bq", "L0_xattn_bk", "L0_xattn_bv", "L0_xattn_be", "L0_ffn_gamma", "L0_ffn_beta")]
    entry = np.arange(P) // DH % 2
    cols += [(entry[:, None] == np.arange(2)[None, :]).astype(np.float32)]
    cols += [slotted_bias(f(n)) for n in ("L0_attn_bq", "L0_attn_bk", "L1_attn_q_b", "L1_attn_k_b")]
    a = dict(
        x=x, ctxT=ctx.T, ctx=ctx, mask=np.ascontiguousarray(f("mask_Bx1xS2_bk0").reshape(-1, D).T).view(np.uint32), consts=constants(),
        rows=np.concatenate(rows, axis=1), cols=np.concatenate(cols, axis=1),
        wq0=slotted(f("L0_attn_wq"), 1), wk0=slotted(f("L0_attn_wk"), 2), wv0=by_parity(repeat(f("L0_attn_wv")).T), wo0=f("L0_attn_wo").T,
        xWq=f("L0_xattn_Wq"), xWk=f("L0_xattn_Wk"), xWvT=f("L0_xattn_Wv").T, xWeT=f("L0_xattn_We").T,
        wqk=f("L0_ffn_w_q"), keysT=f("L0_ffn_keys").transpose(2, 0, 3, 1).reshape(2 * PH, D, NKEY),
        key_inT=f("L0_ffn_key_in").T, key_out=f("L0_ffn_key_out"),
        wq1=slotted(f("L1_attn_q_w"), 1), wk1=slotted(f("L1_attn_k_w"), 2), wv1=by_parity(f("L1_attn_v_w").T), wo1=f("L1_attn_o_w").T,
        selq=slotted(np.eye(D, dtype=np.float32), 2), selk=slotted(np.eye(D, dtype=np.float32), 1), wout=f("L1_xattn_W_out").T,
        scal=np.broadcast_to(np.stack([f("L1_xattn_scale"), f("L1_xattn_log_C")])[None], (D, 2)),
        router=f("L1_ffn_router_w"), up=f("L1_ffn_up_w"), down=f("L1_ffn_down_w"))
    return {k: np.ascontiguousarray(v) for k, v in a.items()}


def kernel(**inputs):
    import concourse.bacc as bacc
    from concourse.bass_utils import run_bass_kernel_spmd as run

    nc = bacc.Bacc("TRN2", target_bir_lowering=False, num_devices=1)
    arrays = {f"in_{k}": v for k, v in layout(inputs).items()}
    args = [nc.dram_tensor(k, v.shape, mybir.dt.from_np(v.dtype), kind="ExternalInput").ap() for k, v in arrays.items()]
    out = nc.dram_tensor("out", arrays["in_x"].shape, F32, kind="ExternalOutput").ap()
    build(nc, *args, out)
    r = run(nc, [arrays], core_ids=[0])
    return r.results[0]["out"].reshape(np.asarray(inputs["x"]).shape)
```

```python
from contextlib import ExitStack

import numpy as np

import concourse.bass as bass
from concourse import mybir

P = 128
SEQ = 64
HEADS = 16
DH = P // HEADS
PAIRS = HEADS // 2
SETS = 2
PER_SET = HEADS // SETS
PARTS = 3
MASK_ROWS = SEQ + 2 * PARTS
EPS = 1e-5
MAGIC = 1.5 * 2.0 ** 23
NEG = -1e30
NKEY = 32
GATES = 7
HRING = 4
PH = 8
TOPK = 8
NEXP = NKEY * NKEY
CHUNKS = NEXP // P
GROUP = 4
MOE = 8
MOE_K = 4
HID = 512

F32 = mybir.dt.float32
BF16 = mybir.dt.bfloat16
U8 = mybir.dt.uint8
U32 = mybir.dt.uint32
F32R = mybir.dt.float32r
ALU = mybir.AluOpType
ACT = mybir.ActivationFunctionType
X = mybir.AxisListType.X

CONST = {}
_at = 0
for _name, _n in (("ident", P), ("own_head", PER_SET), ("mask_q", P), ("mask_k", HEADS * SEQ),
                  ("vones_pairs", PAIRS * 4 * (DH + 1)), ("vones_heads", HEADS * 2 * (DH + 1)), ("pick", MOE)):
    CONST[_name] = (_at, _n)
    _at += _n
CONSTS = _at
ROWS = ("bv0", "bo0", "g0", "b0", "bv1", "bo1")
COLS = {"xbq": (0, 1), "xbk": (1, 1), "xbv": (2, 1), "xbe": (3, 1), "gamma": (4, 1), "beta": (5, 1), "bq0": (6, SETS),
        "bk0": (6 + SETS, SETS), "bq1": (6 + 2 * SETS, SETS), "bk1": (6 + 3 * SETS, SETS)}
NCOLS = 6 + 4 * SETS


class Tile:

    def __init__(self, t, u, pair):
        self.t, self.u, self.pair = t, u, pair

    def now(self, base=0):
        return self.t + (base + 1)

    def before(self, n, base=0):
        return self.t + (base + 1 - n)

    def ahead(self, n, base, tiles):
        if isinstance(self.t, int):
            return min(self.t + n, tiles - 1) + base + 1
        return self.t + (base + 1 + n)

    def step(self, per_tile, k, base=0):
        return self.t * per_tile + (base * per_tile + k)


def need(eng, sem, value):
    if isinstance(value, int) and value <= 0:
        return
    eng.wait_ge(sem, value)


def tile_col(block, T):
    return block.rearrange("p (t o) -> p t o", o=1)[:, T.t, :]


def staggered(nc, eng, tiles, segments):
    lag = max(l for l, _ in segments)
    peel = lag + 2 + lag % 2
    for s in range(peel):
        for l, seg in segments:
            if s >= l:
                seg(Tile(s - l, (s - l) % 2, (s - l) // 2))
    with nc.Fori(peel // 2, tiles // 2, engines=[eng.engine]) as i:
        for u in range(2):
            for l, seg in segments:
                seg(Tile(2 * i + (u - l), (u - l) % 2, i + (u - l) // 2))
    for s in range(tiles, tiles + lag):
        for l, seg in segments:
            if s - l < tiles:
                seg(Tile(s - l, (s - l) % 2, (s - l) // 2))


def build(nc, x, ctxT, ctx, mask, consts, rows, cols, wq0, wk0, wv0, wo0, xWq, xWk, xWvT, xWeT, wqk, keysT, key_inT,
          key_out, wq1, wk1, wv1, wo1, wout, scal, router, up, down, out):
    NT = x.shape[0] // P
    NG = NT // GROUP
    with ExitStack() as es:
        def sb(name, shape, dt=F32):
            return es.enter_context(nc.sbuf_tensor(name, shape, dt))

        def sem(name):
            return es.enter_context(nc.semaphore(name))

        xs = sb("x_all", [P, NT, P])
        cT = sb("ctxT_all", [P, NT * P])
        cst = sb("consts_sb", [P, CONSTS])
        row = sb("rows_sb", [P, len(ROWS) * P])
        col = sb("cols_sb", [P, NCOLS])
        wq1_s = sb("wq1_sb", [P, P])
        wk1_s = sb("wk1_sb", [P, P])
        small = sb("small_w", [P, 8, P])
        WV0, WO0, A1, A2, XWV, WV1, WO1, WOUT = range(8)
        wo0_b = sb("wo0_bf", [P, P], BF16)
        rt = sb("router_sb", [P, MOE])
        Mk = sb("Mk", [P, 2 * PH * NKEY])
        bq_s = sb("bq", [P, SETS])
        bk_s = sb("bk", [P, SETS])
        maskq_b = sb("mask_q_bf", [P, P], BF16)
        maskk_b = sb("mask_k_bf", [P, 2, HEADS * SEQ // 2], BF16)
        mv = sb("mv", [P, 2, NT])
        st_all = sb("st_all", [P, NT, 6])
        rs = sb("rstd", [P, NT])
        t64 = sb("t64", [P, 8, NT])
        sc = sb("scalars", [P, 32])
        mask4 = sb("mask4", [P, NT // 4], U32)
        mbias = sb("mbias", [P, NT])
        ones = sb("ones", [P, P])
        s_in = sb("quant_scale", [P, 2, NT])
        bnst = sb("bn_stats_all", [P, NG, 6])

        def C(name):
            a, n = CONST[name]
            return cst[:, a:a + n]

        def R(name):
            a = ROWS.index(name) * P
            return row[:, a:a + P]

        def K(name):
            a, n = COLS[name]
            return col[:, a:a + n]

        ident = C("ident")

        WORK = 14848
        work_space = ExitStack()
        w8 = work_space.enter_context(nc.sbuf_tensor("w8", [P, 2 * NEXP], F32))
        big = work_space.enter_context(nc.sbuf_tensor("big", [P, 2 * MOE * HID], F32))
        work = work_space.enter_context(nc.sbuf_tensor("work", [P, WORK], F32))
        o_all = big[:, 0:NT * P].rearrange("p (t d) -> p t d", d=P)
        xT_all = big[:, 0:NT * P]
        up_w = big[:, 0:MOE * HID].rearrange("p (e h) -> p e h", e=MOE)
        down_w = big[:, MOE * HID:2 * MOE * HID].rearrange("p (e c d) -> p e c d", e=MOE, c=HID // P)
        wq0_s, wk0_s = w8[:, 0:P], w8[:, P:2 * P]
        kin = w8[:, 0:NEXP]
        kout = w8[:, 1024:2048].rearrange("p (c d) -> p c d", c=CHUNKS)
        top = [0]

        def carve(n):
            a = top[0]
            top[0] += n
            assert top[0] <= WORK, top[0]
            return work[:, a:a + n]

        xn = carve(2 * P).rearrange("p (u d) -> p u d", u=2)
        aT = carve(2 * P).rearrange("p (u d) -> p u d", u=2)
        QB = carve(2 * SETS * P).rearrange("p (u g c) -> p u g c", u=2, g=SETS)
        KC = carve(2 * SETS * SEQ).rearrange("p (u g k) -> p u g k", u=2, g=SETS)
        KX = carve(2 * HEADS * SEQ).rearrange("p (u g n) -> p u g n", u=2, g=SETS)
        VB = carve(2 * PAIRS * 4 * (DH + 1)).rearrange("p (u n) -> p u n", u=2)
        VBp = VB.rearrange("p u (b i h d) -> p u b i h d", b=2, i=PAIRS, h=2)
        VBh = VB.rearrange("p u (h b d) -> p u h b d", h=HEADS, b=2)
        PQ = carve(2 * HEADS * SEQ).rearrange("p (u n) -> p u n", u=2)
        PT = carve(2 * HEADS * SEQ).rearrange("p (u n) -> p u n", u=2)
        O = carve(2 * 2 * P).rearrange("p (u b d) -> p u b d", u=2, b=2)
        OT = carve(2 * P).rearrange("p (u d) -> p u d", u=2)
        mx = carve(2 * HEADS).rearrange("p (u h) -> p u h", u=2)
        rec = carve(2 * HEADS * 2).rearrange("p (u n) -> p u n", u=2)
        ctile = carve(2 * P).rearrange("p (u d) -> p u d", u=2)
        ytmp = carve(2 * P).rearrange("p (u d) -> p u d", u=2)
        top[0] = 0
        raw = carve(4 * P).rearrange("p (n d) -> p n d", n=4)
        RWQ, RWK, RWE1, RWE2 = range(4)
        rqk = carve(2 * PH * P).rearrange("p (n d) -> p n d", n=2 * PH)
        rkey = carve(2 * PH * NKEY).rearrange("p (n d) -> p n d", n=2 * PH)
        def by_group(block):
            return block.rearrange("p (g t) d -> p g t d", t=GROUP)

        def group_buffer(u=2):
            return carve(u * GROUP * P).rearrange("p (u t d) -> p u t d", u=u, t=GROUP)

        def group_cols(block):
            return block.rearrange("p (g t) -> p g t", t=GROUP)

        top[0] = 0
        xng, aTg = group_buffer(), group_buffer()
        after_aTg = top[0]
        ints = carve(GROUP * P).bitcast(BF16).rearrange("p (u t d) -> p u t d", u=2, t=GROUP)
        yg = group_buffer()
        ent, VT, Vt, PB, PBT = group_buffer(), group_buffer(), group_buffer(), group_buffer(), group_buffer()
        SX = carve(2 * GROUP * SEQ).rearrange("p (u t k) -> p u t k", u=2, t=GROUP)
        xden = carve(3 * 2 * GROUP).rearrange("p (n u t) -> p n u t", n=3, u=2)
        top[0] = 0
        NS = 2 * PH * NKEY
        xb = carve(2 * P).rearrange("p (u d) -> p u d", u=2)
        EX = carve(2 * (NS + 2 * PH * TOPK)).rearrange("p (u n) -> p u n", u=2)
        V8 = carve(2 * 2 * PH * TOPK).rearrange("p (u n k) -> p u n k", u=2, k=TOPK)
        CD = carve(PH * TOPK * TOPK).rearrange("p (h n) -> p h n", h=PH)
        T8 = carve(2 * PH * TOPK).rearrange("p (u h k) -> p u h k", u=2, k=TOPK)
        Z = carve(2 * PH).rearrange("p (u h) -> p u h", u=2)
        RZ = carve(2 * PH).rearrange("p (u h) -> p u h", u=2)
        RT = carve(2).rearrange("p (u o) -> p u o", u=2)
        DG = carve(2 * PH * P).rearrange("p (u h d) -> p u h d", u=2, h=PH)
        EE = carve(HRING * NEXP).rearrange("p (u n) -> p u n", u=HRING)
        WW = carve(HRING * NEXP).rearrange("p (u n) -> p u n", u=HRING)
        HT = carve(NEXP).rearrange("p (c d) -> p c d", c=CHUNKS)
        HG = carve(NEXP).rearrange("p (c d) -> p c d", c=CHUNKS)
        HC = HID // P
        DUO = 2
        RING = 2
        top[0] = after_aTg
        lg_at = top[0]
        lg = carve(NT * MOE).rearrange("p (t e) -> p t e", e=MOE)
        l8 = carve(NT * MOE).rearrange("p (t e) -> p t e", e=MOE)
        le = carve(NT * MOE).rearrange("p (t e) -> p t e", e=MOE)
        lw = carve(NT * MOE).rearrange("p (t e) -> p t e", e=MOE)
        l8_of = carve(2 * GROUP * MOE).rearrange("p (u t e) -> p u t e", u=2, t=GROUP)
        lz = carve(2 * NT).rearrange("p (n t) -> p n t", n=2)
        gates_at = work[:, lg_at:lg_at + NT * 2 * MOE].rearrange("p (t n) -> p t n", n=2 * MOE)
        acc = le.rearrange("p t e -> p (t e)").rearrange("p (u n) -> p u n", u=2)
        hid = [C("mask_k").rearrange("p (c d) -> p c d", c=HC), small[:, :, :].rearrange("p (c t) d -> p c (t d)", t=DUO)]
        lg_end = top[0]
        work_space.close()
        h_up = sb("h_up", [P, RING, HC, DUO * P], F32R)
        w_low, d_low = sb("w_low", [P, MOE, HID], F32R), sb("d_low", [P, MOE, HC, P], F32R)
        h_low = sb("h_low", [P, RING, HC, DUO * P], F32R)
        assert RING * HC * DUO * P == after_aTg
        sb("routing_work", [P, lg_end - after_aTg])
        a_up, a_low = sb("a_up", [P, 2, DUO * P], F32R), sb("a_low", [P, 2, DUO * P], F32R)
        w_up, d_up = sb("w_up", [P, MOE, HID], F32R), sb("d_up", [P, MOE, HC, P], F32R)
        lw_up = sb("lw_up", [P, NT, MOE], F32R)
        gT = sb("gates_turned", [P, 2, DUO * P], F32R)
        prod = sb("weighted", [P, DUO * P])
        pick = sb("pick_expert", [P, MOE], F32R)
        assert lg_end + 4 * DUO * P + 2 * MOE * HID + NT * MOE + 3 * DUO * P + MOE <= WORK

        ps = es.enter_context(nc.psum_tensor("ps", [P, 8, 512], F32))

        def bank(b, a, n=P):
            return ps[:, b, a:a + n]

        psS = ps[:, 0:2, :].rearrange("p b (n k) -> p (b n) k", k=SEQ)
        psPT = ps[:, 2:4, :]
        psST = ps[:, 0:2, :]
        psA, psOT = bank(4, 0), bank(4, P)
        psQ = bank(4, 2 * P, SETS * SEQ).rearrange("p (g c) -> p g c", g=SETS)
        psKc = bank(5, 0, SETS * SEQ).rearrange("p (g c) -> p g c", g=SETS)
        psKd = bank(2, 0, SETS * SEQ).rearrange("p (g c) -> p g c", g=SETS)
        psV, psY = bank(6, 0), bank(6, P)
        psOq = bank(7, 0, HEADS * (DH + 1)).rearrange("p (h d) -> p h d", h=HEADS)
        psOh = ps[0:SEQ, 7, 0:HEADS * 2 * (DH + 1)].rearrange("p (h b d) -> p h b d", h=HEADS, b=2)
        def group_bank(b, n=P):
            return ps[:, b, 0:GROUP * n].rearrange("p (t d) -> p t d", t=GROUP)

        psE, psVT, psSx, psVx, psAx, psXT, psXO = (group_bank(0), group_bank(1), group_bank(2, SEQ), group_bank(3), group_bank(4),
                                                   group_bank(5), group_bank(6))
        psAg, psYg = [group_bank(4), group_bank(5)], [group_bank(6), group_bank(7)]
        psRg = [group_bank(6, MOE), group_bank(7, MOE)]
        psG = [ps[:, 1:3, :].rearrange("p b (c d) -> p (b c) d", d=P), ps[:, 3:5, :].rearrange("p b (c d) -> p (b c) d", d=P)]
        psH = ps[:, 5:7, :].rearrange("p b (c d) -> p (b c) d", d=P)
        psM = bank(7, 0)
        psU = [ps[:, 2 * n:2 * n + 2, :].rearrange("p b (c d) -> p (b c) d", d=DUO * P) for n in range(RING)]
        psD, psGB = [bank(4 + n, 0, DUO * P) for n in range(2)], bank(6, 0, DUO * P)
        GB = Mk[:, :].rearrange("p (u n) -> p u n", u=2)
        gates_of = t64[:, 0:8, :].rearrange("p n t -> p (n t)")[:, 0:2 * DUO * 2 * MOE].rearrange("p (u t n) -> p u t n", u=2, t=DUO)
        psGT = ps[0:2 * MOE, 7, DUO * P:2 * DUO * P]
        psB = bank(7, 0, DUO * P).rearrange("p (t d) -> p t d", t=DUO)

        cTv = cT[:, :].rearrange("p (t b q) -> p t b q", b=2, q=SEQ)
        cTt = cT[:, :].rearrange("p (t d) -> p t d", d=P)
        xTt = xT_all.rearrange("p (t d) -> p t d", d=P)
        cT_duo = cT[:, :].rearrange("p (t d) -> p t d", d=DUO * P)
        xs_duo = xs[:, :, :].rearrange("p (s t) d -> p s t d", t=DUO)
        xs_g, o_g, xT_g, cT_g = by_group(xs), by_group(o_all), by_group(xTt), by_group(cTt)
        rs_g, mean_g = group_cols(rs[:, :]), group_cols(mv[:, 0, :])

        loaded, ctx_loaded, tables, experts_in, stored = sem("loaded"), sem("ctxT_loaded"), sem("tables_loaded"), sem("experts_loaded"), sem("stored")
        X_PARTS = 4
        x_in = [sem(f"x_part{n}_in") for n in range(X_PARTS)]
        ctx_in = [sem("ctx_tile0_in"), sem("ctx_tile1_in")]
        ones_ready, sums_done, quantised, folds_done, folds_ready, bound_ready = (
            sem("ones_ready"), sem("sums_done"), sem("quantised"), sem("folds_done"), sem("folds_ready"), sem("bound_ready"))
        phase = sem("phase_ready")
        var_ready, std_ready = sem("var_ready"), sem("std_ready")
        xn_step, xn_ready, aT_raw, aT_ready = sem("xn_step"), sem("xn_ready"), sem("aT_raw"), sem("aT_ready")
        q_done, k_done, v_done = sem("q_done"), sem("k_done"), sem("v_done")
        qb_ready, kc_ready, kx_ready, vb_ready = sem("qb_ready"), sem("kc_ready"), sem("kx_ready"), sem("vb_ready")
        s_done, mx_ready, less_max, probs_ready = sem("scores_done"), sem("max_ready"), sem("less_max"), sem("probs_ready")
        turned, turned_ready = sem("probsT_done"), sem("probsT_ready")
        sT_done, tanh_done, pv_done = sem("scoresT_done"), sem("tanh_done"), sem("pv_done")
        rec_ready, o_ready, oT_done, oT_ready = sem("rec_ready"), sem("o_ready"), sem("oT_done"), sem("oT_ready")
        y_done, y_used = sem("y_done"), sem("y_used")
        x_added, x_seen = sem("x_added"), sem("x_seen")
        ln_step, ln_gain, ln_ready, squares_done = sem("ln_step"), sem("ln_gain"), sem("ln_ready"), sem("squares_done")
        o_seen, xT_seen, sim_seen, ln_seen, y_seen, pe_seen = sem("o_seen"), sem("xT_seen"), sem("sim_seen"), sem("ln_seen"), sem("y_seen"), sem("pe_seen")
        e_done, vT_done, e_ready, vT_ready, v_raw, v_ready = (
            sem("e_done"), sem("vT_done"), sem("e_ready"), sem("vT_ready"), sem("v_raw"), sem("v_ready"))
        xs_done, xmx_ready, nmx_ready, p_ready, pT_raw, pT_ready, xo_done, rden_ready, xrec_ready = (
            sem("xscores_done"), sem("xmax_ready"), sem("xnegmax_ready"), sem("xprobs_ready"), sem("xprobsT_raw"),
            sem("xprobsT_ready"), sem("xout_done"), sem("rden_ready"), sem("xrec_ready"))
        bn_done = sem("bn_done")
        xb_ready, sim_done, v8_ready, d_ready, ex_ready = (
            sem("xb_ready"), sem("sim_done"), sem("v8_ready"), sem("d_ready"), sem("ex_ready"))
        t8_ready, z_ready, rz_ready, dg_ready = (
            sem("t8_ready"), sem("z_ready"), sem("rz_ready"), sem("dg_ready"))
        ee_ready, ww_ready, g_part = sem("ee_ready"), sem("ww_ready"), sem("g_part")
        rt_ready, pair_ready, cd_ready, cd_seen = sem("rt_ready"), sem("pair_ready"), sem("cd_ready"), sem("cd_seen")
        h_done, h_ready, hg_ready, m_done = sem("h_done"), sem("h_ready"), sem("hg_ready"), sem("m_done")
        y_used_x, y_used_m = sem("xout_used"), sem("memory_used")
        lg_done, lg_ready, lg_less_max, le_ready = sem("lg_done"), sem("lg_ready"), sem("lg_less_max"), sem("le_ready")
        a_step, a_split, w_step, w_split = sem("a_step"), sem("a_split"), sem("w_step"), sem("w_split")
        d_step, d_split, pick_ready, g_turned, gT_ready, g_ready = sem("d_step"), sem("d_split"), sem("pick_ready"), sem("gates_turned_done"), sem("gates_turned_ready"), sem("gates_taken")
        up_done, hid_ready, h_up_ready, h_split, down_done = (
            sem("up_done"), sem("hidden_ready"), sem("hidden_up_ready"), sem("hidden_split"), sem("down_done"))
        gb_done, gb_ready = sem("gates_spread_done"), sem("gates_spread_ready")
        prod_ready, acc_done, back_done, out_ready = sem("prod_ready"), sem("acc_done"), sem("back_done"), sem("out_ready")

        PHASE = dict(attn0=1, norm0=2, out0=3, cross0=4, bn=5, memory=6, attn1=7, cross1=8, routing=9, experts=10)
        NORM = dict(attn0=0, out0=NT, cross0=NT + NG, bn=NT + 2 * NG, attn1=NT + 3 * NG, cross1=2 * NT + 3 * NG, routing=3 * NT + 3 * NG)
        ATTN = dict(attn0=0, attn1=NT, cross1=2 * NT)
        OUTT = dict(attn1=0, cross1=NT)
        PROJ = dict(out0=0, attn1=NG, cross1=NG + NT)
        XSCALE = float(P) ** -0.5
        HSCALE = float(DH) ** -0.5
        N_LOADS = 22

        block = es.enter_context(nc.Block())

        @block.sync
        def _(sp):
            loads = [
                (cst[:, :], consts), (row[:, :], rows), (col[:, :], cols), (wq0_s, wq0), (wk0_s, wk0),
                (small[:, WV0, :], wv0), (small[:, WO0, :], wo0), (small[:, XWV, :], xWvT), (small[:, WV1, :], wv1),
                (small[:, WO1, :], wo1), (small[:, WOUT, :], wout), (raw[:, RWQ, :], xWq), (raw[:, RWK, :], xWk),
                (raw[:, RWE1, :], xWeT[0:P, :]), (raw[:, RWE2, :], xWeT[P:2 * P, :]),
                (rqk, wqk.rearrange("(n p) d -> p n d", p=P)), (rkey, keysT.rearrange("n p k -> p n k")), (rt[:, :], router),
                (mask4[:, :], mask), (sc[:, 0:2], scal),
                (wq1_s[:, :], wq1), (wk1_s[:, :], wk1),
            ]
            assert len(loads) == N_LOADS
            xv = x.rearrange("(t p) d -> p t d", p=P)
            for n in range(X_PARTS):
                part = slice(n * NT // X_PARTS, (n + 1) * NT // X_PARTS)
                sp.dma_start(xs[:, part, :], xv[:, part, :]).then_inc(x_in[n], 16)
            for dst, src in loads:
                sp.dma_start(dst, src).then_inc(loaded, 16)
            sp.dma_start(cT[:, :], ctxT).then_inc(ctx_loaded, 16)
            sp.wait_ge(phase, PHASE["norm0"])
            sp.dma_start(kin, key_inT).then_inc(tables, 16)
            sp.dma_start(kout, key_out.rearrange("(c p) d -> p c d", p=P)).then_inc(tables, 16)
            sp.wait_ge(phase, PHASE["attn1"])
            sp.dma_start(up_w, up.rearrange("e p h -> p e h")).then_inc(experts_in, 16)
            sp.dma_start(down_w, down.rearrange("e (c p) d -> p e c d", p=P)).then_inc(experts_in, 16)
            sp.wait_ge(phase, PHASE["cross1"])
            ctx_v = ctx.rearrange("(t p) d -> t p d", p=P)

            def ctx_load(T):
                need(sp, vb_ready, T.before(2, ATTN["cross1"]))
                need(sp, k_done, T.before(2, ATTN["cross1"]))
                sp.dma_start(ctile[:, T.u, :], ctx_v[T.t]).then_inc(ctx_in[T.u], 16)
            staggered(nc, sp, NT, [(0, ctx_load)])
            ov = out.rearrange("(t p) d -> p t d", p=P)
            parts = 4
            for n in range(parts):
                a, b = n * NT // parts, (n + 1) * NT // parts
                sp.wait_ge(out_ready, b // DUO)
                sp.dma_start(ov[:, a:b, :], xs[:, a:b, :]).then_inc(stored, 16)
            sp.wait_ge(stored, 16 * parts)

        @block.gpsimd
        def _(pool):
            pool.memset(ones[:, :], 1.0).then_inc(ones_ready, 1)

            own_head = C("own_head").unsqueeze(1).unsqueeze(3).to_broadcast([P, SETS, PER_SET, SEQ])

            def spread(base):
                def seg(T):
                    u = T.u
                    if base == ATTN["cross1"]:
                        pool.wait_ge(aT_ready, T.now(NORM["cross1"]))
                        need(pool, sT_done, T.before(2))
                    else:
                        pool.wait_ge(kc_ready, T.now(base))
                        need(pool, s_done, T.step(SETS, -SETS, base))
                    pool.tensor_tensor(KX[:, u].rearrange("p g (h k) -> p g h k", h=PER_SET),
                                       KC[:, u].unsqueeze(2).to_broadcast([P, SETS, PER_SET, SEQ]), own_head, ALU.mult)\
                        .then_inc(kx_ready, 1)
                return seg

            pool.wait_ge(phase, PHASE["attn0"])
            staggered(nc, pool, NT, [(0, spread(ATTN["attn0"]))])

            pool.wait_ge(phase, PHASE["norm0"])

            def gain_and_shift(T):
                o = o_g[:, T.t]
                pool.wait_ge(ln_step, T.now())
                pool.sem_inc(ln_seen, 1)
                pool.tensor_tensor(o, o, R("g0").unsqueeze(1).to_broadcast([P, GROUP, P]), ALU.mult).then_inc(ln_gain, 1)
                pool.wait_ge(ln_gain, T.now())
                pool.sem_inc(ln_seen, 1)
                pool.tensor_tensor(o, o, R("b0").unsqueeze(1).to_broadcast([P, GROUP, P]), ALU.add).then_inc(ln_ready, 1)
            staggered(nc, pool, NG, [(0, gain_and_shift)])

            def add_projection(T):
                pool.wait_ge(y_used, T.now(PROJ["out0"]))
                pool.sem_inc(y_seen, 1)
                pool.tensor_tensor(xs_g[:, T.t], xs_g[:, T.t], yg[:, T.u], ALU.add).then_inc(x_added, 1)
            staggered(nc, pool, NG, [(0, add_projection)])

            pool.wait_ge(phase, PHASE["memory"])

            def outer(T):
                pool.wait_ge(ex_ready, T.now())
                best = EX[:, T.u, NS:].rearrange("p (n k) -> p n k", k=TOPK)
                need(pool, t8_ready, T.before(1))
                pool.tensor_tensor(CD.rearrange("p h (i j) -> p h i j", i=TOPK),
                                   best[:, 0:PH].unsqueeze(3).to_broadcast([P, PH, TOPK, TOPK]),
                                   best[:, PH:].unsqueeze(2).to_broadcast([P, PH, TOPK, TOPK]), ALU.mult).then_inc(cd_ready, 1)
                for h in range(PH):
                    a, b = NKEY * h, NKEY * (PH + h)
                    need(pool, ww_ready, T.step(PH, h + 1 - HRING))
                    pool.tensor_tensor(EE[:, h % HRING, :].rearrange("p (i j) -> p i j", i=NKEY),
                                       EX[:, T.u, a:a + NKEY].unsqueeze(2).to_broadcast([P, NKEY, NKEY]),
                                       EX[:, T.u, b:b + NKEY].unsqueeze(1).to_broadcast([P, NKEY, NKEY]),
                                       ALU.mult).then_inc(ee_ready, 1)
            staggered(nc, pool, NT, [(0, outer)])

            pool.wait_ge(phase, PHASE["attn1"])
            staggered(nc, pool, NT, [(0, spread(ATTN["attn1"]))])
            pool.wait_ge(phase, PHASE["cross1"])
            staggered(nc, pool, NT, [(0, spread(ATTN["cross1"]))])

            pool.wait_ge(w_step, 1)
            pool.tensor_tensor(w_low[:, :, :], up_w, w_up[:, :, :].bitcast(F32), ALU.subtract).then_inc(w_split, 1)
            pool.tensor_copy(d_up[:, :, :, :], down_w).then_inc(d_step, 1)
            pool.wait_ge(d_step, 1)
            pool.tensor_tensor(d_low[:, :, :, :], down_w, d_up[:, :, :, :].bitcast(F32), ALU.subtract).then_inc(d_split, 1)

        @block.scalar
        def _(act):
            act.wait_ge(loaded, 16 * N_LOADS)
            act.activation(sc[:, 2:3], sc[:, 1:2], ACT.Exp).then_inc(bound_ready, 1)
            act.wait_ge(folds_done, 1)
            act.activation(small[:, A1, :], bank(0, 0), ACT.Copy)
            act.activation(small[:, A2, :], bank(0, P), ACT.Copy)
            act.activation(Mk[:, :], ps[:, 1, :], ACT.Copy).then_inc(folds_ready, 1)

            def deviations(n, width=NT):
                act.wait_ge(var_ready, n)
                act.activation(t64[:, 1, 0:width], t64[:, 0, 0:width], ACT.Sqrt).then_inc(std_ready, 1)

            def copy_aT(base, projected, projected_base):
                def seg(T):
                    act.wait_ge(aT_raw, T.now(base))
                    need(act, projected, T.before(2, projected_base))
                    act.activation(aT[:, T.u, :], psA, ACT.Copy).then_inc(aT_ready, 1)
                return seg

            def exps(base):
                def seg(T):
                    act.wait_ge(less_max, T.step(SETS, SETS, base))
                    act.activation(PQ[:, T.u, :], PQ[:, T.u, :], ACT.Exp).then_inc(probs_ready, 1)
                return seg

            def copy_probsT(base, half):
                def seg(T):
                    act.wait_ge(turned, T.step(2, half + 1, base))
                    if half == 0:
                        need(act, pv_done, T.before(2, base))
                    act.activation(PT[:, T.u, half * 512:half * 512 + 512], psPT[:, half, :], ACT.Copy).then_inc(turned_ready, 1)
                return seg

            def copy_k(base):
                def seg(T):
                    act.wait_ge(k_done, T.now(base))
                    need(act, kx_ready, T.before(2, base))
                    for g in range(SETS):
                        ins = act.activation(KC[:, T.u, g, :], psKc[:, g, :], ACT.Identity, bias=bk_s[:, g:g + 1])
                    ins.then_inc(kc_ready, 1)
                return seg

            def copy_q(base):
                def seg(T):
                    act.wait_ge(q_done, T.now(base))
                    need(act, s_done, T.step(SETS, -SETS, base))
                    for g in range(SETS):
                        for b in range(2):
                            part = slice(SEQ * b, SEQ * b + SEQ)
                            ins = act.activation(QB[part, T.u, g, part], psQ[part, g, :], ACT.Identity, bias=bq_s[part, g:g + 1])
                    ins.then_inc(qb_ready, 1)
                return seg

            def copy_oT(base):
                def seg(T):
                    act.wait_ge(oT_done, T.now(base))
                    need(act, y_done, T.before(2, PROJ["attn1" if base == OUTT["attn1"] else "cross1"]))
                    act.activation(OT[:, T.u, :], psOT, ACT.Copy).then_inc(oT_ready, 1)
                return seg

            deviations(1)
            deviations(2)
            act.wait_ge(phase, PHASE["attn0"])

            b0 = ATTN["attn0"]
            staggered(nc, act, NT, [(1, copy_aT(NORM["attn0"], v_done, b0)), (4, copy_probsT(b0, 0)), (1, copy_k(b0)),
                                    (4, copy_probsT(b0, 1)), (1, copy_q(b0)), (3, exps(b0))])

            deviations(3)

            def squares(T):
                act.wait_ge(ln_ready, T.now())
                need(act, squares_done, T.step(GROUP, -GROUP))
                for t in range(GROUP):
                    act.activation(aTg[:, T.u, t, :], o_g[:, T.t, t, :], ACT.Square, accum_out=group_cols(t64[:, 2, :])[:, T.t, t:t + 1])\
                        .then_inc(squares_done, 1)
            staggered(nc, act, NG, [(0, squares)])
            deviations(4)

            def copy_ints(T):
                act.wait_ge(aT_raw, T.now(NORM["out0"]))
                need(act, y_done, T.before(2, PROJ["out0"]))
                act.activation(ints[:, T.u], psAg[T.u], ACT.Identity, bias=sc[:, 25:26]).then_inc(aT_ready, 1)
            staggered(nc, act, NG, [(1, copy_ints)])

            deviations(5)
            act.wait_ge(phase, PHASE["cross0"])

            def copy_xnT(T):
                act.wait_ge(aT_raw, T.now(NORM["cross0"]))
                need(act, e_done, T.before(2))
                act.activation(aTg[:, T.u], psAx, ACT.Copy).then_inc(aT_ready, 1)

            def entangle(T):
                u = T.u
                act.wait_ge(e_done, T.now())
                need(act, xs_done, T.before(2))
                act.activation(ent[:, u], psE, ACT.Tanh, bias=sc[:, 12:13]).then_inc(e_ready, 1)
                act.wait_ge(vT_done, T.now())
                need(act, v_raw, T.before(2))
                act.activation(VT[:, u], psVT, ACT.Identity, bias=K("xbv")).then_inc(vT_ready, 1)

            def x_exps(T):
                u = T.u
                act.wait_ge(v_raw, T.now())
                need(act, xo_done, T.before(2))
                act.activation(Vt[:, u], psVx, ACT.Copy).then_inc(v_ready, 1)
                act.wait_ge(nmx_ready, T.now())
                need(act, pT_raw, T.before(2))
                need(act, rden_ready, T.before(2))
                for b in range(2):
                    part = slice(SEQ * b, SEQ * b + SEQ)
                    ins = act.activation(PB[part, u, :, part], SX[part, u], ACT.Exp, scale=XSCALE)
                ins.then_inc(p_ready, 1)

            def copy_pT(T):
                act.wait_ge(pT_raw, T.now())
                need(act, xo_done, T.before(2))
                act.activation(PBT[:, T.u], psXT, ACT.Copy).then_inc(pT_ready, 1)
            staggered(nc, act, NG, [(1, copy_xnT), (3, copy_pT), (2, x_exps), (1, entangle)])

            deviations(6)

            def keep_xT(T):
                act.wait_ge(aT_raw, T.now(NORM["bn"]))
                act.activation(xT_g[:, T.t], psAg[T.u], ACT.Copy).then_inc(aT_ready, 1)
            staggered(nc, act, NG, [(1, keep_xT)])
            deviations(7, 1)

            act.wait_ge(phase, PHASE["memory"])

            def normed(T):
                need(act, sim_done, T.before(2))
                act.activation(xb[:, T.u, :], xTt[:, T.t, :], ACT.Identity, scale=sc[:, 13:14], bias=sc[:, 14:15])\
                    .then_inc(xb_ready, 1)

            def key_exps(T):
                act.wait_ge(d_ready, T.now())
                act.activation(EX[:, T.u, :], EX[:, T.u, :], ACT.Exp).then_inc(ex_ready, 1)

            def diagonals(T):
                act.wait_ge(rz_ready, T.now())
                need(act, g_part, T.step(GATES, -GATES))
                for h in range(GATES):
                    ins = act.activation(DG[:, T.u, h, :], ident, ACT.Copy, scale=RZ[:, T.u, h:h + 1])
                ins.then_inc(dg_ready, 1)

            def hidden(T):
                act.wait_ge(h_done, T.now())
                need(act, hg_ready, T.before(1))
                act.activation(HT, psH, ACT.Gelu).then_inc(h_ready, 1)
            staggered(nc, act, NT, [(0, normed), (1, hidden), (0, key_exps), (0, diagonals)])

            deviations(8)
            act.wait_ge(phase, PHASE["attn1"])
            b1 = ATTN["attn1"]
            staggered(nc, act, NT, [(1, copy_aT(NORM["attn1"], v_done, b1)), (4, copy_probsT(b1, 0)), (5, copy_oT(OUTT["attn1"])),
                                    (1, copy_k(b1)), (4, copy_probsT(b1, 1)), (1, copy_q(b1)), (3, exps(b1))])

            deviations(9)
            act.wait_ge(phase, PHASE["cross1"])

            b2 = ATTN["cross1"]

            def tanhs(T):
                act.wait_ge(sT_done, T.now())
                need(act, pv_done, T.before(2, b2))
                act.activation(PT[:, T.u, :], psST, ACT.Tanh, scale=sc[:, 3:4]).then_inc(tanh_done, 1)

            def bounded_exps(T):
                act.wait_ge(tanh_done, T.now())
                act.activation(PT[:, T.u, :], PT[:, T.u, :], ACT.Exp, scale=sc[:, 2:3], bias=tile_col(mbias[:, :], T))\
                    .then_inc(probs_ready, 1)

            def copy_q_as_is(T):
                act.wait_ge(aT_raw, T.now(NORM["cross1"]))
                need(act, kx_ready, T.before(2, b2))
                act.activation(KC[:, T.u], psKc, ACT.Copy).then_inc(aT_ready, 1)
            staggered(nc, act, NT, [(3, tanhs), (5, copy_oT(OUTT["cross1"])), (1, copy_q_as_is), (3, bounded_exps)])

            deviations(10)
            act.wait_ge(phase, PHASE["routing"])
            act.wait_ge(experts_in, 32)
            act.activation(w_up[:, :, :], up_w, ACT.Copy).then_inc(w_step, 1)

            def keep_aT(T):
                act.wait_ge(aT_raw, T.now(NORM["routing"]))
                need(act, lg_done, T.before(2))
                act.activation(cT_g[:, T.t], psAg[T.u], ACT.Copy)
                act.activation(aTg[:, T.u], psAg[T.u], ACT.Copy).then_inc(aT_ready, 1)
            staggered(nc, act, NG, [(1, keep_aT)])
            act.wait_ge(lg_less_max, 1)
            act.activation(le, le, ACT.Exp).then_inc(le_ready, 1)
            act.wait_ge(phase, PHASE["experts"])

            def gelu(T, e):
                n = e % RING
                act.wait_ge(up_done, T.step(MOE, e + 1))
                need(act, h_split, T.step(MOE, e + 1 - RING))
                act.activation(hid[n], psU[n], ACT.Gelu_apprx_tanh).then_inc(hid_ready, 1)

            def upper_half(T, e):
                n = e % RING
                act.wait_ge(hid_ready, T.step(MOE, e + 1))
                need(act, down_done, T.step(MOE, e + 1 - RING))
                act.activation(h_up[:, n], hid[n], ACT.Copy).then_inc(h_up_ready, 1)

            def keep_gates(T, e):
                act.wait_ge(gb_done, T.step(MOE, e + 1))
                need(act, prod_ready, T.step(MOE, e - 1))
                act.activation(GB[:, e % 2], psGB, ACT.Copy).then_inc(gb_ready, 1)

            def of(step, e):
                return lambda T: step(T, e)

            def between(T):
                for e in range(RING, MOE):
                    gelu(T, e)
                    keep_gates(T, e - RING)
                    upper_half(T, e)
            staggered(nc, act, NT // DUO, [(0, of(gelu, 0)), (1, of(keep_gates, MOE - 2)), (0, of(upper_half, 0)), (0, of(gelu, 1)),
                                           (1, of(keep_gates, MOE - 1)), (0, of(upper_half, 1)), (0, between)])

        @block.tensor
        def _(pe):
            pe.wait_ge(loaded, 16 * N_LOADS)
            pe.wait_ge(ones_ready, 1)
            pe.wait_ge(quantised, 1)
            pe.matmul(bank(3, 0, 4), ones[:, :], sc[:, 4:8], start=True, stop=True).then_inc(sums_done, 1)
            pe.matmul(bank(0, 0), raw[:, RWQ, :], raw[:, RWE1, :], start=True, stop=True)
            pe.matmul(bank(0, P), raw[:, RWK, :], raw[:, RWE2, :], start=True, stop=True)
            pe.matmul(bank(4, 0, 1), raw[:, RWE1, :], K("xbq"), start=True, stop=False)
            pe.matmul(bank(4, 0, 1), raw[:, RWE2, :], K("xbk"), start=False, stop=True)
            for n in range(2 * PH):
                ins = pe.matmul(bank(1, n * NKEY, NKEY), rqk[:, n, :], rkey[:, n, :], start=True, stop=True)
            ins.then_inc(folds_done, 1)

            def transposed(base, banks):
                def seg(T):
                    pe.wait_ge(xn_ready, T.now(base))
                    need(pe, aT_ready, T.before(len(banks), base))
                    for t in range(GROUP):
                        ins = pe.transpose(banks[T.u % len(banks)][:, t, :], xng[:, T.u, t, :], ident)
                    ins.then_inc(aT_raw, 1)
                return seg

            def transposed_beside_q(base, nbase):
                def seg(T):
                    pe.wait_ge(xn_ready, T.now(nbase))
                    need(pe, qb_ready, T.before(1, base))
                    pe.transpose(psA, xn[:, T.u, :], ident).then_inc(aT_raw, 1)
                return seg

            def project_k(base, nbase, w):
                def seg(T):
                    pe.wait_ge(aT_ready, T.now(nbase))
                    need(pe, kc_ready, T.before(1, base))
                    for g in range(SETS):
                        for b in range(2):
                            part = slice(SEQ * b, SEQ * b + SEQ)
                            ins = pe.matmul(psKc[part, g, :], w[:, SEQ * g:SEQ * g + SEQ], aT[:, T.u, part], start=True, stop=True)
                    ins.then_inc(k_done, 1)
                return seg

            def project_q(base, w, obase):
                def seg(T):
                    if obase is not None:
                        need(pe, oT_ready, T.before(4, obase))
                    for g in range(SETS):
                        for b in range(2):
                            part = slice(SEQ * b, SEQ * b + SEQ)
                            ins = pe.matmul(psQ[part, g, :], w[:, SEQ * g:SEQ * g + SEQ], aT[:, T.u, part], start=True, stop=True)
                    ins.then_inc(q_done, 1)
                return seg

            def project_v(base, w, ybase):
                def seg(T):
                    need(pe, vb_ready, T.before(1, base))
                    if ybase is not None:
                        need(pe, y_used, T.before(3, ybase))
                    for b in range(2):
                        for h in range(2):
                            ins = pe.matmul(psV[SEQ * h:SEQ * h + SEQ, SEQ * b:SEQ * b + SEQ], aT[:, T.u, SEQ * b:SEQ * b + SEQ],
                                            w[:, SEQ * h:SEQ * h + SEQ], start=True, stop=True)
                    ins.then_inc(v_done, 1)
                return seg

            def scores(base, causal, g):
                def seg(T):
                    u = T.u
                    if g == 0:
                        pe.wait_ge(qb_ready, T.now(base))
                        pe.wait_ge(kx_ready, T.now(base))
                    need(pe, less_max, T.step(SETS, g + 1 - SETS, base))
                    if causal:
                        pe.matmul(ps[:, g, :], maskq_b[0:MASK_ROWS, :], maskk_b[0:MASK_ROWS, g, :], start=True, stop=False)
                    pe.matmul(ps[:, g, :], QB[:, u, g, :], KX[:, u, g, :], start=not causal, stop=True).then_inc(s_done, 1)
                return seg

            def scoresT(base):
                def seg(T):
                    u = T.u
                    pe.wait_ge(qb_ready, T.now(base))
                    pe.wait_ge(kx_ready, T.now(base))
                    need(pe, tanh_done, T.before(1))
                    for g in range(SETS):
                        ins = pe.matmul(psST[:, g, :], QB[:, u, g, :], KX[:, u, g, :], start=True, stop=True)
                    ins.then_inc(sT_done, 1)
                return seg

            def probsT(base, half):
                def seg(T):
                    if half == 0:
                        pe.wait_ge(probs_ready, T.now(base))
                    need(pe, turned_ready, T.step(2, half - 1, base))
                    for n in range(PAIRS // 2):
                        i = half * (PAIRS // 2) + n
                        ins = pe.transpose(psPT[:, half, n * P:n * P + P], PQ[:, T.u, i * P:i * P + P], ident)
                    ins.then_inc(turned, 1)
                return seg

            def values_of_pairs(base):
                def seg(T):
                    u = T.u
                    pe.wait_ge(vb_ready, T.now(base))
                    need(pe, o_ready, T.before(1, base))
                    for i in range(PAIRS):
                        if i % (PAIRS // 2) == 0:
                            pe.wait_ge(turned_ready, T.step(2, i // (PAIRS // 2) + 1, base))
                        for b in range(2):
                            part = slice(SEQ * b, SEQ * b + SEQ)
                            a = i * P + SEQ * b
                            ins = pe.matmul(psOq[part, 2 * i:2 * i + 2, :].rearrange("p h d -> p (h d)"), PT[:, u, a:a + SEQ],
                                            VBp[:, u, b, i].rearrange("p h d -> p (h d)"), start=True, stop=True)
                    ins.then_inc(pv_done, 1)
                return seg

            def values_of_heads(base):
                def seg(T):
                    u = T.u
                    pe.wait_ge(probs_ready, T.now(base))
                    pe.wait_ge(vb_ready, T.now(base))
                    need(pe, o_ready, T.before(1, base))
                    for h in range(HEADS):
                        ins = pe.matmul(psOh[:, h].rearrange("p b d -> p (b d)"), PT[:, u, h * SEQ:h * SEQ + SEQ],
                                        VBh[:, u, h].rearrange("p b d -> p (b d)"), start=True, stop=True)
                    ins.then_inc(pv_done, 1)
                return seg

            def outputT(base, nbase):
                def seg(T):
                    pe.wait_ge(o_ready, T.now(base))
                    if base == ATTN["cross1"]:
                        need(pe, oT_ready, T.before(1, OUTT["cross1"]))
                        pe.sem_inc(pe_seen, 1)
                        for b in range(2):
                            ins = pe.transpose(psOT[:, SEQ * b:SEQ * b + SEQ], O[0:SEQ, T.u, b], ident[0:SEQ, 0:SEQ])
                    else:
                        pe.wait_ge(aT_ready, T.ahead(4, nbase, NT))
                        ins = pe.transpose(psOT, O[:, T.u, 0], ident)
                    ins.then_inc(oT_done, 1)
                return seg

            def out_project(ready, rbase, base, src, w, shared=None):
                def seg(T):
                    pe.wait_ge(ready, T.now(rbase))
                    need(pe, y_used, T.before(1, base))
                    if shared is not None:
                        sem, n, sbase = shared
                        pe.wait_ge(sem, T.ahead(n, sbase, NT))
                    pe.matmul(psY, src(T.u), w, start=True, stop=True).then_inc(y_done, 1)
                return seg

            b0 = ATTN["attn0"]
            pe.wait_ge(phase, PHASE["attn0"])
            n0 = NORM["attn0"]
            staggered(nc, pe, NT, [(3, scores(b0, False, 0)), (3, scores(b0, False, 1)), (3, project_v(b0, small[:, WV0, :], None)), (1, transposed_beside_q(b0, n0)),
                                   (4, probsT(b0, 0)), (1, project_k(b0, n0, wk0_s)), (4, probsT(b0, 1)),
                                   (1, project_q(b0, wq0_s, None)), (4, values_of_pairs(b0))])
            pe.wait_ge(phase, PHASE["out0"])

            def project_ints(T):
                pe.wait_ge(aT_ready, T.now(NORM["out0"]))
                need(pe, y_used, T.before(2, PROJ["out0"]))
                for t in range(GROUP):
                    ins = pe.matmul(psYg[T.u][:, t, :], ints[:, T.u, t, :], wo0_b[:, :], start=True, stop=True)
                ins.then_inc(y_done, 1)
            staggered(nc, pe, NG, [(1, transposed(NORM["out0"], psAg)), (2, project_ints)])

            pe.wait_ge(phase, PHASE["cross0"])
            pe.wait_ge(ctx_loaded, 16)

            def entangled(T):
                need(pe, e_ready, T.before(1))
                pe.matmul(psE, small[:, A2, :], cT_g[:, T.t], start=True, stop=False)
                pe.wait_ge(aT_ready, T.now(NORM["cross0"]))
                pe.matmul(psE, small[:, A1, :], aTg[:, T.u], start=False, stop=True).then_inc(e_done, 1)
                need(pe, vT_ready, T.before(1))
                pe.matmul(psVT, small[:, XWV, :], cT_g[:, T.t], start=True, stop=True).then_inc(vT_done, 1)

            def x_scores(T):
                u = T.u
                pe.wait_ge(e_ready, T.now())
                pe.wait_ge(vT_ready, T.now())
                need(pe, nmx_ready, T.before(1))
                for t in range(GROUP):
                    for b in range(2):
                        part = slice(SEQ * b, SEQ * b + SEQ)
                        ins = pe.matmul(psSx[part, t, :], ent[:, u, t, part], VT[:, u, t, part], start=True, stop=True)
                ins.then_inc(xs_done, 1)
                need(pe, v_ready, T.before(1))
                for t in range(GROUP):
                    ins = pe.transpose(psVx[:, t, :], VT[:, u, t, :], ident)
                ins.then_inc(v_raw, 1)

            def x_probsT(T):
                pe.wait_ge(p_ready, T.now())
                need(pe, pT_ready, T.before(1))
                for t in range(GROUP):
                    ins = pe.transpose(psXT[:, t, :], PB[:, T.u, t, :], ident)
                ins.then_inc(pT_raw, 1)

            def x_values(T):
                pe.wait_ge(pT_ready, T.now())
                pe.wait_ge(v_ready, T.now())
                need(pe, y_used_x, T.before(1))
                for t in range(GROUP):
                    ins = pe.matmul(psXO[:, t, :], PBT[:, T.u, t, :], Vt[:, T.u, t, :], start=True, stop=True)
                ins.then_inc(xo_done, 1)
            staggered(nc, pe, NG, [(2, x_scores), (1, transposed(NORM["cross0"], [psAx])), (3, x_probsT), (1, entangled), (3, x_values)])

            pe.wait_ge(phase, PHASE["bn"])
            staggered(nc, pe, NG, [(1, transposed(NORM["bn"], psAg))])

            pe.wait_ge(phase, PHASE["memory"])
            pe.wait_ge(tables, 32)

            def key_scores(T):
                pe.wait_ge(xb_ready, T.now())
                need(pe, d_ready, T.before(1))
                pe.matmul(ps[:, 0, :], xb[:, T.u, :], Mk[:, :], start=True, stop=True).then_inc(sim_done, 1)

            def hidden(T):
                need(pe, h_ready, T.before(1))
                for c in range(CHUNKS):
                    ins = pe.matmul(psH[:, c, :], kin[:, c * P:c * P + P], xTt[:, T.t, :], start=True, stop=True)
                ins.then_inc(h_done, 1)

            def gates(first, last):
                def seg(T):
                    for h in range(first, last):
                        if h == PH - 2:
                            pe.wait_ge(pair_ready, T.now())
                        else:
                            pe.wait_ge(ww_ready, T.step(PH, h + 1))
                        if h == 0:
                            pe.wait_ge(dg_ready, T.now())
                            need(pe, hg_ready, T.before(2))
                        for c in range(CHUNKS):
                            ins = pe.matmul(psG[T.u][:, c, :], WW[:, h % HRING, c * P:c * P + P], DG[:, T.u, h, :],
                                            start=h == 0 and c % 4 == 0, stop=h == GATES - 1, skip_group_check=True)
                        ins.then_inc(g_part, 1)
                return seg

            def mixed(T):
                pe.wait_ge(hg_ready, T.now())
                need(pe, y_used_m, T.before(1))
                for c in range(CHUNKS):
                    ins = pe.matmul(psM, HG[:, c, :], kout[:, c, :], start=c == 0, stop=c == CHUNKS - 1)
                ins.then_inc(m_done, 1)
            staggered(nc, pe, NT, [(0, key_scores), (1, hidden), (1, gates(0, 3)), (2, mixed), (1, gates(3, PH - 1))])

            b1 = ATTN["attn1"]
            pe.wait_ge(phase, PHASE["attn1"])
            n1 = NORM["attn1"]
            staggered(nc, pe, NT, [
                (3, scores(b1, True, 0)), (3, scores(b1, True, 1)), (3, project_v(b1, small[:, WV1, :], PROJ["attn1"])), (1, transposed_beside_q(b1, n1)),
                (4, probsT(b1, 0)), (5, outputT(b1, n1)), (1, project_k(b1, n1, wk1_s)), (4, probsT(b1, 1)),
                (1, project_q(b1, wq1_s, OUTT["attn1"])), (4, values_of_pairs(b1)),
                (5, out_project(oT_ready, OUTT["attn1"], PROJ["attn1"], lambda u: OT[:, u, :], small[:, WO1, :],
                                (vb_ready, 2, b1)))])

            b2 = ATTN["cross1"]
            pe.wait_ge(phase, PHASE["cross1"])
            n2 = NORM["cross1"]

            def place_q(T):
                pe.wait_ge(xn_ready, T.now(n2))
                need(pe, aT_ready, T.before(1, n2))
                pe.sem_inc(pe_seen, 1)
                for g in range(SETS):
                    for b in range(2):
                        part = slice(SEQ * b, SEQ * b + SEQ)
                        ins = pe.matmul(psKc[part, g, :], xn[part, T.u, SEQ * g:SEQ * g + SEQ], ident[part, part], start=True, stop=True)
                ins.then_inc(aT_raw, 1)

            def place_k(T):
                pe.wait_ge(ctx_in[T.u], T.pair * 16 + 16)
                need(pe, qb_ready, T.before(1, b2))
                pe.sem_inc(pe_seen, 1)
                for g in range(SETS):
                    for b in range(2):
                        part = slice(SEQ * b, SEQ * b + SEQ)
                        ins = pe.matmul(psKd[part, g, :], ctile[part, T.u, SEQ * g:SEQ * g + SEQ], ident[part, part], start=True, stop=True)
                ins.then_inc(k_done, 1)
            staggered(nc, pe, NT, [
                (3, scoresT(b2)), (5, outputT(b2, n2)), (1, place_q), (2, place_k), (4, values_of_heads(b2)),
                (5, out_project(oT_ready, OUTT["cross1"], PROJ["cross1"], lambda u: OT[:, u, :], small[:, WOUT, :]))])

            pe.wait_ge(phase, PHASE["routing"])

            def route(T):
                pe.wait_ge(aT_ready, T.now(NORM["routing"]))
                need(pe, lg_ready, T.before(2))
                for t in range(GROUP):
                    ins = pe.matmul(psRg[T.u][:, t, :], aTg[:, T.u, t, :], rt[:, :], start=True, stop=True)
                ins.then_inc(lg_done, 1)
            staggered(nc, pe, NG, [(3, route), (1, transposed(NORM["routing"], psAg))])
            pe.wait_ge(phase, PHASE["experts"])
            pe.wait_ge(experts_in, 32)

            def up_project(T, e):
                if e == 0:
                    pe.wait_ge(a_split, T.now())
                need(pe, hid_ready, T.step(MOE, e + 1 - RING))
                u = T.u
                for c in range(HC):
                    part = slice(c * P, c * P + P)
                    upper, lower = w_up[:, e, part], w_low[:, e, part]
                    to = psU[e % RING][:, c, :]
                    pe.matmul(to, upper, a_low[:, u, :], start=True, stop=False)
                    pe.matmul(to, upper, a_up[:, u, :], start=False, stop=False)
                    ins = pe.matmul(to, lower, a_up[:, u, :], start=False, stop=True)
                ins.then_inc(up_done, 1)

            def turn_gates(T):
                pe.wait_ge(g_ready, T.now())
                need(pe, out_ready, T.before(3))
                need(pe, gT_ready, T.before(1))
                for t in range(DUO):
                    ins = pe.transpose(psGT[:, t * P:t * P + P], gates_of[:, T.u, t, :], ident)
                ins.then_inc(g_turned, 1)

            def down_project(T, e):
                n = e % 2
                if e == 0:
                    pe.wait_ge(gT_ready, T.now())
                need(pe, gb_ready, T.step(MOE, e))
                pe.matmul(psGB, pick[0:2 * MOE, e:e + 1].to_broadcast([2 * MOE, P]), gT[0:2 * MOE, T.u, :], start=True, stop=True)\
                    .then_inc(gb_done, 1)
                need(pe, prod_ready, T.step(MOE, e - 1))
                pe.wait_ge(h_split, T.step(MOE, e + 1))
                for c in range(HC):
                    pe.matmul(psD[n], d_up[:, e, c, :], h_low[:, e % RING, c, :], start=c == 0, stop=False)
                    pe.matmul(psD[n], d_up[:, e, c, :], h_up[:, e % RING, c, :], start=False, stop=False)
                    ins = pe.matmul(psD[n], d_low[:, e, c, :], h_up[:, e % RING, c, :], start=False, stop=c == HC - 1)
                ins.then_inc(down_done, 1)

            def back(T):
                pe.wait_ge(acc_done, T.step(MOE, MOE))
                pe.wait_ge(gT_ready, T.ahead(2, 0, NT // DUO))
                need(pe, out_ready, T.before(1))
                for t in range(DUO):
                    ins = pe.transpose(psB[:, t, :], acc[:, T.u, t * P:t * P + P], ident)
                ins.then_inc(back_done, 1)

            def ups(e):
                return lambda T: up_project(T, e)

            def downs(e):
                return lambda T: down_project(T, e)

            def between(first, last):
                def seg(T):
                    for e in range(first, last):
                        up_project(T, e)
                        down_project(T, e - RING)
                return seg
            pe.wait_ge(pick_ready, 1)
            pe.wait_ge(w_split, 1)
            pe.wait_ge(d_split, 1)
            staggered(nc, pe, NT // DUO, [(1, ups(0)), (2, downs(MOE - 2)), (1, ups(1)), (2, downs(MOE - 1)), (0, turn_gates),
                                          (1, between(2, 6)), (2, back), (1, between(6, MOE))])

        @block.vector
        def _(dve):
            seen = [0]

            def rsqrt(dst, src, width=NT):
                seen[0] += 1
                dve.tensor_scalar(t64[:, 0, 0:width], src, EPS, None, ALU.add).then_inc(var_ready, 1)
                dve.wait_ge(std_ready, seen[0])
                dve.reciprocal(dst, t64[:, 1, 0:width])
                dve.drain()

            for n in range(X_PARTS):
                first, last = n * NT // X_PARTS, (n + 1) * NT // X_PARTS
                dve.wait_ge(x_in[n], 16)
                dve.tensor_reduce(t64[:, 3, first:last], xs[:, first:last, :], X, ALU.max)
                dve.tensor_reduce(t64[:, 4, first:last], xs[:, first:last, :], X, ALU.min)

                def input_stats(T):
                    dve.bn_stats(st_all[:, T.t + first, :], xs[:, T.t + first, :])
                staggered(nc, dve, last - first, [(0, input_stats)])

            dve.wait_ge(loaded, 16 * N_LOADS)
            quant = ((wq0_s, P * P), (wk0_s, 2 * SEQ * P), (small[:, WV0, :], 2 * SEQ * P),
                     (small[:, WO0, :], P * P))
            for n, (w, count) in enumerate(quant):
                dve.tensor_reduce(sc[:, 4 + n:5 + n], w, X, ALU.add, apply_absolute_value=True)
                dve.drain()
            dve.sem_inc(quantised, 1)
            dve.wait_ge(sums_done, 1)
            for n, (w, count) in enumerate(quant):
                dve.tensor_scalar(sc[:, 16 + n:17 + n], bank(3, n, 1), 1.0 / count, 1e-5, ALU.mult, ALU.max)
            dve.drain()
            dve.reciprocal(sc[:, 20:24], sc[:, 16:20])
            dve.tensor_scalar(sc[:, 24:25], sc[:, 16:17], HSCALE, None, ALU.mult)
            dve.drain()
            for n, (w, count) in enumerate(quant):
                dve.tensor_scalar(w, w, sc[:, 20 + n:21 + n], MAGIC, ALU.mult, ALU.add)
                dve.drain()
                dve.tensor_scalar(w, w, -MAGIC, 1.0, ALU.add, ALU.min)
                dve.drain()
                if n < 3:
                    dve.tensor_scalar(w, w, -1.0, sc[:, 24:25] if n == 0 else sc[:, 16 + n:17 + n], ALU.max, ALU.mult)
                else:
                    dve.tensor_scalar(wo0_b[:, :], w, -1.0, None, ALU.max)
            dve.tensor_scalar(wq1_s[:, :], wq1_s[:, :], HSCALE, None, ALU.mult)
            for name in ("bq0", "bq1"):
                dve.tensor_scalar(K(name), K(name), HSCALE, None, ALU.mult)
            dve.tensor_copy(maskq_b[:, :], C("mask_q"))
            dve.tensor_copy(maskk_b[:, :, :].rearrange("p g c -> p (g c)"), C("mask_k"))
            dve.wait_ge(folds_done, 1)
            dve.tensor_tensor(sc[:, 12:13], bank(4, 0, 1), K("xbe"), ALU.add)
            dve.tensor_scalar(sc[:, 3:4], sc[:, 0:1], HSCALE, None, ALU.mult)
            dve.tensor_copy(mbias[:, :], mask4[:, :].bitcast(U8))
            dve.wait_ge(bound_ready, 1)
            dve.drain()
            dve.tensor_scalar(mbias[:, :], mbias[:, :], NEG, sc[:, 2:3], ALU.mult, ALU.subtract)
            dve.wait_ge(folds_ready, 1)

            def blank_values(name):
                for u in range(2):
                    dve.tensor_copy(VB[:, u, :], C(name))
                dve.memset(QB[:, :, :, :], 0.0)

            def bias_columns(bq, bk):
                dve.tensor_copy(bq_s[:, :], K(bq))
                dve.tensor_copy(bk_s[:, :], K(bk))

            dve.drain()
            dve.memset(sc[:, 25:26], -MAGIC)
            blank_values("vones_pairs")
            bias_columns("bq0", "bk0")

            def row_moments():
                dve.drain()
                even, odd = st_all[:, :, 1], st_all[:, :, 4]
                dve.tensor_tensor(mv[:, 0, :], even, odd, ALU.add)
                dve.tensor_tensor(t64[:, 0, :], even, odd, ALU.subtract)
                dve.tensor_tensor(mv[:, 1, :], st_all[:, :, 2], st_all[:, :, 5], ALU.add)
                dve.drain()
                dve.tensor_scalar(mv[:, 0, :], mv[:, 0, :], 0.5, None, ALU.mult)
                dve.scalar_tensor_tensor(out=t64[:, 0, :], in0=t64[:, 0, :], scalar=0.25, in1=t64[:, 0, :], op0=ALU.mult, op1=ALU.mult)
                dve.drain()
                dve.scalar_tensor_tensor(out=mv[:, 1, :], in0=mv[:, 1, :], scalar=1.0 / P, in1=t64[:, 0, :], op0=ALU.mult, op1=ALU.add)
                dve.drain()

            row_moments()
            mean, var = mv[:, 0, :], mv[:, 1, :]
            rsqrt(rs[:, :], var)
            dve.tensor_tensor(t64[:, 5, :], rs[:, :], rs[:, :], ALU.mult)
            dve.tensor_tensor(t64[:, 3, :], t64[:, 3, :], mean, ALU.subtract)
            dve.tensor_tensor(t64[:, 4, :], mean, t64[:, 4, :], ALU.subtract)
            dve.drain()
            dve.tensor_tensor(t64[:, 5, :], t64[:, 5, :], var, ALU.mult)
            dve.tensor_tensor(t64[:, 3, :], t64[:, 3, :], t64[:, 4, :], ALU.max)
            dve.drain()
            rsqrt(t64[:, 6, :], t64[:, 5, :])
            dve.tensor_tensor(rs[:, :], rs[:, :], t64[:, 6, :], ALU.mult)
            dve.drain()

            def quant_factors(largest, factor, back=None):
                dve.tensor_tensor(t64[:, 7, :], largest, factor, ALU.mult)
                dve.drain()
                dve.tensor_scalar(t64[:, 7, :], t64[:, 7, :], 1e-5, 1.0 / 127.0, ALU.max, ALU.mult)
                dve.drain()
                dve.reciprocal(t64[:, 4, :], t64[:, 7, :])
                if back is None:
                    dve.tensor_copy(s_in[:, 1, :], t64[:, 7, :])
                else:
                    dve.tensor_scalar(s_in[:, 1, :], t64[:, 7, :], back, None, ALU.mult)
                dve.drain()
                dve.tensor_tensor(s_in[:, 0, :], t64[:, 4, :], factor, ALU.mult)
                dve.drain()
            quant_factors(t64[:, 3, :], rs[:, :])
            dve.sem_inc(phase, 1)

            def quantised_rows(T):
                u = T.u
                need(dve, aT_raw, T.before(2, NORM["attn0"]))
                dve.tensor_scalar(xn[:, u, :], xs[:, T.t, :], tile_col(mv[:, 0, :], T), tile_col(s_in[:, 0, :], T), ALU.subtract, ALU.mult)\
                    .then_inc(xn_step, 1)
                dve.wait_ge(xn_step, T.step(2, 1))
                dve.tensor_scalar(xn[:, u, :], xn[:, u, :], MAGIC, -MAGIC, ALU.add, ALU.add).then_inc(xn_step, 1)
                dve.wait_ge(xn_step, T.step(2, 2))
                dve.tensor_scalar(xn[:, u, :], xn[:, u, :], tile_col(s_in[:, 1, :], T), None, ALU.mult).then_inc(xn_ready, 1)

            def normed_groups(base):
                def seg(T):
                    need(dve, aT_raw, T.before(2, base))
                    for t in range(GROUP):
                        ins = dve.tensor_scalar(xng[:, T.u, t, :], xs_g[:, T.t, t, :], mean_g[:, T.t, t:t + 1], rs_g[:, T.t, t:t + 1],
                                                ALU.subtract, ALU.mult)
                    ins.then_inc(xn_ready, 1)
                return seg

            def normed_rows(base):
                def seg(T):
                    need(dve, aT_raw, T.before(2, base))
                    dve.tensor_scalar(xn[:, T.u, :], xs[:, T.t, :], tile_col(mv[:, 0, :], T), tile_col(rs[:, :], T), ALU.subtract, ALU.mult)\
                        .then_inc(xn_ready, 1)
                return seg

            def place_v(base, bv):
                def seg(T):
                    dve.wait_ge(v_done, T.now(base))
                    need(dve, pv_done, T.before(2, base))
                    for h in range(2):
                        part = slice(SEQ * h, SEQ * h + SEQ)
                        ins = dve.tensor_tensor(VBp[part, T.u, :, :, h, 0:DH], psV[part, :].rearrange("p (b i d) -> p b i d", b=2, i=PAIRS),
                                                bv[part, :].rearrange("p (b i d) -> p b i d", b=2, i=PAIRS), ALU.add)
                    ins.then_inc(vb_ready, 1)
                return seg

            def set_of(block, u, g):
                n = PER_SET * SEQ
                return block[:, u, g * n:g * n + n].rearrange("p (h k) -> p h k", h=PER_SET)

            def maxima(base, g):
                def seg(T):
                    dve.wait_ge(s_done, T.step(SETS, g + 1, base))
                    dve.tensor_reduce(mx[:, T.u, g * PER_SET:g * PER_SET + PER_SET], psS[:, g * PER_SET:g * PER_SET + PER_SET, :], X, ALU.max)\
                        .then_inc(mx_ready, 1)
                return seg

            def less_maxima(base, g):
                def seg(T):
                    heads = slice(g * PER_SET, g * PER_SET + PER_SET)
                    dve.wait_ge(mx_ready, T.step(SETS, g + 1, base))
                    need(dve, turned, T.step(2, -2, base))
                    dve.tensor_tensor(set_of(PQ, T.u, g), psS[:, heads, :],
                                      mx[:, T.u, heads].unsqueeze(2).to_broadcast([P, PER_SET, SEQ]), ALU.subtract).then_inc(less_max, 1)
                return seg

            def normalised(base, obase):
                def seg(T):
                    u = T.u
                    dve.wait_ge(pv_done, T.now(base))
                    dve.reciprocal(rec[:, u, 0:HEADS], psOq[:, :, DH]).then_inc(rec_ready, 1)
                    dve.wait_ge(rec_ready, T.now(base))
                    if obase is not None:
                        need(dve, oT_done, T.before(2, obase))
                    to = o_all[:, T.t, :] if obase is None else O[:, u, 0]
                    dve.tensor_tensor(to.rearrange("p (h d) -> p h d", h=HEADS), psOq[:, :, 0:DH],
                                      rec[:, u, 0:HEADS].unsqueeze(2).to_broadcast([P, HEADS, DH]), ALU.mult).then_inc(o_ready, 1)
                return seg

            st_g = by_group(st_all[:, :, :])

            def stats_of_new(T):
                dve.drain()
                dve.bn_stats(st_all[:, T.t, :], xs[:, T.t, :])

            def add_output(name, bias, scale=None):
                base = PROJ[name]

                def seg(T):
                    u = T.u
                    dve.wait_ge(y_done, T.now(base))
                    if bias is None:
                        dve.tensor_tensor(xs[:, T.t, :], psY, xs[:, T.t, :], ALU.add).then_inc(y_used, 1)
                        stats_of_new(T)
                        return
                    if scale is None:
                        dve.tensor_tensor(ytmp[:, u, :], psY, bias, ALU.add).then_inc(y_used, 1)
                    else:
                        dve.scalar_tensor_tensor(out=ytmp[:, u, :], in0=psY, scalar=tile_col(scale[:, :], T), in1=bias, op0=ALU.mult,
                                                 op1=ALU.add).then_inc(y_used, 1)
                    dve.wait_ge(y_used, T.now(base))
                    dve.tensor_tensor(xs[:, T.t, :], xs[:, T.t, :], ytmp[:, u, :], ALU.add)
                    stats_of_new(T)
                return seg

            def output_stats(T):
                dve.wait_ge(o_ready, T.now())
                dve.sem_inc(o_seen, 1)
                dve.bn_stats(st_all[:, T.t, :], o_all[:, T.t, :])
            b0 = ATTN["attn0"]
            staggered(nc, dve, NT, [(5, normalised(b0, None)), (3, maxima(b0, 0)), (3, maxima(b0, 1)), (3, less_maxima(b0, 0)), (3, less_maxima(b0, 1)),
                                    (5, output_stats), (3, place_v(b0, R("bv0"))),
                                    (0, quantised_rows)])
            row_moments()
            rsqrt(rs[:, :], var)
            dve.sem_inc(phase, 1)

            def output_norm(T):
                for t in range(GROUP):
                    o = o_g[:, T.t, t, :]
                    ins = dve.tensor_scalar(o, o, mean_g[:, T.t, t:t + 1], rs_g[:, T.t, t:t + 1], ALU.subtract, ALU.mult)
                ins.then_inc(ln_step, 1)

            def output_max(T):
                dve.wait_ge(ln_ready, T.now())
                dve.tensor_reduce(group_cols(t64[:, 3, :])[:, T.t], o_g[:, T.t], X, ALU.max, apply_absolute_value=True)
            staggered(nc, dve, NG, [(0, output_norm), (3, output_max)])
            dve.wait_ge(squares_done, NT)
            dve.drain()
            dve.tensor_scalar(t64[:, 5, :], t64[:, 2, :], 1.0 / P, None, ALU.mult)
            dve.drain()
            rsqrt(t64[:, 6, :], t64[:, 5, :])
            quant_factors(t64[:, 3, :], t64[:, 6, :], sc[:, 19:20])
            dve.sem_inc(phase, 1)

            quant_g, back_g = group_cols(s_in[:, 0, :]), group_cols(s_in[:, 1, :])

            def quantised_output(T):
                u = T.u
                need(dve, aT_raw, T.before(2, NORM["out0"]))
                for t in range(GROUP):
                    ins = dve.tensor_scalar(xng[:, u, t, :], o_g[:, T.t, t, :], quant_g[:, T.t, t:t + 1], MAGIC, ALU.mult, ALU.add)
                ins.then_inc(xn_ready, 1)

            def scaled_projection(T):
                dve.wait_ge(y_done, T.now(PROJ["out0"]))
                need(dve, x_added, T.before(2))
                for t in range(GROUP):
                    ins = dve.scalar_tensor_tensor(out=yg[:, T.u, t, :], in0=psYg[T.u][:, t, :], scalar=back_g[:, T.t, t:t + 1],
                                                   in1=R("bo0"), op0=ALU.mult, op1=ALU.add)
                ins.then_inc(y_used, 1)

            def stats_of_added(T):
                dve.wait_ge(x_added, T.now())
                dve.sem_inc(x_seen, 1)
                for t in range(GROUP):
                    dve.bn_stats(st_g[:, T.t, t, :], xs_g[:, T.t, t, :])
            staggered(nc, dve, NG, [(0, quantised_output), (3, scaled_projection), (5, stats_of_added)])

            row_moments()
            rsqrt(rs[:, :], var)
            dve.memset(PB[:, :, :], 0.0)
            dve.drain()
            dve.sem_inc(phase, 1)

            def x_maxima(T):
                u = T.u
                dve.wait_ge(xs_done, T.now())
                dve.tensor_reduce(xden[:, 0, u, :], psSx, X, ALU.max).then_inc(xmx_ready, 1)
                dve.wait_ge(xmx_ready, T.now())
                need(dve, p_ready, T.before(2))
                dve.tensor_tensor(SX[:, u], psSx, xden[:, 0, u, :].unsqueeze(2).to_broadcast([P, GROUP, SEQ]), ALU.subtract)\
                    .then_inc(nmx_ready, 1)

            def x_sums(T):
                u = T.u
                dve.wait_ge(p_ready, T.now())
                dve.tensor_reduce(xden[:, 1, u, :], PB[:, u], X, ALU.add).then_inc(rden_ready, 1)
                dve.wait_ge(rden_ready, T.now())
                dve.reciprocal(xden[:, 2, u, :], xden[:, 1, u, :]).then_inc(xrec_ready, 1)

            def add_cross(T):
                u = T.u
                dve.wait_ge(xrec_ready, T.now())
                dve.wait_ge(xo_done, T.now())
                for t in range(GROUP):
                    ins = dve.scalar_tensor_tensor(out=xs_g[:, T.t, t, :], in0=psXO[:, t, :], scalar=xden[:, 2, u, t:t + 1],
                                                   in1=xs_g[:, T.t, t, :], op0=ALU.mult, op1=ALU.add)
                ins.then_inc(y_used_x, 1)
                dve.drain()
                for t in range(GROUP):
                    dve.bn_stats(st_g[:, T.t, t, :], xs_g[:, T.t, t, :])
            staggered(nc, dve, NG, [(2, x_maxima), (3, x_sums), (4, add_cross), (0, normed_groups(NORM["cross0"]))])

            row_moments()
            rsqrt(rs[:, :], var)
            dve.sem_inc(phase, 1)

            def feature_stats(T):
                dve.wait_ge(aT_ready, T.now(NORM["bn"]))
                dve.sem_inc(xT_seen, 1)
                dve.bn_stats(bnst[:, T.t, :], xT_g[:, T.t].rearrange("p t d -> p (t d)")).then_inc(bn_done, 1)
            staggered(nc, dve, NG, [(0, normed_groups(NORM["bn"])), (2, feature_stats)])
            dve.wait_ge(bn_done, NG)
            dve.bn_aggr(sc[:, 26:28], bnst[:, :, :].rearrange("p t s -> p (t s)"))
            dve.drain()
            rsqrt(sc[:, 28:29], sc[:, 27:28], 1)
            dve.tensor_tensor(sc[:, 13:14], sc[:, 28:29], K("gamma"), ALU.mult)
            dve.drain()
            dve.tensor_tensor(sc[:, 29:30], sc[:, 26:27], sc[:, 13:14], ALU.mult)
            dve.drain()
            dve.tensor_tensor(sc[:, 14:15], K("beta"), sc[:, 29:30], ALU.subtract)
            dve.wait_ge(aT_ready, NORM["bn"] + NG)
            dve.drain()
            dve.sem_inc(phase, 1)

            sim = ps[:, 0, :].rearrange("p (n k) -> p n k", k=NKEY)

            def top_keys(T):
                dve.wait_ge(sim_done, T.now())
                dve.sem_inc(sim_seen, 1)
                for n in range(2 * PH):
                    ins = dve.max(V8[:, T.u, n, :], sim[:, n, :])
                ins.then_inc(v8_ready, 1)

            def less_best(T):
                u = T.u
                dve.wait_ge(v8_ready, T.now())
                need(dve, ee_ready, T.step(PH, -PH))
                dve.tensor_tensor(EX[:, u, NS:].rearrange("p (n k) -> p n k", k=TOPK), V8[:, u],
                                  V8[:, u, :, 0:1].to_broadcast([P, 2 * PH, TOPK]), ALU.subtract)
                dve.tensor_tensor(EX[:, u, 0:NS].rearrange("p (n k) -> p n k", k=NKEY), sim,
                                  V8[:, u, :, 0:1].to_broadcast([P, 2 * PH, NKEY]), ALU.subtract).then_inc(d_ready, 1)

            def top_pairs(T):
                dve.wait_ge(cd_ready, T.now())
                dve.sem_inc(cd_seen, 1)
                for h in range(PH):
                    ins = dve.max(T8[:, T.u, h, :], CD[:, h, :])
                ins.then_inc(t8_ready, 1)

            def pair_sums(T):
                dve.wait_ge(t8_ready, T.now())
                dve.tensor_reduce(Z[:, T.u, :], T8[:, T.u], X, ALU.add).then_inc(z_ready, 1)

            def pair_shares(T):
                dve.wait_ge(z_ready, T.now())
                need(dve, dg_ready, T.before(2))
                dve.reciprocal(RZ[:, T.u, :], Z[:, T.u, :]).then_inc(rz_ready, 1)

            def chosen(first, last):
                def seg(T):
                    for h in range(first, last):
                        dve.wait_ge(ee_ready, T.step(PH, h + 1))
                        if h == HRING - 1:
                            need(dve, pair_ready, T.before(1))
                        else:
                            need(dve, g_part, T.step(GATES, h + 1 - HRING if h >= HRING else h + 1 + PH - HRING - GATES))
                        dve.scalar_tensor_tensor(out=WW[:, h % HRING, :], in0=EE[:, h % HRING, :], scalar=T8[:, T.u, h, TOPK - 1:TOPK],
                                                 in1=EE[:, h % HRING, :], op0=ALU.is_ge, op1=ALU.mult).then_inc(ww_ready, 1)
                return seg

            def exchange_rate(T):
                dve.wait_ge(rz_ready, T.now())
                need(dve, pair_ready, T.before(2))
                dve.tensor_tensor(RT[:, T.u, 0:1], Z[:, T.u, PH - 2:PH - 1], RZ[:, T.u, PH - 1:PH], ALU.mult).then_inc(rt_ready, 1)

            def last_pair(T):
                dve.wait_ge(ww_ready, T.step(PH, PH))
                dve.wait_ge(rt_ready, T.now())
                a, b = WW[:, (PH - 2) % HRING, :], WW[:, (PH - 1) % HRING, :]
                dve.scalar_tensor_tensor(out=a, in0=b, scalar=RT[:, T.u, 0:1], in1=a, op0=ALU.mult, op1=ALU.add)\
                    .then_inc(pair_ready, 1)

            def gated(T):
                dve.wait_ge(h_ready, T.now())
                dve.wait_ge(g_part, T.step(GATES, GATES))
                need(dve, m_done, T.before(1))
                dve.tensor_tensor(HG, psG[T.u], HT, ALU.mult).then_inc(hg_ready, 1)

            def add_memory(T):
                dve.wait_ge(m_done, T.now())
                dve.tensor_tensor(xs[:, T.t, :], psM, xs[:, T.t, :], ALU.add).then_inc(y_used_m, 1)
                stats_of_new(T)
            staggered(nc, dve, NT, [(1, chosen(0, 3)), (2, gated), (1, chosen(3, 4)), (0, top_keys), (1, chosen(4, 5)), (0, less_best),
                                    (1, chosen(5, 7)), (0, top_pairs), (2, add_memory),
                                    (0, pair_sums), (1, chosen(7, PH)), (0, pair_shares), (1, last_pair), (0, exchange_rate)])

            row_moments()
            rsqrt(rs[:, :], var)
            blank_values("vones_pairs")
            bias_columns("bq1", "bk1")
            dve.drain()
            dve.sem_inc(phase, 1)
            b1 = ATTN["attn1"]
            staggered(nc, dve, NT, [(5, normalised(b1, OUTT["attn1"])), (6, add_output("attn1", R("bo1"))), (3, maxima(b1, 0)), (3, maxima(b1, 1)),
                                    (3, less_maxima(b1, 0)), (3, less_maxima(b1, 1)),
                                    (3, place_v(b1, R("bv1"))), (0, normed_rows(NORM["attn1"]))])

            row_moments()
            rsqrt(rs[:, :], var)
            blank_values("vones_heads")
            dve.drain()
            dve.sem_inc(phase, 1)
            b2 = ATTN["cross1"]

            def ctx_values(T):
                u = T.u
                dve.wait_ge(ctx_in[u], T.pair * 16 + 16)
                need(dve, pv_done, T.before(2, b2))
                for b in range(2):
                    part = slice(SEQ * b, SEQ * b + SEQ)
                    ins = dve.tensor_copy(VBh[part, u, :, b, 0:DH], ctile[part, u, :].rearrange("p (h d) -> p h d", h=HEADS))
                ins.then_inc(vb_ready, 1)

            def place_heads(T):
                u = T.u
                dve.wait_ge(k_done, T.now(b2))
                need(dve, sT_done, T.before(2))
                for b in range(2):
                    part = slice(SEQ * b, SEQ * b + SEQ)
                    ins = dve.tensor_copy(QB[part, u, :, part], psKd[part])
                ins.then_inc(qb_ready, 1)

            def normalised_heads(T):
                u = T.u
                dve.wait_ge(pv_done, T.now(b2))
                r = rec[0:SEQ, u, :].rearrange("p (h b) -> p h b", h=HEADS)
                dve.reciprocal(r, psOh[:, :, :, DH]).then_inc(rec_ready, 1)
                dve.wait_ge(rec_ready, T.now(b2))
                need(dve, oT_done, T.before(2, OUTT["cross1"]))
                dve.tensor_tensor(O[0:SEQ, u].rearrange("p b (h d) -> p h b d", h=HEADS), psOh[:, :, :, 0:DH],
                                  r.unsqueeze(3).to_broadcast([SEQ, HEADS, 2, DH]), ALU.mult).then_inc(o_ready, 1)
            staggered(nc, dve, NT, [(6, add_output("cross1", None)), (3, ctx_values), (0, normed_rows(NORM["cross1"])),
                                    (2, place_heads), (4, normalised_heads)])

            row_moments()
            rsqrt(rs[:, :], var)
            dve.sem_inc(phase, 1)

            def logits(T):
                dve.wait_ge(lg_done, T.now())
                dve.tensor_copy(by_group(lg)[:, T.t], psRg[T.u])
                for t in range(GROUP):
                    ins = dve.max(l8_of[:, T.u, t, :], psRg[T.u][:, t, :])
                ins.then_inc(lg_ready, 1)

            def keep_largest(T):
                dve.wait_ge(lg_ready, T.now())
                dve.tensor_copy(by_group(l8)[:, T.t], l8_of[:, T.u])
            staggered(nc, dve, NG, [(5, keep_largest), (4, logits), (0, normed_groups(NORM["routing"]))])
            dve.drain()
            dve.tensor_tensor(le, lg, l8[:, :, 0:1].to_broadcast([P, NT, MOE]), ALU.subtract).then_inc(lg_less_max, 1)
            dve.tensor_tensor(lw, lg, l8[:, :, MOE_K - 1:MOE_K].to_broadcast([P, NT, MOE]), ALU.is_ge)
            dve.wait_ge(le_ready, 1)
            dve.drain()
            dve.tensor_tensor(lw, lw, le, ALU.mult)
            dve.drain()
            dve.tensor_reduce(lz[:, 0, :], lw, X, ALU.add)
            dve.drain()
            dve.reciprocal(lz[:, 1, :], lz[:, 0, :])
            dve.drain()
            dve.tensor_tensor(lw, lw, lz[:, 1, :].unsqueeze(2).to_broadcast([P, NT, MOE]), ALU.mult)
            dve.drain()
            dve.tensor_copy(lw_up[:, :, :], lw)
            dve.tensor_copy(pick[:, :], C("pick"))
            dve.drain()
            dve.tensor_copy(gates_at[:, :, 0:MOE], lw_up[:, :, :].bitcast(F32))
            dve.tensor_tensor(gates_at[:, :, MOE:2 * MOE], lw, lw_up[:, :, :].bitcast(F32), ALU.subtract).then_inc(pick_ready, 1)
            dve.drain()
            dve.sem_inc(phase, 1)

            def halves(T):
                u = T.u
                need(dve, up_done, T.step(MOE, -MOE))
                dve.tensor_copy(a_up[:, u, :], cT_duo[:, T.t, :]).then_inc(a_step, 1)
                dve.wait_ge(a_step, T.now())
                dve.tensor_tensor(a_low[:, u, :], cT_duo[:, T.t, :], a_up[:, u, :].bitcast(F32), ALU.subtract).then_inc(a_split, 1)

            gates_duo = gates_at.rearrange("p (s t) n -> p s t n", t=DUO)

            def take_gates(T):
                need(dve, g_turned, T.before(2))
                dve.tensor_copy(gates_of[:, T.u], gates_duo[:, T.t]).then_inc(g_ready, 1)

            def gates(T):
                dve.wait_ge(g_turned, T.now())
                need(dve, down_done, T.step(MOE, -MOE))
                dve.tensor_copy(gT[0:2 * MOE, T.u, :], psGT).then_inc(gT_ready, 1)

            def weighted(T, e):
                dve.wait_ge(down_done, T.step(MOE, e + 1))
                need(dve, acc_done, T.step(MOE, e))
                dve.wait_ge(gb_ready, T.step(MOE, e + 1))
                dve.tensor_tensor(prod[:, :], psD[e % 2], GB[:, e % 2], ALU.mult).then_inc(prod_ready, 1)

            def lower_half(T, e):
                n = e % RING
                dve.wait_ge(h_up_ready, T.step(MOE, e + 1))
                need(dve, down_done, T.step(MOE, e + 1 - RING))
                dve.tensor_tensor(h_low[:, n], hid[n], h_up[:, n].bitcast(F32), ALU.subtract).then_inc(h_split, 1)

            def added(T, e):
                dve.wait_ge(prod_ready, T.step(MOE, e + 1))
                if e == 0:
                    need(dve, back_done, T.before(2))
                    dve.tensor_copy(acc[:, T.u, :], prod[:, :]).then_inc(acc_done, 1)
                else:
                    dve.tensor_tensor(acc[:, T.u, :], acc[:, T.u, :], prod[:, :], ALU.add).then_inc(acc_done, 1)

            def of(step, e):
                return lambda T: step(T, e)

            def between(first, last):
                def seg(T):
                    for e in range(first, last):
                        weighted(T, e - RING)
                        lower_half(T, e)
                        added(T, e - RING)
                return seg

            def add_experts(T):
                dve.wait_ge(back_done, T.now())
                dve.tensor_tensor(xs_duo[:, T.t], xs_duo[:, T.t], psB, ALU.add).then_inc(out_ready, 1)
            staggered(nc, dve, NT // DUO, [(0, take_gates), (0, halves), (2, of(weighted, MOE - 2)), (1, of(lower_half, 0)), (2, of(added, MOE - 2)),
                                           (2, of(weighted, MOE - 1)), (1, of(lower_half, 1)), (2, of(added, MOE - 1)), (1, between(2, 4)),
                                           (0, gates), (1, between(4, 7)), (2, add_experts), (1, between(7, MOE))])


def set_bias(b):
    return np.tile(b.reshape(SETS, SEQ).T, (2, 1))


def by_parity(w):
    return w.reshape(*w.shape[:-1], PAIRS, 2, DH).swapaxes(-3, -2).reshape(w.shape)


def parity_rows(v):
    v = by_parity(v).reshape(2, 1, 1, SEQ)
    return np.broadcast_to(v, (2, SEQ, 2, SEQ)).reshape(P, P)


def bf16_parts(a):
    out = []
    for _ in range(PARTS):
        part = (a.view(np.uint32) & np.uint32(0xFFFF0000)).view(np.float32)
        out.append(part)
        a = a - part
    return np.stack(out)


def constants():
    c = np.zeros((P, CONSTS), np.float32)

    def put(name, a):
        at, n = CONST[name]
        c[:a.shape[0], at:at + n] = a.reshape(a.shape[0], n)

    tok = np.arange(P)
    half, pos = tok // SEQ, tok % SEQ
    put("ident", np.eye(P))
    put("own_head", (tok[:, None] // DH % PER_SET == np.arange(PER_SET)[None, :]).astype(np.float32))
    start = 2.0 ** (-8.0 / HEADS)
    slopes = np.array([start * start ** i for i in range(HEADS)], np.float32)[:, None]
    keys = np.arange(SEQ, dtype=np.float32)
    late = np.where(keys[None, :] > keys[:, None], np.float32(NEG), np.float32(0))
    put("mask_q", np.concatenate([keys[:, None] == pos, np.ones((PARTS, P)), np.broadcast_to(pos, (PARTS, P))]))
    put("mask_k", np.concatenate([np.tile(late, (1, HEADS)), bf16_parts((slopes * keys).reshape(-1)),
                                  bf16_parts(np.repeat(-slopes, SEQ, axis=1).reshape(-1))]))
    v = np.zeros((P, 2, PAIRS, 2, DH + 1), np.float32)
    w = np.zeros((P, HEADS, 2, DH + 1), np.float32)
    for n in range(2):
        v[SEQ * n:SEQ * n + SEQ, :, :, n, DH] = 1.0
        w[SEQ * n:SEQ * n + SEQ, :, n, DH] = 1.0
    put("vones_pairs", v)
    put("vones_heads", w)
    put("pick", np.tile(np.eye(MOE), (2, 1)))
    return c


def layout(i):
    f = lambda name: np.asarray(i[name])
    D = P
    tokens = f("x").shape[0] * SEQ
    x = f("x").reshape(tokens, D)
    ctx = f("ctx_1024").reshape(tokens, D)
    repeat = lambda w: np.repeat(w.reshape(-1, DH, *w.shape[1:]), 2, axis=0).reshape(D, *w.shape[1:])
    row = lambda v: np.broadcast_to(v[None], (D, D))
    rows = (parity_rows(repeat(f("L0_attn_bv"))), row(f("L0_attn_bo")), row(f("L0_attn_ln_g")), row(f("L0_attn_ln_b")),
            parity_rows(f("L1_attn_v_b")), row(f("L1_attn_o_b")))
    cols = [f(n)[:, None] for n in ("L0_xattn_bq", "L0_xattn_bk", "L0_xattn_bv", "L0_xattn_be", "L0_ffn_gamma", "L0_ffn_beta")]
    cols += [set_bias(b) for b in (f("L0_attn_bq"), repeat(f("L0_attn_bk")), f("L1_attn_q_b"), f("L1_attn_k_b"))]
    a = dict(
        x=x, ctxT=ctx.T, ctx=ctx, mask=np.ascontiguousarray(f("mask_Bx1xS2_bk0").reshape(-1, D).T).view(np.uint32), consts=constants(),
        rows=np.concatenate(rows, axis=1), cols=np.concatenate(cols, axis=1),
        wq0=f("L0_attn_wq").T, wk0=repeat(f("L0_attn_wk")).T, wv0=by_parity(repeat(f("L0_attn_wv")).T), wo0=f("L0_attn_wo").T,
        xWq=f("L0_xattn_Wq"), xWk=f("L0_xattn_Wk"), xWvT=f("L0_xattn_Wv").T, xWeT=f("L0_xattn_We").T,
        wqk=f("L0_ffn_w_q"), keysT=f("L0_ffn_keys").transpose(2, 0, 3, 1).reshape(2 * PH, D, NKEY),
        key_inT=f("L0_ffn_key_in").T, key_out=f("L0_ffn_key_out"),
        wq1=f("L1_attn_q_w").T, wk1=f("L1_attn_k_w").T, wv1=by_parity(f("L1_attn_v_w").T), wo1=f("L1_attn_o_w").T,
        wout=f("L1_xattn_W_out").T,
        scal=np.broadcast_to(np.stack([f("L1_xattn_scale"), f("L1_xattn_log_C")])[None], (D, 2)),
        router=f("L1_ffn_router_w"), up=f("L1_ffn_up_w"), down=f("L1_ffn_down_w"))
    return {k: np.ascontiguousarray(v) for k, v in a.items()}


def kernel(**inputs):
    import concourse.bacc as bacc
    from concourse.bass_utils import run_bass_kernel_spmd as run

    nc = bacc.Bacc("TRN2", target_bir_lowering=False, num_devices=1)
    arrays = {f"in_{k}": v for k, v in layout(inputs).items()}
    args = [nc.dram_tensor(k, v.shape, mybir.dt.from_np(v.dtype), kind="ExternalInput").ap() for k, v in arrays.items()]
    out = nc.dram_tensor("out", arrays["in_x"].shape, F32, kind="ExternalOutput").ap()
    build(nc, *args, out)
    r = run(nc, [arrays], core_ids=[0])
    return r.results[0]["out"].reshape(np.asarray(inputs["x"]).shape)
```
